# Optimizing a Trainium2 kernel written in Bass

```python
import numpy as np
import jax
import jax.numpy as jnp

def _softmax(x, axis=-1):
    return jax.nn.softmax(x, axis=axis)

def _gelu(x):
    return jax.nn.gelu(x, approximate=True)

def _silu(x):
    return jax.nn.silu(x)

def _sigmoid(x):
    return jax.nn.sigmoid(x)

def _layernorm(x, axis=-1, eps=1e-05):
    m = jnp.mean(x, axis=axis, keepdims=True)
    v = jnp.var(x, axis=axis, keepdims=True)
    return (x - m) / jnp.sqrt(v + eps)

def _scatter_add(tgt, idx, src, axis=0):
    return tgt.at[idx].add(src)

def _segment_sum(src, seg, n):
    return jax.ops.segment_sum(src, seg, n)
kernel_name = 'mk_seq_preln_d2_jaxref_r4_ff10f2'

def setup_inputs(seed: int=0):
    np.random.seed(seed)
    _w = jnp.asarray

    def _L0_attn_setup():
        import jax, jax.numpy as jnp
        import numpy as np
        D_MODEL = 256
        NUM_HEADS = 16
        HEAD_DIM = D_MODEL // NUM_HEADS

        def _rope(x):
            B, H, T, d = x.shape
            pos = jnp.arange(T, dtype=x.dtype)[:, None]
            freq_seq = jnp.arange(d // 2, dtype=x.dtype)
            inv_freq = 1.0 / 10000.0 ** (freq_seq / (d // 2))
            ang = pos * inv_freq[None, :]
            sin = jnp.sin(ang)[None, None]
            cos = jnp.cos(ang)[None, None]
            x1, x2 = (x[..., :d // 2], x[..., d // 2:])
            return jnp.concatenate((x1 * cos - x2 * sin, x1 * sin + x2 * cos), axis=-1)
        key = jax.random.key(seed)
        ks = jax.random.split(key, 9)
        B, T = (2, 512)
        s = 1.0 / np.sqrt(D_MODEL)
        inp = {'x': jax.random.normal(ks[0], (B, T, D_MODEL), dtype=jnp.float32), 'Wq': jax.random.normal(ks[1], (D_MODEL, D_MODEL), dtype=jnp.float32) * s, 'bq': jnp.zeros((D_MODEL,), dtype=jnp.float32), 'Wk': jax.random.normal(ks[2], (D_MODEL, D_MODEL), dtype=jnp.float32) * s, 'bk': jnp.zeros((D_MODEL,), dtype=jnp.float32), 'Wv': jax.random.normal(ks[3], (D_MODEL, D_MODEL), dtype=jnp.float32) * s, 'bv': jnp.zeros((D_MODEL,), dtype=jnp.float32), 'Wo': jax.random.normal(ks[4], (D_MODEL, D_MODEL), dtype=jnp.float32) * s, 'bo': jnp.zeros((D_MODEL,), dtype=jnp.float32)}
        return inp
    _L0_attn_in = _L0_attn_setup()

    def _L0_ffn_setup():
        import jax, jax.numpy as jnp
        import numpy as np
        B, S, D = (4, 1024, 256)
        E, I = (8, 512)
        CAPACITY = 2
        K = max(1, int(S / E * CAPACITY))
        key = jax.random.key(seed)
        k1, k2, k3, k4, k5 = jax.random.split(key, 5)
        x = jax.random.normal(k1, (B, S, D), dtype=jnp.float32)
        gate_w = jax.random.normal(k2, (D, E), dtype=jnp.float32) * 0.006
        Wg = jax.random.normal(k3, (E, D, I), dtype=jnp.float32) * 0.02
        Wu = jax.random.normal(k4, (E, D, I), dtype=jnp.float32) * 0.02
        Wd = jax.random.normal(k5, (E, I, D), dtype=jnp.float32) * 0.02
        return {'x': x, 'gate_w': gate_w, 'Wg': Wg, 'Wu': Wu, 'Wd': Wd}
    _L0_ffn_in = _L0_ffn_setup()

    def _L1_attn_setup():
        import jax, jax.numpy as jnp
        import numpy as np
        import math
        B, L, D, MAXL = (4, 1024, 256, 4096)

        def _shift1(a):
            return jnp.concatenate([jnp.zeros_like(a[:, :1]), a[:, :-1]], axis=1)
        key = jax.random.key(seed)
        ks = jax.random.split(key, 12)
        s = 0.02

        def w(k, shape):
            return jax.random.normal(k, shape, jnp.float32) * s
        return {'x': jax.random.normal(ks[0], (B, L, D), jnp.float32), 'pos_phases': jax.random.normal(ks[1], (MAXL, D), jnp.float32) * math.pi, 'Wpv': w(ks[2], (D, D)), 'bpv': jnp.zeros((D,), jnp.float32), 'Wk': w(ks[3], (D, D)), 'bk': jnp.zeros((D,), jnp.float32), 'Wkv': w(ks[4], (D, D)), 'bkv': jnp.zeros((D,), jnp.float32), 'Wg1': w(ks[5], (2 * D, D)), 'bg1': jnp.zeros((D,), jnp.float32), 'Wg2': w(ks[6], (D, 1)), 'bg2': jnp.zeros((1,), jnp.float32), 'Wb1': w(ks[7], (D, D // 2)), 'bb1': jnp.zeros((D // 2,), jnp.float32), 'Wb2': w(ks[8], (D // 2, 2)), 'bb2': jnp.zeros((2,), jnp.float32), 'ln_g': jnp.ones((D,), jnp.float32), 'ln_b': jnp.zeros((D,), jnp.float32), 'Wo': w(ks[9], (D, D)), 'bo': jnp.zeros((D,), jnp.float32)}
    _L1_attn_in = _L1_attn_setup()

    def _L1_ffn_setup():
        import jax, jax.numpy as jnp
        import numpy as np
        B, M, D = (4, 512, 256)
        N, P = (64, 32)
        key = jax.random.key(seed)
        k1, k2, k3, k4 = jax.random.split(key, 4)
        x = jax.random.normal(k1, (B, M, D), dtype=jnp.float32)
        phi = jax.random.normal(k2, (D, N, P), dtype=jnp.float32) * (1.0 / np.sqrt(D))
        W = jax.random.normal(k3, (N, D, D), dtype=jnp.float32) * (1.0 / np.sqrt(D))
        b = jax.random.normal(k4, (N, D), dtype=jnp.float32) * 0.01
        return {'x': x, 'phi': phi, 'W': W, 'b': b}
    _L1_ffn_in = _L1_ffn_setup()
    _d = {'L0_attn_x': _L0_attn_in['x'], 'L0_attn_Wq': _L0_attn_in['Wq'], 'L0_attn_bq': _L0_attn_in['bq'], 'L0_attn_Wk': _L0_attn_in['Wk'], 'L0_attn_bk': _L0_attn_in['bk'], 'L0_attn_Wv': _L0_attn_in['Wv'], 'L0_attn_bv': _L0_attn_in['bv'], 'L0_attn_Wo': _L0_attn_in['Wo'], 'L0_attn_bo': _L0_attn_in['bo'], 'L0_ffn_gate_w': _L0_ffn_in['gate_w'], 'L0_ffn_Wg': _L0_ffn_in['Wg'], 'L0_ffn_Wu': _L0_ffn_in['Wu'], 'L0_ffn_Wd': _L0_ffn_in['Wd'], 'L1_attn_pos_phases': _L1_attn_in['pos_phases'], 'L1_attn_Wpv': _L1_attn_in['Wpv'], 'L1_attn_bpv': _L1_attn_in['bpv'], 'L1_attn_Wk': _L1_attn_in['Wk'], 'L1_attn_bk': _L1_attn_in['bk'], 'L1_attn_Wkv': _L1_attn_in['Wkv'], 'L1_attn_bkv': _L1_attn_in['bkv'], 'L1_attn_Wg1': _L1_attn_in['Wg1'], 'L1_attn_bg1': _L1_attn_in['bg1'], 'L1_attn_Wg2': _L1_attn_in['Wg2'], 'L1_attn_bg2': _L1_attn_in['bg2'], 'L1_attn_Wb1': _L1_attn_in['Wb1'], 'L1_attn_bb1': _L1_attn_in['bb1'], 'L1_attn_Wb2': _L1_attn_in['Wb2'], 'L1_attn_bb2': _L1_attn_in['bb2'], 'L1_attn_ln_g': _L1_attn_in['ln_g'], 'L1_attn_ln_b': _L1_attn_in['ln_b'], 'L1_attn_Wo': _L1_attn_in['Wo'], 'L1_attn_bo': _L1_attn_in['bo'], 'L1_ffn_phi': _L1_ffn_in['phi'], 'L1_ffn_W': _L1_ffn_in['W'], 'L1_ffn_b': _L1_ffn_in['b']}
    _x0 = _d['L0_attn_x']
    _d['L0_attn_x'] = jax.random.normal(jax.random.fold_in(jax.random.key(seed), 1), (8, 1024, 256), dtype=_x0.dtype)
    del _x0
    return _d

def reference(L0_attn_x, L0_attn_Wq, L0_attn_bq, L0_attn_Wk, L0_attn_bk, L0_attn_Wv, L0_attn_bv, L0_attn_Wo, L0_attn_bo, L0_ffn_gate_w, L0_ffn_Wg, L0_ffn_Wu, L0_ffn_Wd, L1_attn_pos_phases, L1_attn_Wpv, L1_attn_bpv, L1_attn_Wk, L1_attn_bk, L1_attn_Wkv, L1_attn_bkv, L1_attn_Wg1, L1_attn_bg1, L1_attn_Wg2, L1_attn_bg2, L1_attn_Wb1, L1_attn_bb1, L1_attn_Wb2, L1_attn_bb2, L1_attn_ln_g, L1_attn_ln_b, L1_attn_Wo, L1_attn_bo, L1_ffn_phi, L1_ffn_W, L1_ffn_b):

    def _L0_attn_ref(x, Wq, bq, Wk, bk, Wv, bv, Wo, bo):
        import jax, jax.numpy as jnp
        import numpy as np
        D_MODEL = 256
        NUM_HEADS = 16
        HEAD_DIM = D_MODEL // NUM_HEADS

        def _rope(x):
            B, H, T, d = x.shape
            pos = jnp.arange(T, dtype=x.dtype)[:, None]
            freq_seq = jnp.arange(d // 2, dtype=x.dtype)
            inv_freq = 1.0 / 10000.0 ** (freq_seq / (d // 2))
            ang = pos * inv_freq[None, :]
            sin = jnp.sin(ang)[None, None]
            cos = jnp.cos(ang)[None, None]
            x1, x2 = (x[..., :d // 2], x[..., d // 2:])
            return jnp.concatenate((x1 * cos - x2 * sin, x1 * sin + x2 * cos), axis=-1)
        B, T, _ = x.shape

        def proj(W, b):
            return (x @ W + b).reshape(B, T, NUM_HEADS, HEAD_DIM).transpose(0, 2, 1, 3)
        q = _rope(proj(Wq, bq))
        k = _rope(proj(Wk, bk))
        v = proj(Wv, bv)
        scores = jnp.einsum('bhqd,bhkd->bhqk', q, k) / jnp.sqrt(jnp.asarray(HEAD_DIM, dtype=x.dtype))
        attn = jax.nn.softmax(scores, axis=-1)
        ctx = jnp.einsum('bhqk,bhkd->bhqd', attn, v)
        ctx = ctx.transpose(0, 2, 1, 3).reshape(B, T, D_MODEL)
        return ctx @ Wo + bo

    def _L0_ffn_ref(x, gate_w, Wg, Wu, Wd):
        import jax, jax.numpy as jnp
        import numpy as np
        B, S, D = (4, 1024, 256)
        E, I = (8, 512)
        CAPACITY = 2
        K = max(1, int(S / E * CAPACITY))
        logits = jnp.einsum('bsd,de->bse', x, gate_w)
        affinity = jax.nn.softmax(logits, axis=-1)
        affinity_T = jnp.transpose(affinity, (0, 2, 1))
        gating, index = jax.lax.top_k(affinity_T, K)
        b_idx = jnp.arange(x.shape[0])[:, None, None]
        x_sel = x[b_idx, index]
        g = jnp.einsum('bekd,edi->beki', x_sel, Wg)
        u = jnp.einsum('bekd,edi->beki', x_sel, Wu)
        h = jax.nn.silu(g) * u
        out = jnp.einsum('beki,eid->bekd', h, Wd)
        contrib = out * gating[..., None]
        x_out = jnp.zeros_like(x).at[b_idx, index].add(contrib)
        return x_out

    def _L1_attn_ref(x, pos_phases, Wpv, bpv, Wk, bk, Wkv, bkv, Wg1, bg1, Wg2, bg2, Wb1, bb1, Wb2, bb2, ln_g, ln_b, Wo, bo):
        import jax, jax.numpy as jnp
        import numpy as np
        import math
        B, L, D, MAXL = (4, 1024, 256, 4096)

        def _shift1(a):
            return jnp.concatenate([jnp.zeros_like(a[:, :1]), a[:, :-1]], axis=1)
        Bq, Lq, Dq = x.shape
        sqrtD = jnp.sqrt(jnp.float32(Dq))
        pp = pos_phases[:Lq]
        pos_cos, pos_sin = (jnp.cos(pp), jnp.sin(pp))
        pos_values = x @ Wpv + bpv
        pos_mem_cos = jnp.cumsum(pos_cos * pos_values, axis=1)
        pos_mem_sin = jnp.cumsum(pos_sin * pos_values, axis=1)
        pos_ret = (pos_cos * pos_mem_cos + pos_sin * pos_mem_sin) / sqrtD
        key_ph = jnp.tanh(x @ Wk + bk) * jnp.pi
        key_cos, key_sin = (jnp.cos(key_ph), jnp.sin(key_ph))
        kv_values = x @ Wkv + bkv
        x_shifted = _shift1(x)
        gate_in = jnp.concatenate([x, x_shifted], axis=-1)
        gh = jax.nn.gelu(gate_in @ Wg1 + bg1, approximate=False)
        value_gates = jax.nn.sigmoid(gh @ Wg2 + bg2)
        kc_s = _shift1(key_cos)
        ks_s = _shift1(key_sin)
        kv_mem_cos = jnp.cumsum(kc_s * kv_values * value_gates, axis=1)
        kv_mem_sin = jnp.cumsum(ks_s * kv_values * value_gates, axis=1)
        gate_cumsum = jnp.maximum(jnp.cumsum(value_gates, axis=1), 1.0)
        kv_ret = (key_cos * kv_mem_cos + key_sin * kv_mem_sin) / (jnp.sqrt(gate_cumsum) * sqrtD)
        bh = jax.nn.gelu(x @ Wb1 + bb1, approximate=False)
        bw = jax.nn.softmax(bh @ Wb2 + bb2, axis=-1)
        blended = bw[..., 0:1] * pos_ret + bw[..., 1:2] * kv_ret
        mu = jnp.mean(blended, axis=-1, keepdims=True)
        var = jnp.var(blended, axis=-1, keepdims=True)
        ln = (blended - mu) / jnp.sqrt(var + 1e-05) * ln_g + ln_b
        return x + ln @ Wo + bo

    def _L1_ffn_ref(x, phi, W, b):
        import jax, jax.numpy as jnp
        import numpy as np
        B, M, D = (4, 512, 256)
        N, P = (64, 32)
        logits = jnp.einsum('bmd,dnp->bmnp', x, phi)
        dispatch = jax.nn.softmax(logits, axis=0)
        bsz, m, n, p = logits.shape
        combine = jax.nn.softmax(logits.reshape(bsz, m, n * p), axis=-1).reshape(bsz, m, n, p)
        slots = jnp.einsum('bmd,bmnp->bnpd', x, dispatch)
        y = jnp.einsum('bnpd,nde->bnpe', slots, W) + b[None, :, None, :]
        out = jnp.einsum('bnpd,bmnp->bmd', y, combine)
        return out
    x = L0_attn_x
    x = x + _L0_attn_ref(_layernorm(x, axis=-1), L0_attn_Wq, L0_attn_bq, L0_attn_Wk, L0_attn_bk, L0_attn_Wv, L0_attn_bv, L0_attn_Wo, L0_attn_bo)
    x = x + _L0_ffn_ref(_layernorm(x, axis=-1), L0_ffn_gate_w, L0_ffn_Wg, L0_ffn_Wu, L0_ffn_Wd)
    x = x + _L1_attn_ref(_layernorm(x, axis=-1), L1_attn_pos_phases, L1_attn_Wpv, L1_attn_bpv, L1_attn_Wk, L1_attn_bk, L1_attn_Wkv, L1_attn_bkv, L1_attn_Wg1, L1_attn_bg1, L1_attn_Wg2, L1_attn_bg2, L1_attn_Wb1, L1_attn_bb1, L1_attn_Wb2, L1_attn_bb2, L1_attn_ln_g, L1_attn_ln_b, L1_attn_Wo, L1_attn_bo)
    x = x + _L1_ffn_ref(_layernorm(x, axis=-1), L1_ffn_phi, L1_ffn_W, L1_ffn_b)
    return x

_drawn_inputs = setup_inputs


def setup_inputs(seed=0):
    import zlib

    import numpy as np

    out = dict(_drawn_inputs(seed))
    spreads = {'L0_attn_bq': (0.0, 0.495),
     'L0_attn_bk': (0.0, 0.8),
     'L0_attn_bv': (0.0, 0.1),
     'L0_attn_bo': (0.0, 0.1),
     'L1_attn_bpv': (0.0, 0.608),
     'L1_attn_bk': (0.0, 2.0),
     'L1_attn_bkv': (0.0, 0.47),
     'L1_attn_bg1': (0.0, 2.0),
     'L1_attn_bb1': (0.0, 2.0),
     'L1_attn_bb2': (0.0, 2.0),
     'L1_attn_ln_g': (1.0, 0.6),
     'L1_attn_ln_b': (0.0, 0.721),
     'L1_attn_bo': (0.0, 0.1)}
    factors = {'L0_ffn_gate_w': 8.0,
     'L0_ffn_Wg': 8.0,
     'L0_ffn_Wu': 8.0,
     'L0_ffn_Wd': 8.0,
     'L1_attn_Wk': 54.64,
     'L1_attn_Wg1': 200.0,
     'L1_attn_Wg2': 200.0,
     'L1_attn_Wb1': 29.264,
     'L1_attn_Wb2': 24.54,
     'L1_ffn_b': 200.0,
     'L1_attn_Wkv': 28.861}
    for name, (base, spread) in spreads.items():
        noise = np.random.default_rng([zlib.crc32(name.encode()), seed]).standard_normal(out[name].shape)
        drawn = base * np.exp(spread * noise) if base else spread * noise
        out[name] = jnp.asarray(drawn.astype(out[name].dtype))
    for name, factor in factors.items():
        out[name] = (out[name] * factor).astype(out[name].dtype)
    return out
```

```python
from contextlib import ExitStack

import numpy as np
import concourse.bass as bass
from concourse import mybir

F32 = mybir.dt.float32
BF16 = mybir.dt.bfloat16
ALU = mybir.AluOpType
ACT = mybir.ActivationFunctionType
AX = mybir.AxisListType

P = 128
B, T, D = 8, 1024, 256
NT = T // P
TILES = B * NT
KD = D // P
H, HD = 16, 16
G = 4
HG = H // G
GW = HG * HD
E, I, CAP = 8, 512, 256
N_EXP, SLOTS = 64, 32
NP = N_EXP * SLOTS
LN_EPS = 1e-5
FLOOR = 1


class Chain:

    def __init__(self, eng, sem, turn=0, per=0):
        self.eng, self.sem, self.base, self.per, self.n = eng, sem, turn * per, per, 0

    def link(self, ins):
        ins.then_inc(self.sem, 1)
        self.n += 1
        self.eng.wait_ge(self.sem, FLOOR + (self.base + self.n))

    def close(self):
        assert self.n == self.per, (self.n, self.per)


class Stage:

    def __init__(self, nc, tag):
        self.nc, self.tag, self.ctx, self.sems = nc, tag, ExitStack(), []

    def __enter__(self):
        self.ctx.__enter__()
        self.mark = self.sem("mark")
        return self

    def settle(self, eng):
        eng.sem_inc(self.mark, 1)

    def __exit__(self, *a):
        if a[0] is None:
            self.nc.clear_and_free_semaphores(self.sems)
        return self.ctx.__exit__(*a)

    def block(self):
        for s in self.sems:
            self.nc.gpsimd.sem_inc(s, FLOOR)
        self.nc.all_engine_barrier()
        return self.nc.Block()

    def sb(self, name, shape, dt=F32):
        return self.ctx.enter_context(self.nc.sbuf_tensor(f"{self.tag}_{name}", shape, dt))

    def ps(self, name, shape, dt=F32):
        return self.ctx.enter_context(self.nc.psum_tensor(f"{self.tag}_{name}", shape, dt))

    def sem(self, name):
        self.sems.append(self.nc.alloc_semaphore(f"{self.tag}_{name}"))
        return self.sems[-1]


def col_bcast(vec, p=P):
    return vec.rearrange("(a n) -> a n", a=1).to_broadcast([p, vec.shape[0]])


def normalise(nc, tag, x_d, xn_d, xnT_d, ident_d):
    with Stage(nc, tag) as st:
        x = st.sb("x", [P, TILES, D])
        ident = st.sb("ident", [P, P])
        stats = st.sb("stats", [P, NT, 6])
        mvb = st.sb("mvb", [P, NT, 2])
        mv = st.sb("mv", [P, TILES, 2])
        rstd = st.sb("rstd", [P, TILES])
        nmr = st.sb("nmr", [P, TILES])
        xn = [st.sb(f"xn{j}", [P, NT, D]) for j in range(2)]
        xnT = [st.sb(f"xnT{j}", [P, KD, T]) for j in range(2)]
        tr = [st.ps(f"tr{j}", [P, KD, 512]) for j in range(2)]
        x_in = st.sem("x_in")
        c_in = st.sem("c_in")
        chain = st.sem("chain")
        var_ready = st.sem("var_ready")
        dev_ready = st.sem("dev_ready")
        xn_ready = st.sem("xn_ready")
        turned = st.sem("turned")
        xnT_ready = st.sem("xnT_ready")
        stored = [st.sem(f"stored{j}") for j in range(2)]
        with st.block() as block:

            @block.sync
            def _(sp):
                sp.dma_start(ident[:], ident_d).then_inc(c_in, 16)
                for b in range(B):
                    sp.dma_start(x[:, b * NT:(b + 1) * NT, :],
                                 x_d[b * T:(b + 1) * T, :].rearrange("(t p) d -> p t d", p=P)).then_inc(x_in, 16)
                with sp.Fori(0, B // 2) as i:
                    for j in range(2):
                        turn = i * 2 + j
                        sp.wait_ge(xn_ready, FLOOR + (turn + 1))
                        sp.dma_start(xn_d[bass.ts(turn, T), :].rearrange("(t p) d -> p t d", p=P),
                                     xn[j][:]).then_inc(stored[j], 16)
                        sp.wait_ge(xnT_ready, FLOOR + ((turn + 1) * 4))
                        st.settle(sp)
                        for k in range(KD):
                            sp.dma_start(xnT_d[k, :, bass.ts(turn, T)], xnT[j][:, k, :]).then_inc(stored[j], 16)
                for j in range(2):
                    sp.wait_ge(stored[j], FLOOR + 48 * B // 2)

            @block.vector
            def _(dve):
                dve.wait_ge(x_in, FLOOR + 16 * B)
                with dve.Fori(0, B) as b:
                    ch = Chain(dve, chain, b, 3)
                    for t in range(NT):
                        ins = dve.bn_stats(stats[:, t, :], x[:, b * NT + t, :])
                    ch.link(ins)
                    st.settle(dve)
                    for t in range(NT):
                        ins = dve.bn_aggr(mvb[:, t, :], stats[:, t, :])
                    ch.link(ins)
                    ch.link(dve.tensor_copy(mv[:, bass.ts(b, NT), :], mvb[:]))
                    ch.close()
                ch = Chain(dve, chain)
                ch.base = 3 * B
                dve.tensor_scalar(rstd[:], mv[:, :, 1], LN_EPS, None, ALU.add).then_inc(var_ready, 1)
                dve.wait_ge(dev_ready, FLOOR + 1)
                ch.link(dve.reciprocal(rstd[:], rstd[:]))
                ch.link(dve.scalar_tensor_tensor(nmr[:], mv[:, :, 0], -1.0, rstd[:], ALU.mult, ALU.mult))
                with dve.Fori(0, B // 2) as i:
                    for j in range(2):
                        turn = i * 2 + j
                        dve.wait_ge(stored[j], FLOOR + i * 48)
                        for t in range(NT):
                            tt = turn * NT + t
                            ins = dve.tensor_scalar(xn[j][:, t, :], x[:, tt, :], rstd[:, bass.ds(tt, 1)],
                                                    nmr[:, bass.ds(tt, 1)], ALU.mult, ALU.add)
                        ins.then_inc(xn_ready, 1)

            @block.tensor
            def _(pe):
                pe.wait_ge(c_in, FLOOR + 16)
                with pe.Fori(0, B // 2) as i:
                    for j in range(2):
                        turn = i * 2 + j
                        pe.wait_ge(xn_ready, FLOOR + (turn + 1))
                        for half in range(2):
                            pe.wait_ge(xnT_ready, FLOOR + (turn * 4 + 2 * half))
                            for k in range(KD):
                                for t in range(NT // 2):
                                    ins = pe.transpose(tr[half][:, k, t * P:(t + 1) * P],
                                                       xn[j][:, half * NT // 2 + t, k * P:(k + 1) * P], ident[:])
                            ins.then_inc(turned, 1)

            @block.scalar
            def _(act):
                act.wait_ge(var_ready, FLOOR + 1)
                act.activation(rstd[:], rstd[:], ACT.Sqrt).then_inc(dev_ready, 1)
                with act.Fori(0, B // 2) as i:
                    for j in range(2):
                        turn = i * 2 + j
                        act.wait_ge(stored[j], FLOOR + i * 48)
                        for half in range(2):
                            act.wait_ge(turned, FLOOR + (turn * 2 + half + 1))
                            for k in range(KD):
                                act.activation(xnT[j][:, k, half * 512:(half + 1) * 512], tr[half][:, k, :],
                                               ACT.Copy).then_inc(xnT_ready, 1)
def qkv_rope(nc, xnT_d, wq, wk, wv, bq, bk, bv, cos_d, sin_d, qkv_d):
    W = 3 * D
    with Stage(nc, "qkv") as st:
        w = st.sb("w", [P, KD, G, 3, GW])
        bias = st.sb("bias", [P, G, 3, GW])
        cos = st.sb("cos", [P, NT, 8])
        sin = st.sb("sin", [P, NT, 8])
        xT = [st.sb(f"xT{j}", [P, KD, P]) for j in range(2)]
        y = [st.sb(f"y{j}", [P, G, 3 * GW]) for j in range(2)]
        a = [st.sb(f"a{j}", [P, G, 16, 8]) for j in range(2)]
        b_ = [st.sb(f"b{j}", [P, G, 16, 8]) for j in range(2)]
        mm = [st.ps(f"mm{j}", [P, 2, 512]) for j in range(2)]
        c_in = st.sem("c_in")
        x_in = [st.sem(f"x_in{j}") for j in range(2)]
        made = st.sem("made")
        biased = st.sem("biased")
        parts = st.sem("parts")
        turned = st.sem("turned")
        stored = [st.sem(f"stored{j}") for j in range(2)]
        n_const = 8
        with st.block() as block:

            @block.sync
            def _(sp):
                for c, (wm, bm) in enumerate(((wq, bq), (wk, bk), (wv, bv))):
                    for k in range(KD):
                        sp.dma_start(w[:, k, :, c, :], wm[k * P:(k + 1) * P, :].rearrange("p (g n) -> p g n", g=G)
                                     ).then_inc(c_in, 16)
                    sp.dma_start(bias[:, :, c, :], col_bcast(bm).rearrange("p (g n) -> p g n", g=G)).then_inc(c_in, 16)
                sp.dma_start(cos[:], cos_d).then_inc(c_in, 16)
                sp.dma_start(sin[:], sin_d).then_inc(c_in, 16)
                with sp.Fori(0, TILES // 2) as i:
                    for j in range(2):
                        t = i * 2 + j
                        sp.wait_ge(made, FLOOR + i * 2)
                        sp.dma_start(xT[j][:], xnT_d[:, :, bass.ts(t, P)].rearrange("k p t -> p k t")
                                     ).then_inc(x_in[j], 16)

            @block.tensor
            def _(pe):
                pe.wait_ge(c_in, FLOOR + 16 * 11)
                with pe.Fori(0, TILES // 2) as i:
                    for j in range(2):
                        t = i * 2 + j
                        pe.wait_ge(x_in[j], FLOOR + (i * 16 + 16))
                        pe.wait_ge(biased, FLOOR + i * 2)
                        for k in range(KD):
                            wk_ = w[:, k].rearrange("p g c n -> p (g c n)")
                            pe.matmul(mm[j][:, 0, :], xT[j][:, k, :], wk_[:, 0:512], start=k == 0, stop=k == KD - 1)
                        for k in range(KD):
                            wk_ = w[:, k].rearrange("p g c n -> p (g c n)")
                            ins = pe.matmul(mm[j][:, 1, 0:W - 512], xT[j][:, k, :], wk_[:, 512:W],
                                            start=k == 0, stop=k == KD - 1)
                        ins.then_inc(made, 1)

            @block.vector
            def _(dve):
                dve.wait_ge(c_in, FLOOR + 16 * 11)
                with dve.Fori(0, TILES // 2) as i:
                    for j in range(2):
                        t = i * 2 + j
                        dve.wait_ge(made, FLOOR + (t + 1))
                        dve.wait_ge(stored[j], FLOOR + i * 16)
                        dve.tensor_tensor(y[j][:].rearrange("p g n -> p (g n)"),
                                          mm[j][:].rearrange("p a n -> p (a n)")[:, 0:W],
                                          bias[:].rearrange("p g c n -> p (g c n)"), ALU.add).then_inc(biased, 1)

            @block.gpsimd
            def _(pool):
                pool.wait_ge(c_in, FLOOR + 16 * 11)
                with pool.Fori(0, TILES // 2) as i:
                    for j in range(2):
                        t = i * 2 + j
                        tt = (i * 2 + j) % NT
                        pool.wait_ge(biased, FLOOR + (t + 1))
                        qk = y[j][:, :, 0:2 * GW].rearrange("p g (h e) -> p g h e", e=8)
                        for hb in range(G):
                            cb = cos[:, bass.ds(tt, 1), :].broadcast_to([P, 16, 8])
                            sb_ = sin[:, bass.ds(tt, 1), :].broadcast_to([P, 16, 8])
                            pool.tensor_tensor(a[j][:, hb], qk[:, hb], cb, ALU.mult)
                            ins = pool.tensor_tensor(b_[j][:, hb], qk[:, hb], sb_, ALU.mult)
                        ins.then_inc(parts, 1)
                        pool.wait_ge(parts, FLOOR + (t + 1))
                        pool.tensor_tensor(qk[:, :, 0::2, :], a[j][:, :, 0::2, :], b_[j][:, :, 1::2, :], ALU.subtract)
                        pool.tensor_tensor(qk[:, :, 1::2, :], b_[j][:, :, 0::2, :], a[j][:, :, 1::2, :], ALU.add
                                           ).then_inc(turned, 1)

            @block.scalar
            def _(act):
                with act.Fori(0, TILES // 2) as i:
                    for j in range(2):
                        t = i * 2 + j
                        act.wait_ge(turned, FLOOR + (t + 1))
                        act.dma_start(qkv_d[bass.ts(t, P), :], y[j][:].rearrange("p g n -> p (g n)")
                                      ).then_inc(stored[j], 16)
                for j in range(2):
                    act.wait_ge(stored[j], FLOOR + 16 * TILES // 2)


def consts(nc_unused=None):
    pos = np.arange(T, dtype=np.float32)[:, None]
    inv = (np.float32(1.0) / np.float32(10000.0) ** (np.arange(8, dtype=np.float32) / np.float32(8))).astype(np.float32)
    ang = (pos * inv[None, :]).astype(np.float32)
    lay = lambda m: np.ascontiguousarray(m.astype(np.float32).reshape(NT, P, 8).transpose(1, 0, 2))
    kaug = np.zeros((32, HG), np.float32)
    for h in range(HG):
        kaug[3 * h:3 * h + 3, h] = 1.0
    tok = np.arange(T).reshape(NT, P).T
    iota = np.broadcast_to(np.arange(T, dtype=np.float32), (P, T)).copy()
    tok2 = np.stack([tok // 32 * 32, tok % 32], -1).astype(np.float32)
    return {"iota": iota, "tok": tok2, "kaug": kaug, "cos": lay(np.cos(ang)), "sin": lay(np.sin(ang)), "ident": np.eye(P, dtype=np.float32)}
def attend(nc, qkv_d, ident_d, kaug_d, ctx_d):
    NG = B * G
    S6 = 6
    ROWS = S6 * HD
    STEPS = 2 * (NT // 2)
    UNITS = 2 * HG * NT
    SINGLES = 64
    FIRST, PLACES = 5, 70
    Q_SLOT = {"h": (0, 1, 2), "m": (3, 4), "l": (5,)}
    K_SLOT = {"h": (0, 3, 5), "m": (1, 4), "l": (2,)}
    nc.disable_value_cache = True
    with Stage(nc, "att") as st:
        gin = [st.sb(f"gin{j}", [P, NT, 3 * GW]) for j in range(2)]
        hi = st.sb("hi", [P, NT, 2 * GW], BF16)
        mid = st.sb("mid", [P, NT, 2 * GW], BF16)
        low = st.sb("low", [P, NT, 2 * GW], BF16)
        rest = st.sb("rest", [P, NT, 2 * GW])
        nat = st.sb("nat", [P, NT, 2, HG, S6, HD], BF16)
        va = [st.sb(f"va{j}", [P, NT, HG, 32]) for j in range(2)]
        QT = [st.sb(f"QT{j}", [P, HG, T], BF16) for j in range(2)]
        KT = [st.sb(f"KT{j}", [P, HG, T], BF16) for j in range(2)]
        ident = st.sb("ident", [P, P])
        identb = st.sb("identb", [P, P], BF16)
        kaug = st.sb("kaug", [P, HG])
        mx2 = st.sb("mx2", [P, NT, HG, 2])
        mx = st.sb("mx", [P, NT, HG])
        mrest = st.sb("mrest", [P, NT, HG])
        naug = st.sb("naug", [P, NT, 32], BF16)
        pt = st.sb("pt", [P, 8, 2, 512])
        osb = st.sb("osb", [P, T])
        rec = st.sb("rec", [P, NT // 2, HG])
        ctx = [st.sb(f"ctx{j}", [P, NT, HG, HD]) for j in range(2)]
        s1 = st.ps("s1", [P, 3, 512])
        sT = st.ps("sT", [P, 3, 512])
        o = st.ps("o", [P, 512])
        tr = st.ps("tr", [P, 512])
        trb = tr[:].bitcast(BF16)
        c_in = st.sem("c_in")
        g_in = [st.sem(f"g_in{j}") for j in range(2)]
        ready0 = st.sem("ready0")
        chain = st.sem("chain")
        pchain = st.sem("pchain")
        nat_done = st.sem("nat_done")
        v_ready = st.sem("v_ready")
        turned = st.sem("turned")
        evac = st.sem("evac")
        scored = st.sem("scored")
        maxed = st.sem("maxed")
        naug_ready = st.sem("naug_ready")
        aug_turned = st.sem("aug_turned")
        aug_ready = st.sem("aug_ready")
        st_done = st.sem("st_done")
        exp_done = st.sem("exp_done")
        pv_done = st.sem("pv_done")
        o_evac = st.sem("o_evac")
        o_turned = st.sem("o_turned")
        rec_ready = st.sem("rec_ready")
        ctx_ready = st.sem("ctx_ready")
        stored = [st.sem(f"stored{j}") for j in range(2)]
        qkv_v = qkv_d.rearrange("(b t p) (g n) -> b p t g n", p=P, t=NT, g=G)
        ctx_v = ctx_d.rearrange("(b t p) (g n) -> b p t g n", p=P, t=NT, g=G)

        at_place = {FIRST + u * PLACES // UNITS: u for u in range(UNITS)}

        with st.block() as block:

            @block.sync
            def _(sp):
                sp.dma_start(ident[:], ident_d).then_inc(c_in, 16)
                sp.dma_start(kaug[96:P, :], kaug_d).then_inc(c_in, 16)
                sp.dma_start(gin[0][:], qkv_v[0, :, :, 0, :]).then_inc(g_in[0], 16)
                sp.dma_start(gin[1][:], qkv_v[0, :, :, 1, :]).then_inc(g_in[1], 16)
                with sp.Fori(0, NG // 2) as i:
                    for j in range(2):
                        g = i * 2 + j
                        n = (i * 2 + (j + 2)) % NG
                        sp.wait_ge(v_ready, FLOOR + (g + 1))
                        sp.dma_start(gin[j][:], qkv_v[n // G, :, :, n % G, :]).then_inc(g_in[j], 16)
                        sp.wait_ge(ctx_ready, FLOOR + (g * 2 + 2))
                        g_ = i * 2 + j
                        sp.dma_start(ctx_v[g_ // G, :, :, g_ % G, :],
                                     ctx[j][:].rearrange("p t h e -> p t (h e)")).then_inc(stored[j], 16)
                for j in range(2):
                    sp.wait_ge(g_in[j], FLOOR + (16 * (NG // 2 + 1)))
                    sp.wait_ge(stored[j], FLOOR + 16 * NG // 2)

            @block.gpsimd
            def _(pool):
                for j in range(2):
                    ins = pool.memset(va[j][:], 0.0)
                ins.then_inc(pchain, 1)
                pool.wait_ge(pchain, FLOOR + 1)
                for j in range(2):
                    pool.memset(va[j][:, :, :, HD:HD + 1], 1.0)

                def split(n, par, loads):
                    ch = Chain(pool, pchain, n, 4)
                    ch.base = ch.base + 1
                    pool.wait_ge(g_in[par], FLOOR + loads * 16)
                    qk = gin[par][:, :, 0:2 * GW]
                    pool.wait_ge(turned, FLOOR + n * 8)
                    st.settle(pool)
                    ch.link(pool.tensor_copy(hi[:], qk))
                    ch.link(pool.tensor_tensor(rest[:], qk, hi[:], ALU.subtract))
                    st.settle(pool)
                    ch.link(pool.tensor_copy(mid[:], rest[:]))
                    ch.link(pool.tensor_tensor(low[:], rest[:], mid[:], ALU.subtract))
                    ch.close()
                    st.settle(pool)
                    for part, src in (("h", hi), ("m", mid), ("l", low)):
                        for c, slots in enumerate((Q_SLOT[part], K_SLOT[part])):
                            for s in slots:
                                v = src[:, :, c * GW:(c + 1) * GW].rearrange("p t (h e) -> p t h e", h=HG)
                                ins = pool.tensor_copy(nat[:, :, c, :, s, :], v)
                    ins.then_inc(nat_done, 1)
                    if not isinstance(n, int):
                        pool.wait_ge(pv_done, FLOOR + (n * STEPS - STEPS))
                        st.settle(pool)
                    pool.tensor_copy(va[par][:, :, :, 0:HD],
                                     gin[par][:, :, 2 * GW:3 * GW].rearrange("p t (h e) -> p t h e", h=HG)
                                     ).then_inc(v_ready, 1)

                split(0, 0, 1)
                with pool.Fori(0, NG // 2) as i:
                    for j in range(2):
                        split(i * 2 + (j + 1), 1 - j, i + 1 + j)

            @block.tensor
            def _(pe):
                def turn_parts(n, par, c):
                    if c == 0:
                        pe.wait_ge(nat_done, FLOOR + (n + 1))
                        if not isinstance(n, int):
                            pe.wait_ge(ctx_ready, FLOOR + (n * 2 - 2))
                    pe.wait_ge(evac, FLOOR + (n * 8 + c))
                    h, w = c // 2, c % 2
                    for t in range(NT):
                        ins = pe.transpose(trb[0:ROWS, t * P:(t + 1) * P],
                                           nat[:, t, w, h].rearrange("p s e -> p (s e)"), identb[:])
                    ins.then_inc(turned, 1)

                def score_unit(n, par, u):
                    h, t, c = u // (2 * NT), u // 2 % NT, u % 2
                    if u % (2 * NT) == 0:
                        pe.wait_ge(evac, FLOOR + (n * 8 + (2 * h + 2)))
                    pe.wait_ge(maxed, FLOOR + (n * UNITS + max(u - 2, 0)))
                    pe.matmul(s1[:, u % 3, :], QT[par][0:ROWS, h, t * P:(t + 1) * P],
                              KT[par][0:ROWS, h, c * 512:(c + 1) * 512], start=True, stop=True).then_inc(scored, 1)

                def turn_max(n):
                    pe.wait_ge(naug_ready, FLOOR + (n + 1))
                    pe.wait_ge(evac, FLOOR + (n * 8 + 8))
                    for t in range(NT):
                        ins = pe.transpose(trb[96:P, t * P:(t + 1) * P], naug[:, t, :], identb[:])
                    ins.then_inc(aug_turned, 1)

                def score_T(g, par, s, c, h):
                    idx = (s * 2 + c) * HG + h
                    pe.wait_ge(exp_done, FLOOR + (g * SINGLES + max(idx - 2, 0)))
                    kt = s % 4 * 2 + c
                    pe.matmul(sT[:, idx % 3, :], KT[par][:, h, kt * P:(kt + 1) * P],
                              QT[par][:, h, s // 4 * 512:(s // 4 + 1) * 512], start=True, stop=True).then_inc(st_done, 1)

                def times_v(g, par, s, c):
                    kt = s % 4 * 2 + c
                    pe.wait_ge(exp_done, FLOOR + (g * SINGLES + (s * 2 + c + 1) * HG))
                    if s == 0 and c == 0:
                        pe.wait_ge(v_ready, FLOOR + (g + 1))
                    if kt == 0:
                        pe.wait_ge(o_evac, FLOOR + (g * 2 + s // 4))
                    for h in range(HG):
                        ins = pe.matmul(o[32 * h:32 * h + 32, :], va[par][:, kt, h, :],
                                        pt[:, (s % 2) * HG + h, c, :], start=kt == 0, stop=kt == NT - 1)
                    if c == 1:
                        ins.then_inc(pv_done, 1)

                pe.wait_ge(c_in, FLOOR + 32)
                pe.wait_ge(ready0, FLOOR + 1)
                for c in range(8):
                    turn_parts(0, 0, c)
                for u in range(UNITS):
                    score_unit(0, 0, u)
                turn_max(0)
                with pe.Fori(0, NG // 2) as i:
                    for j in range(2):
                        g, n, par = i * 2 + j, i * 2 + (j + 1), 1 - j
                        pe.wait_ge(aug_ready, FLOOR + (g + 1))
                        for k in range(SINGLES):
                            s, c, h = k // 8, k // HG % 2, k % HG
                            if k % 2 == 0 and k < 16:
                                turn_parts(n, par, k // 2)
                            score_T(g, j, s, c, h)
                            place = s * 10 + c * 5 + h
                            if place in at_place:
                                score_unit(n, par, at_place[place])
                            if h == HG - 1:
                                if s > 0:
                                    times_v(g, j, s - 1, c)
                                if place + 1 in at_place:
                                    score_unit(n, par, at_place[place + 1])
                        turn_max(n)
                        for c in range(2):
                            times_v(g, j, STEPS - 1, c)
                        for q in range(2):
                            pe.wait_ge(o_evac, FLOOR + (g * 2 + q + 1))
                            if q == 0:
                                pe.wait_ge(aug_ready, FLOOR + (n + 1))
                            else:
                                pe.wait_ge(ctx_ready, FLOOR + (g * 2 + 1))
                            for t in range(4):
                                ins = pe.transpose(tr[:, t * P:(t + 1) * P], osb[:, (q * 4 + t) * P:(q * 4 + t + 1) * P],
                                                   ident[:])
                            ins.then_inc(o_turned, 1)

            @block.scalar
            def _(act):
                def evacuate(n, par, c):
                    if c == 0:
                        act.wait_ge(st_done, FLOOR + (n * SINGLES - (SINGLES if not isinstance(n, int) else 0)))
                    act.wait_ge(turned, FLOOR + (n * 8 + c + 1))
                    dst = (QT, KT)[c % 2][par]
                    act.activation(dst[0:ROWS, c // 2, :], trb[0:ROWS, :], ACT.Copy).then_inc(evac, 1)

                for c in range(8):
                    evacuate(0, 0, c)
                with act.Fori(0, NG // 2) as i:
                    for j in range(2):
                        g = i * 2 + j
                        for s in range(STEPS):
                            act.wait_ge(pv_done, FLOOR + (g * STEPS + max(s - 1, 0)))
                            for q in range(2 * HG):
                                c, h = q // HG, q % HG
                                k = s * 2 * HG + q
                                if k % 2 == 0 and k < 16:
                                    evacuate(i * 2 + (j + 1), 1 - j, k // 2)
                                act.wait_ge(st_done, FLOOR + (g * SINGLES + (k + 1)))
                                act.activation(pt[:, (s % 2) * HG + h, c], sT[:, k % 3, :], ACT.Exp,
                                               scale=HD ** -0.5).then_inc(exp_done, 1)

            @block.vector
            def _(dve):
                dve.wait_ge(c_in, FLOOR + 32)
                for j in range(2):
                    for h in range(HG):
                        dve.tensor_copy(KT[j][96:P, h, :], kaug[96:P, h:h + 1].broadcast_to([32, T]))
                dve.memset(naug[:], 0.0)
                dve.tensor_copy(identb[:], ident[:]).then_inc(ready0, 1)

                def take_max(n, u):
                    dve.wait_ge(scored, FLOOR + (n * UNITS + u + 1))
                    h, t, c = u // (2 * NT), u // 2 % NT, u % 2
                    dve.tensor_reduce(mx2[:, t, h, c:c + 1], s1[:, u % 3, :], AX.X, ALU.max).then_inc(maxed, 1)

                def split_max(n):
                    ch = Chain(dve, chain, n, 5)
                    dve.wait_ge(maxed, FLOOR + (n * UNITS + UNITS))
                    dve.wait_ge(aug_turned, FLOOR + n)
                    ch.link(dve.tensor_tensor(mx[:], mx2[:, :, :, 0], mx2[:, :, :, 1], ALU.max))
                    ch.link(dve.tensor_scalar(naug[:, :, 0:12:3], mx[:], -1.0, None, ALU.mult))
                    ch.link(dve.scalar_tensor_tensor(mrest[:], mx[:], -1.0, naug[:, :, 0:12:3], ALU.mult, ALU.subtract))
                    ch.link(dve.tensor_copy(naug[:, :, 1:12:3], mrest[:]))
                    dve.tensor_tensor(naug[:, :, 2:12:3], mrest[:], naug[:, :, 1:12:3], ALU.subtract
                                      ).then_inc(naug_ready, 1)
                    return ch

                def place_max(n, par, ch):
                    dve.wait_ge(aug_turned, FLOOR + (n + 1))
                    ch.link(dve.tensor_copy(QT[par][96:P, 0, :], trb[96:P, :]))
                    ch.close()
                    for h in range(1, HG):
                        ins = dve.tensor_copy(QT[par][96:P, h, :], QT[par][96:P, 0, :])
                    ins.then_inc(aug_ready, 1)

                for u in range(UNITS):
                    take_max(0, u)
                place_max(0, 0, split_max(0))
                with dve.Fori(0, NG // 2) as i:
                    for j in range(2):
                        g, n, par = i * 2 + j, i * 2 + (j + 1), 1 - j

                        def o_out(q):
                            dve.wait_ge(pv_done, FLOOR + (g * STEPS + 4 * q + 4))
                            dve.wait_ge(o_turned, FLOOR + g * 2)
                            dve.tensor_copy(osb[:, q * 512:(q + 1) * 512], o[:]).then_inc(o_evac, 1)

                        for place in range(STEPS * 10):
                            if place in at_place:
                                take_max(n, at_place[place])
                            if place == 50:
                                o_out(0)
                        place_max(n, par, split_max(n))
                        o_out(1)
                        dve.wait_ge(stored[j], FLOOR + i * 16)
                        trv = tr[:].rearrange("p (t h e) -> p t h e", t=4, h=HG)
                        for q in range(2):
                            dve.wait_ge(o_turned, FLOOR + (g * 2 + q + 1))
                            dve.reciprocal(rec[:], trv[:, :, :, HD]).then_inc(rec_ready, 1)
                            dve.wait_ge(rec_ready, FLOOR + (g * 2 + q + 1))
                            dve.tensor_tensor(ctx[j][:, 4 * q:4 * q + 4], trv[:, :, :, 0:HD],
                                              rec[:].rearrange("p t (h a) -> p t h a", a=1).broadcast_to([P, 4, HG, HD]),
                                              ALU.mult).then_inc(ctx_ready, 1)
    nc.disable_value_cache = False
def project(nc, tag, ctx_d, w_d, b_d, x_d, ident_d, out_d):
    with Stage(nc, tag) as st:
        w = st.sb("w", [P, KD, D])
        bias = st.sb("bias", [P, D])
        ident = st.sb("ident", [P, P])
        c = [st.sb(f"c{j}", [P, D]) for j in range(2)]
        x = [st.sb(f"x{j}", [P, D]) for j in range(2)]
        cT = [st.sb(f"cT{j}", [P, KD, P]) for j in range(2)]
        tr = [st.ps(f"tr{j}", [P, KD, P]) for j in range(2)]
        mm = [st.ps(f"mm{j}", [P, D]) for j in range(2)]
        c_in = st.sem("c_in")
        t_in = [st.sem(f"t_in{j}") for j in range(2)]
        turned = st.sem("turned")
        cT_ready = st.sem("cT_ready")
        made = st.sem("made")
        biased = st.sem("biased")
        summed = st.sem("summed")
        stored = [st.sem(f"stored{j}") for j in range(2)]
        with st.block() as block:

            @block.sync
            def _(sp):
                for k in range(KD):
                    sp.dma_start(w[:, k, :], w_d[k * P:(k + 1) * P, :]).then_inc(c_in, 16)
                sp.dma_start(bias[:], col_bcast(b_d)).then_inc(c_in, 16)
                sp.dma_start(ident[:], ident_d).then_inc(c_in, 16)
                with sp.Fori(0, TILES // 2) as i:
                    for j in range(2):
                        t = i * 2 + j
                        sp.wait_ge(turned, FLOOR + i * 2)
                        sp.dma_start(c[j][:], ctx_d[bass.ts(t, P), :]).then_inc(t_in[j], 16)
                        sp.wait_ge(stored[j], FLOOR + i * 16)
                        sp.dma_start(x[j][:], x_d[bass.ts(t, P), :]).then_inc(t_in[j], 16)

            @block.tensor
            def _(pe):
                pe.wait_ge(c_in, FLOOR + 64)
                with pe.Fori(0, TILES // 2) as i:
                    for j in range(2):
                        t = i * 2 + j
                        pe.wait_ge(t_in[j], FLOOR + (i * 32 + 32))
                        pe.wait_ge(cT_ready, FLOOR + i * 2)
                        for k in range(KD):
                            ins = pe.transpose(tr[j][:, k, :], c[j][:, k * P:(k + 1) * P], ident[:])
                        ins.then_inc(turned, 1)
                        pe.wait_ge(cT_ready, FLOOR + (t + 1))
                        pe.wait_ge(biased, FLOOR + i * 2)
                        for k in range(KD):
                            ins = pe.matmul(mm[j][:], cT[j][:, k, :], w[:, k, :], start=k == 0, stop=k == KD - 1)
                        ins.then_inc(made, 1)

            @block.scalar
            def _(act):
                with act.Fori(0, TILES // 2) as i:
                    for j in range(2):
                        t = i * 2 + j
                        act.wait_ge(turned, FLOOR + (t + 1))
                        act.wait_ge(made, FLOOR + i * 2)
                        act.activation(cT[j][:], tr[j][:], ACT.Copy).then_inc(cT_ready, 1)
                        act.wait_ge(summed, FLOOR + (t + 1))
                        act.dma_start(out_d[bass.ts(t, P), :], x[j][:]).then_inc(stored[j], 16)
                for j in range(2):
                    act.wait_ge(stored[j], FLOOR + 16 * TILES // 2)

            @block.vector
            def _(dve):
                dve.wait_ge(c_in, FLOOR + 64)
                with dve.Fori(0, TILES // 2) as i:
                    for j in range(2):
                        t = i * 2 + j
                        dve.wait_ge(t_in[j], FLOOR + (i * 32 + 32))

                        dve.wait_ge(made, FLOOR + (t + 1))
                        dve.tensor_tensor(x[j][:], x[j][:], mm[j][:], ALU.add).then_inc(biased, 1)
                        dve.wait_ge(biased, FLOOR + (t + 1))
                        dve.tensor_tensor(x[j][:], x[j][:], bias[:], ALU.add).then_inc(summed, 1)


def route(nc, xnT_d, gate_d, ident_d, pos_d, aff_d):
    with Stage(nc, "rt") as st:
        ident = st.sb("ident", [P, P])
        gw = st.sb("gw", [P, KD, E])
        xT = [st.sb(f"xT{j}", [P, KD, T]) for j in range(2)]
        lg = st.sb("lg", [P, NT, E])
        ex = st.sb("ex", [P, NT, E])
        mx = st.sb("mx", [P, NT])
        sm = st.sb("sm", [P, NT])
        aff = st.sb("aff", [P, NT, B, E])
        work = st.sb("work", [B * E, T])
        sel = st.sb("sel", [B * E, T])
        ones = st.sb("ones", [B * E, T])
        pos = st.sb("pos", [B * E, T])
        m8 = st.sb("m8", [B * E, 8])
        posT = st.sb("posT", [P, NT, B * E])
        lp = [st.ps(f"lp{j}", [P, NT, E]) for j in range(2)]
        rows = st.ps("rows", [B * E, T])
        cols = st.ps("cols", [P, NT, B * E])
        c_in = st.sem("c_in")
        x_in = [st.sem(f"x_in{j}") for j in range(2)]
        made = st.sem("made")
        read = st.sem("read")
        shifted = st.sem("shifted")
        exped = st.sem("exped")
        chain = st.sem("chain")
        aff_ready = st.sem("aff_ready")
        turned = st.sem("turned")
        pos_ready = st.sem("pos_ready")
        turned_back = st.sem("turned_back")
        posT_ready = st.sem("posT_ready")
        stored = st.sem("stored")
        PER = 6
        with st.block() as block:

            @block.sync
            def _(sp):
                sp.dma_start(ident[:], ident_d).then_inc(c_in, 16)
                sp.dma_start(gw[:], gate_d.rearrange("(k p) e -> p k e", p=P)).then_inc(c_in, 16)
                with sp.Fori(0, B // 2) as i:
                    for j in range(2):
                        b = i * 2 + j
                        sp.wait_ge(made, FLOOR + i * 2)
                        sp.dma_start(xT[j][:], xnT_d[:, :, bass.ts(b, T)].rearrange("k p t -> p k t")
                                     ).then_inc(x_in[j], 16)
                sp.wait_ge(aff_ready, FLOOR + 1)
                sp.dma_start(aff_d, aff[:]).then_inc(stored, 16)
                sp.wait_ge(posT_ready, FLOOR + 1)
                sp.dma_start(pos_d, posT[:]).then_inc(stored, 16)
                sp.wait_ge(stored, FLOOR + 32)

            @block.tensor
            def _(pe):
                pe.wait_ge(c_in, FLOOR + 32)
                with pe.Fori(0, B // 2) as i:
                    for j in range(2):
                        pe.wait_ge(x_in[j], FLOOR + (i * 16 + 16))
                        pe.wait_ge(read, FLOOR + i * 2)
                        for t in range(NT):
                            for k in range(KD):
                                ins = pe.matmul(lp[j][:, t, :], xT[j][:, k, t * P:(t + 1) * P], gw[:, k, :],
                                                start=k == 0, stop=k == KD - 1)
                        ins.then_inc(made, 1)
                pe.wait_ge(aff_ready, FLOOR + 1)
                for t in range(NT):
                    ins = pe.transpose(rows[:, t * P:(t + 1) * P], aff[:, t].rearrange("p b e -> p (b e)"), ident[:])
                ins.then_inc(turned, 1)
                pe.wait_ge(pos_ready, FLOOR + 1)
                for t in range(NT):
                    ins = pe.transpose(cols[:, t, :], pos[:, t * P:(t + 1) * P], ident[0:B * E, 0:B * E])
                ins.then_inc(turned_back, 1)

            @block.scalar
            def _(act):
                with act.Fori(0, B) as b:
                    act.wait_ge(shifted, FLOOR + (b + 1))
                    act.activation(ex[:], lg[:], ACT.Exp).then_inc(exped, 1)

            @block.vector
            def _(dve):
                dve.memset(ones[:], 1.0)
                with dve.Fori(0, B // 2) as i:
                    for j in range(2):
                        b = i * 2 + j
                        ch = Chain(dve, chain, b, 4)
                        dve.wait_ge(made, FLOOR + (b + 1))
                        ch.link(dve.tensor_reduce(mx[:], lp[j][:], AX.X, ALU.max))
                        dve.tensor_tensor(lg[:], lp[j][:], mx[:].rearrange("p (t a) -> p t a", a=1).broadcast_to([P, NT, E]),
                                          ALU.subtract).then_inc(shifted, 1)
                        dve.wait_ge(shifted, FLOOR + (b + 1))
                        dve.wait_ge(exped, FLOOR + (b + 1))
                        ch.link(dve.tensor_reduce(sm[:], ex[:], AX.X, ALU.add))
                        ch.link(dve.reciprocal(sm[:], sm[:]))
                        ch.link(dve.tensor_tensor(aff[:, :, b, :], ex[:],
                                                  sm[:].rearrange("p (t a) -> p t a", a=1).broadcast_to([P, NT, E]),
                                                  ALU.mult))
                        ch.close()
                        dve.sem_inc(read, 1)
                dve.sem_inc(aff_ready, 1)
                dve.wait_ge(turned, FLOOR + 1)
                ch = Chain(dve, chain)
                ch.base = 4 * B
                ch.link(dve.tensor_copy(work[:], rows[:]))
                with dve.Fori(0, CAP // 8) as r:
                    cr = Chain(dve, chain, r, 2)
                    cr.base = cr.base + (4 * B + 1)
                    cr.link(dve.max(m8[:], work[:]))
                    st.settle(dve)
                    cr.link(dve.match_replace(work[:], m8[:], work[:], -1.0))
                ch.base += 2 * CAP // 8
                ch.link(dve.tensor_scalar(sel[:], work[:], 0.0, None, ALU.is_lt))
                ch.link(dve.tensor_tensor_scan(pos[:], ones[:], sel[:], 0.0, ALU.mult, ALU.add))
                ch.link(dve.tensor_tensor(pos[:], pos[:], sel[:], ALU.mult))
                dve.tensor_scalar(pos[:], pos[:], -1.0, None, ALU.add).then_inc(pos_ready, 1)
                dve.wait_ge(turned_back, FLOOR + 1)
                dve.tensor_copy(posT[:], cols[:]).then_inc(posT_ready, 1)


def experts(nc, xn_d, pos_d, aff_d, wg_d, wu_d, wd_d, iota_d, tok_d, x_d, out_d):
    NB = 4
    NI = I // P
    NS = CAP // P
    WAY = (B // NB) * E
    xn_v = xn_d.rearrange("(b t p) d -> b p t d", p=P, t=NT)
    x_v = x_d.rearrange("(b t p) d -> b p t d", p=P, t=NT)
    out_v = out_d.rearrange("(b t p) d -> b p t d", p=P, t=NT)
    with Stage(nc, "moe") as st:
        iota = st.sb("iota", [P, T])
        iotab = st.sb("iotab", [P, CAP], BF16)
        posT = st.sb("posT", [P, NT, B * E])
        aff = st.sb("aff", [P, NT, B * E])
        arest = st.sb("arest", [P, NT, B * E])
        affs = st.sb("affs", [P, NT, B * E, 5], BF16)
        tok = st.sb("tok", [P, NT, 2])
        stage = st.sb("stage", [P, NT, D])
        xs = [st.sb(f"xs{b}", [P, NT, 3, D], BF16) for b in range(NB)]
        acc = [st.sb(f"acc{b}", [P, NT, D]) for b in range(NB)]
        wg = st.sb("wg", [P, KD, I])
        wu = st.sb("wu", [P, KD, I])
        wd = st.sb("wd", [P, NI, D])
        onehot = st.sb("onehot", [P, NT, CAP], BF16)
        onehotT = st.sb("onehotT", [P, NS, T])
        gi = st.sb("gi", [P, NS, 5])
        gate = st.sb("gate", [P, NS])
        idx = st.sb("idx", [P, NS])
        xsel = st.sb("xsel", [P, KD, CAP])
        sg = st.sb("sg", [P, NI, CAP])
        hT = st.sb("hT", [P, NI, CAP])
        y = st.sb("y", [P, NS, D])
        pg = st.ps("pg", [P, KD, CAP])
        pi = st.ps("pi", [P, NS, 5])
        gp = st.ps("gp", [P, NI, CAP])
        up = st.ps("up", [P, NI, CAP])
        yp = st.ps("yp", [P, NS, D])
        sp_ = st.ps("sp", [P, 2, D])
        c_in = st.sem("c_in")
        w_in = st.sem("w_in")
        wd_in = st.sem("wd_in")
        stage_in = st.sem("stage_in")
        acc_in = [st.sem(f"acc_in{b}") for b in range(NB)]
        acc_out = [st.sem(f"acc_out{b}") for b in range(NB)]
        ready0 = st.sem("ready0")
        split = st.sem("split")
        pchain = st.sem("pchain")
        chain = st.sem("chain")
        hot_ready = st.sem("hot_ready")
        gathered = st.sem("gathered")
        xsel_ready = st.sem("xsel_ready")
        hotT_ready = st.sem("hotT_ready")
        gu_done = st.sem("gu_done")
        silued = st.sem("silued")
        h_ready = st.sem("h_ready")
        down = st.sem("down")
        y_ready = st.sem("y_ready")
        scat = st.sem("scat")
        added = st.sem("added")
        with st.block() as block:

            @block.sync
            def _(sp):
                sp.dma_start(iota[:], iota_d).then_inc(c_in, 16)
                sp.dma_start(posT[:], pos_d).then_inc(c_in, 16)
                sp.dma_start(aff[:], aff_d.rearrange("p t b e -> p t (b e)")).then_inc(c_in, 16)
                sp.dma_start(tok[:], tok_d).then_inc(c_in, 16)
                def weights(i, e):
                    sp.wait_ge(gu_done, FLOOR + i * NB)
                    sp.dma_start(wg[:], wg_d[e, :, :].rearrange("(k p) n -> p k n", p=P)).then_inc(w_in, 16)
                    sp.dma_start(wu[:], wu_d[e, :, :].rearrange("(k p) n -> p k n", p=P)).then_inc(w_in, 16)
                    sp.wait_ge(down, FLOOR + i * NB)
                    sp.dma_start(wd[:], wd_d[e, :, :].rearrange("(k p) n -> p k n", p=P)).then_inc(wd_in, 16)

                with sp.Fori(0, E) as i:
                    weights(i, i)
                for b in range(NB):
                    sp.wait_ge(split, FLOOR + (NB + b))
                    sp.dma_start(stage[:], xn_v[NB + b]).then_inc(stage_in, 16)
                weights(E, 0)
                for b in range(NB):
                    sp.wait_ge(added, FLOOR + (4 * (NB * (E - 1) + b + 1)))
                    sp.dma_start(out_v[b], acc[b][:]).then_inc(acc_out[b], 16)
                for b in range(NB):
                    sp.wait_ge(acc_out[b], FLOOR + 16)
                    sp.dma_start(acc[b][:], x_v[NB + b]).then_inc(acc_in[b], 16)
                with sp.Fori(E + 1, 2 * E) as i:
                    weights(i, i - E)
                for b in range(NB):
                    sp.wait_ge(added, FLOOR + (4 * (NB * (2 * E - 1) + b + 1)))
                    sp.dma_start(out_v[NB + b], acc[b][:]).then_inc(acc_out[b], 16)
                for b in range(NB):
                    sp.wait_ge(acc_out[b], FLOOR + 32)

            @block.scalar
            def _(act):
                for b in range(NB):
                    act.wait_ge(split, FLOOR + b) if b else None
                    act.dma_start(stage[:], xn_v[b]).then_inc(stage_in, 16)
                    act.dma_start(acc[b][:], x_v[b]).then_inc(acc_in[b], 16)
                with act.Fori(0, WAY) as i:
                    for b in range(NB):
                        turn = i * NB + b
                        act.wait_ge(gathered, FLOOR + (turn + 1))
                        act.activation(xsel[:], pg[:], ACT.Copy).then_inc(xsel_ready, 1)
                        act.wait_ge(gu_done, FLOOR + (turn + 1))
                        act.activation(sg[:], gp[:], ACT.Silu).then_inc(silued, 1)
                        act.wait_ge(down, FLOOR + (turn + 1))
                        act.wait_ge(scat, FLOOR + turn * 4)
                        for s in range(NS):
                            act.activation(y[:, s, :], yp[:, s, :], ACT.Copy, scale=gate[:, s:s + 1]
                                           ).then_inc(y_ready, 1)

            @block.gpsimd
            def _(pool):
                ch = Chain(pool, pchain)

                def split_batch(b):
                    ch.link(pool.tensor_copy(xs[b][:, :, 0, :], stage[:]))
                    ch.link(pool.tensor_tensor(stage[:], stage[:], xs[b][:, :, 0, :], ALU.subtract))
                    ch.link(pool.tensor_copy(xs[b][:, :, 1, :], stage[:]))
                    pool.tensor_tensor(xs[b][:, :, 2, :], stage[:], xs[b][:, :, 1, :], ALU.subtract).then_inc(split, 1)

                for b in range(NB):
                    pool.wait_ge(stage_in, FLOOR + (16 * (b + 1)))
                    split_batch(b)
                for b in range(NB):
                    pool.wait_ge(gathered, FLOOR + (NB * (E - 1) + b + 1))
                    pool.wait_ge(stage_in, FLOOR + (16 * (NB + b + 1)))
                    split_batch(b)

            @block.vector
            def _(dve):
                ch0 = Chain(dve, chain)
                dve.wait_ge(c_in, FLOOR + 64)
                ch0.link(dve.tensor_copy(iotab[:], iota[:, 0:CAP]))
                ch0.link(dve.tensor_copy(affs[:, :, :, 0], aff[:]))
                ch0.link(dve.tensor_tensor(arest[:], aff[:], affs[:, :, :, 0], ALU.subtract))
                ch0.link(dve.tensor_copy(affs[:, :, :, 1], arest[:]))
                ch0.link(dve.tensor_tensor(affs[:, :, :, 2], arest[:], affs[:, :, :, 1], ALU.subtract))
                for c in range(2):
                    ch0.link(dve.tensor_copy(affs[:, :, :, 3 + c], tok[:, :, c:c + 1].broadcast_to([P, NT, B * E])))
                N0 = ch0.n

                def make_onehot(n, col):
                    dve.wait_ge(gathered, FLOOR + n)
                    for t in range(NT):
                        ins = dve.tensor_scalar(onehot[:, t, :], iotab[:], posT[:, t, bass.ds(col, 1)], None, ALU.is_equal)
                    ins.then_inc(hot_ready, 1)

                make_onehot(0, 0)
                with dve.Fori(0, WAY) as i:
                    for b in range(NB):
                        turn = i * NB + b
                        ch = Chain(dve, chain, turn, 4)
                        ch.base = ch.base + N0
                        dve.wait_ge(gathered, FLOOR + (turn + 1))
                        ch.link(dve.tensor_copy(gi[:], pi[:]))
                        dve.wait_ge(y_ready, FLOOR + turn * NS)
                        ch.link(dve.tensor_tensor(gate[:], gi[:, :, 0], gi[:, :, 1], ALU.add))
                        ch.link(dve.tensor_tensor(gate[:], gate[:], gi[:, :, 2], ALU.add))
                        ch.link(dve.tensor_tensor(idx[:], gi[:, :, 3], gi[:, :, 4], ALU.add))
                        ch.close()
                        dve.wait_ge(scat, FLOOR + turn * 4)
                        for s in range(NS):
                            ins = dve.tensor_scalar(onehotT[:, s, :], iota[:], idx[:, s:s + 1], None, ALU.is_equal)
                        ins.then_inc(hotT_ready, 1)
                        n = turn + 1
                        if b < NB - 1:
                            col = ((i // E) * NB + (b + 1)) * E + i % E
                        else:
                            i1 = (i + 1) % WAY
                            col = ((i1 // E) * NB) * E + i1 % E
                        make_onehot(n, col)
                        dve.wait_ge(silued, FLOOR + (turn + 1))
                        dve.wait_ge(down, FLOOR + turn)
                        dve.tensor_tensor(hT[:], sg[:], up[:], ALU.mult).then_inc(h_ready, 1)
                        dve.wait_ge(acc_in[b], FLOOR + ((i // E + 1) * 16))
                        for q in range(4):
                            dve.wait_ge(scat, FLOOR + (turn * 4 + (q + 1)))
                            dve.tensor_tensor(acc[b][:, 2 * q:2 * q + 2, :], acc[b][:, 2 * q:2 * q + 2, :], sp_[:],
                                              ALU.add).then_inc(added, 1)

            @block.tensor
            def _(pe):
                def gather(n, b, col, need):
                    pe.wait_ge(hot_ready, FLOOR + (n + 1))
                    pe.wait_ge(split, FLOOR + need)
                    pe.wait_ge(xsel_ready, FLOOR + n)
                    for k in range(KD):
                        for t in range(NT):
                            for part in range(3):
                                pe.matmul(pg[:, k, :], xs[b][:, t, part, k * P:(k + 1) * P], onehot[:, t, :],
                                          start=t == 0 and part == 0, stop=t == NT - 1 and part == 2)
                    pe.wait_ge(hotT_ready, FLOOR + n)
                    for s in range(NS):
                        for t in range(NT):
                            ins = pe.matmul(pi[:, s, :], onehot[:, t, s * P:(s + 1) * P],
                                            affs[:, t, bass.ds(col, 1), :].rearrange("p a c -> p (a c)"),
                                            start=t == 0, stop=t == NT - 1)
                    ins.then_inc(gathered, 1)

                gather(0, 0, 0, 1)
                with pe.Fori(0, WAY) as i:
                    for b in range(NB):
                        turn = i * NB + b
                        if b == 0:
                            pe.wait_ge(w_in, FLOOR + (i * 32 + 32))
                            pe.wait_ge(wd_in, FLOOR + (i * 16 + 16))
                        pe.wait_ge(xsel_ready, FLOOR + (turn + 1))
                        pe.wait_ge(h_ready, FLOOR + turn)
                        for w_, o_ in ((wg, gp), (wu, up)):
                            for m in range(NI):
                                for k in range(KD):
                                    ins = pe.matmul(o_[:, m, :], w_[:, k, m * P:(m + 1) * P], xsel[:, k, :],
                                                    start=k == 0, stop=k == KD - 1)
                        ins.then_inc(gu_done, 1)
                        if b < NB - 1:
                            gather(turn + 1, b + 1, ((i // E) * NB + (b + 1)) * E + i % E, (i // E) * NB + (b + 2))
                        else:
                            i1 = (i + 1) % WAY
                            gather(turn + 1, 0, ((i1 // E) * NB) * E + i1 % E, (i1 // E) * NB + 1)
                        pe.wait_ge(h_ready, FLOOR + (turn + 1))
                        pe.wait_ge(y_ready, FLOOR + turn * NS)
                        for s in range(NS):
                            for m in range(NI):
                                ins = pe.matmul(yp[:, s, :], hT[:, m, s * P:(s + 1) * P], wd[:, m, :],
                                                start=m == 0, stop=m == NI - 1)
                        ins.then_inc(down, 1)
                        pe.wait_ge(y_ready, FLOOR + (turn * NS + NS))
                        pe.wait_ge(hotT_ready, FLOOR + (turn + 1))
                        for q in range(4):
                            pe.wait_ge(added, FLOOR + (turn * 4 + q))
                            for t in range(2):
                                for s in range(NS):
                                    ins = pe.matmul(sp_[:, t, :], onehotT[:, s, (2 * q + t) * P:(2 * q + t + 1) * P],
                                                    y[:, s, :], start=s == 0, stop=s == NS - 1)
                            ins.then_inc(scat, 1)
PI = 3.14159265358979
TWO_PI_PARTS = (6.28125, 0.0019353071795864769)
PI_IN = 3.1415925
ROUND = 12582912.0


def phases(nc, xn_d, xnT_d, x_d, ppT_d, wpv, bpv, wk, bk, wkv, bkv, wg1, bg1, wg2, bg2, wb1, bb1, wb2, bb2,
           ln_g, ln_b, wo, bo, out_d):
    C = 2
    NAMES = ["k0", "kv0", "pv0", "k1", "kv1", "pv1", "gh0", "gh1", "bh", "gate", "z", "mean", "var", "outA", "outB"]
    FRONT = NAMES[6:11]
    NPROD, NPRE = len(NAMES), len(FRONT)
    SLOT = {n: q % 4 for q, n in enumerate(NAMES)}

    def made_at(name, turn):
        if turn is None:
            return FRONT.index(name) + 1
        return turn * NPROD + (NPRE + NAMES.index(name) + 1)

    def before(name, turn):
        s = SLOT[name]
        if turn is None:
            return [n for n in FRONT if SLOT[n] == s].index(name)
        mates = [n for n in NAMES if SLOT[n] == s]
        return turn * len(mates) + (len([n for n in FRONT if SLOT[n] == s]) + mates.index(name))

    with Stage(nc, "ph") as st:
        cosP = st.sb("cosP", [P, KD, T])
        sinP = st.sb("sinP", [P, KD, T])
        wpv_s, wk_s, wkv_s, wo_s = [st.sb(n, [P, KD, D]) for n in ("wpv", "wk", "wkv", "wo")]
        wg1_s = st.sb("wg1", [P, 2 * KD, D])
        wb1_s = st.sb("wb1", [P, KD, P])
        wg2_c = st.sb("wg2c", [P, KD])
        wb2_c = st.sb("wb2c", [P, 2])
        wb2_n = st.sb("wb2n", [P, 1])
        wg2_s = st.sb("wg2", [P, KD, P])
        wbd_s = st.sb("wbd", [P, P])
        col = st.sb("col", [P, 12])
        bb1_c = st.sb("bb1", [P, 1])
        bg2_c = st.sb("bg2", [P, 1])
        bb2_c = st.sb("bb2", [P, 2])
        bd = st.sb("bd", [P, 2])
        bo_r = st.sb("bo", [P, D])
        ones = st.sb("ones", [P, T])
        avg = st.sb("avg", [P, P])
        avg16 = st.sb("avg16", [P, P])
        xT = [st.sb(f"xT{j}", [P, KD, 1 + T]) for j in range(2)]
        gh = st.sb("gh", [P, KD, T])
        bh = st.sb("bh", [P, T])
        gt = [st.sb(f"gt{j}", [P, T]) for j in range(2)]
        w0 = [st.sb(f"w0{j}", [P, T]) for j in range(2)]
        w1 = [st.sb(f"w1{j}", [P, T]) for j in range(2)]
        th = st.sb("th", [P, T])
        hs = st.sb("hs", [P, T])
        kc = st.sb("kc", [P, 1 + T])
        ks = st.sb("ks", [P, 1 + T])
        kvg = st.sb("kvg", [P, T])
        a = st.sb("a", [P, T])
        b_ = st.sb("b", [P, T])
        sa = st.sb("sa", [P, T])
        sb_ = st.sb("sb", [P, T])
        mc = st.sb("mc", [P, T])
        ms = st.sb("ms", [P, T])
        bl = st.sb("bl", [P, KD, T])
        sq = st.sb("sq", [P, KD, T])
        cs = st.sb("cs", [P, T])
        vd = st.sb("vd", [P, T])
        eps = st.sb("eps", [P, 1])
        base = st.sb("base", [P, NT, D])
        xnat = st.sb("xnat", [P, NT, D])
        ps = [st.ps(f"ps{s}", [P, C, 512]) for s in range(4)]
        psf = [q[:].rearrange("p c n -> p (c n)") for q in ps]
        c_in = st.sem("c_in")
        x_in = [st.sem(f"x_in{j}") for j in range(2)]
        nat_in = st.sem("nat_in")
        made = st.sem("made")
        freed = [st.sem(f"freed{s}") for s in range(4)]
        ready0 = st.sem("ready0")
        zeroed = st.sem("zeroed")
        chain = st.sem("chain")
        achain = st.sem("achain")
        pchain = st.sem("pchain")
        cs_ready = st.sem("cs_ready")
        dev_ready = st.sem("dev_ready")
        reduced = st.sem("reduced")
        k_ready = st.sem("k_ready")
        kc_ready = st.sem("kc_ready")
        m_ready = st.sem("m_ready")
        m_used = st.sem("m_used")
        blended = st.sem("blended")
        cent = st.sem("cent")
        squared = st.sem("squared")
        ln_ready = st.sem("ln_ready")
        base_ready = st.sem("base_ready")
        stored = st.sem("stored")

        def taken(eng, name, turn):
            eng.wait_ge(freed[SLOT[name]], FLOOR + (before(name, turn) + 1))

        with st.block() as block:

            @block.sync
            def _(sp):
                for dst, src in ((wpv_s, wpv), (wk_s, wk), (wkv_s, wkv), (wo_s, wo), (wg1_s, wg1), (wb1_s, wb1)):
                    sp.dma_start(dst[:], src.rearrange("(k p) n -> p k n", p=P)).then_inc(c_in, 16)
                sp.dma_start(wg2_c[:], wg2.rearrange("(k p) a -> p (k a)", p=P), allow_slow_non_contiguous=True).then_inc(c_in, 16)
                sp.dma_start(wb2_c[:], wb2).then_inc(c_in, 16)
                for q, v in enumerate((bpv, bk, bkv, bg1, ln_g, ln_b)):
                    sp.dma_start(col[:, 2 * q:2 * q + 2], v.rearrange("(k p) -> p k", p=P),
                                 allow_slow_non_contiguous=True).then_inc(c_in, 16)
                sp.dma_start(bb1_c[:], bb1.rearrange("(p a) -> p a", a=1)).then_inc(c_in, 16)
                sp.dma_start(bg2_c[:], col_bcast(bg2)).then_inc(c_in, 16)
                sp.dma_start(bb2_c[:], col_bcast(bb2)).then_inc(c_in, 16)
                sp.dma_start(bo_r[:], col_bcast(bo)).then_inc(c_in, 16)
                sp.dma_start(cosP[:], ppT_d.rearrange("(k p) t -> p k t", p=P)).then_inc(c_in, 16)
                sp.wait_ge(zeroed, FLOOR + 1)
                for k in range(KD):
                    sp.dma_start(xT[0][:, k, 1:], xnT_d[k, :, 0:T]).then_inc(x_in[0], 16)
                with sp.Fori(0, B // 2) as i:
                    for j in range(2):
                        turn, n = i * 2 + j, i * 2 + (j + 1)
                        sp.wait_ge(made, FLOOR + turn * NPROD)
                        for k in range(KD):
                            sp.dma_start(xT[1 - j][:, k, 1:], xnT_d[k, :, bass.ds((n % B) * T, T)]).then_inc(x_in[1 - j], 16)
                        sp.wait_ge(stored, FLOOR + turn * 16)
                        sp.dma_start(base[:], x_d[bass.ds(turn * T, T), :].rearrange("(t p) d -> p t d", p=P)).then_inc(nat_in, 16)
                        sp.wait_ge(base_ready, FLOOR + turn)
                        sp.dma_start(xnat[:], xn_d[bass.ds(turn * T, T), :].rearrange("(t p) d -> p t d", p=P)).then_inc(nat_in, 16)
                        taken(sp, "outA", turn)
                        st.settle(sp)
                        taken(sp, "outB", turn)
                        st.settle(sp)
                        sp.dma_start(out_d[bass.ds(turn * T, T), :].rearrange("(t p) d -> p t d", p=P), base[:]).then_inc(stored, 16)
                sp.wait_ge(stored, FLOOR + 16 * B)
                sp.wait_ge(x_in[0], FLOOR + (32 * (B // 2 + 1)))

            NC = 19

            @block.gpsimd
            def _(pool):
                for j in range(2):
                    pool.memset(xT[j][:, :, 0:1], 0.0)
                pool.memset(kc[:, 0:1], 0.0)
                pool.memset(ks[:, 0:1], 0.0).then_inc(zeroed, 1)
                pool.memset(avg[:], 1.0 / D)
                pool.memset(avg16[:], 1.0 / D / 16).then_inc(zeroed, 1)
                pool.wait_ge(c_in, FLOOR + 16 * NC)
                with pool.Fori(0, B) as i:
                    ch = Chain(pool, pchain, i, 1)
                    pool.wait_ge(nat_in, FLOOR + (i * 32 + 32))
                    ch.link(pool.tensor_tensor(base[:], base[:], xnat[:], ALU.add))
                    pool.tensor_tensor(base[:], base[:], bo_r[:].rearrange("p (a n) -> p a n", a=1).broadcast_to([P, NT, D]),
                                       ALU.add).then_inc(base_ready, 1)
                    for mo in range(KD):
                        u = i * 2 + mo
                        pool.wait_ge(k_ready, FLOOR + (u + 1))
                        pool.wait_ge(m_used, FLOOR + u)
                        st.settle(pool)
                        pool.tensor_scalar(kc[:, 1:], hs[:], -2.0, 1.0, ALU.mult, ALU.add).then_inc(kc_ready, 1)
                        pool.wait_ge(kc_ready, FLOOR + (u + 1))
                        taken(pool, f"kv{mo}", i)
                        pool.tensor_tensor(mc[:], kvg[:], kc[:, 0:T], ALU.mult)
                        pool.tensor_tensor(ms[:], kvg[:], ks[:, 0:T], ALU.mult).then_inc(m_ready, 1)
                    ch.close()

            @block.tensor
            def _(pe):
                def product(name, turn, lhs, rhs, nk):
                    pe.wait_ge(freed[SLOT[name]], FLOOR + before(name, turn))
                    for c in range(C):
                        for k in range(nk):
                            ins = pe.matmul(ps[SLOT[name]][:, c, :], lhs(k), rhs(k, c), start=k == 0, stop=k == nk - 1)
                    ins.then_inc(made, 1)

                def front(n, par, loads):
                    pe.wait_ge(x_in[par], FLOOR + loads)
                    for mo in range(KD):
                        product(f"gh{mo}", n, lambda k: wg1_s[:, k, mo * P:(mo + 1) * P],
                                lambda k, c: xT[par][:, k % KD, 1 - k // KD + c * 512:1 - k // KD + (c + 1) * 512], 2 * KD)
                    product("bh", n, lambda k: wb1_s[:, k, :], lambda k, c: xT[par][:, k, 1 + c * 512:1 + (c + 1) * 512], KD)
                    taken(pe, "gh0", n)
                    taken(pe, "gh1", n)
                    product("gate", n, lambda k: wg2_s[:, k, :], lambda k, c: gh[:, k, c * 512:(c + 1) * 512], KD)
                    taken(pe, "bh", n)
                    product("z", n, lambda k: wbd_s[:], lambda k, c: bh[:, c * 512:(c + 1) * 512], 1)

                pe.wait_ge(c_in, FLOOR + 16 * NC)
                pe.wait_ge(zeroed, FLOOR + 2)
                pe.wait_ge(ready0, FLOOR + 1)
                front(None, 0, 32)
                with pe.Fori(0, B // 2) as i:
                    for j in range(2):
                        turn = i * 2 + j
                        for mo in range(KD):
                            for nm, w_ in (("k", wk_s), ("kv", wkv_s), ("pv", wpv_s)):
                                product(f"{nm}{mo}", turn, lambda k: w_[:, k, mo * P:(mo + 1) * P],
                                        lambda k, c: xT[j][:, k, 1 + c * 512:1 + (c + 1) * 512], KD)
                        front(turn, 1 - j, (i + (1 + j)) * 32)
                        pe.wait_ge(blended, FLOOR + (turn * 2 + 2))
                        product("mean", turn, lambda k: avg16[:], lambda k, c: bl[:, k, c * 512:(c + 1) * 512], KD)
                        pe.wait_ge(squared, FLOOR + (turn * 2 + 2))
                        product("var", turn, lambda k: avg[:], lambda k, c: sq[:, k, c * 512:(c + 1) * 512], KD)
                        pe.wait_ge(ln_ready, FLOOR + (turn * 2 + 2))
                        for hf, name in enumerate(("outA", "outB")):
                            pe.wait_ge(freed[SLOT[name]], FLOOR + before(name, turn))
                            pv = psf[SLOT[name]].rearrange("p (t n) -> p t n", n=D)
                            for t in range(4):
                                for k in range(KD):
                                    tt = hf * 4 + t
                                    ins = pe.matmul(pv[:, t, :], bl[:, k, tt * P:(tt + 1) * P], wo_s[:, k, :],
                                                    start=k == 0, stop=k == KD - 1)
                            ins.then_inc(made, 1)

            @block.scalar
            def _(act):
                def front(n, t, par):
                    for name, dst, bias in (("gh0", gh[:, 0, :], col[:, 6:7]), ("gh1", gh[:, 1, :], col[:, 7:8]),
                                            ("bh", bh[:], bb1_c[:, 0:1])):
                        act.wait_ge(made, FLOOR + made_at(name, t))
                        act.activation(dst, psf[SLOT[name]], ACT.Gelu, bias=bias).then_inc(freed[SLOT[name]], 1)
                    if t is not None:
                        act.wait_ge(blended, FLOOR + t * 2)
                    act.wait_ge(made, FLOOR + made_at("gate", t))
                    act.activation(gt[par][:], psf[SLOT["gate"]], ACT.Sigmoid, bias=bg2_c[:, 0:1]
                                   ).then_inc(freed[SLOT["gate"]], 1)
                    act.wait_ge(made, FLOOR + made_at("z", t))
                    act.activation(w0[par][:], psf[SLOT["z"]], ACT.Sigmoid, bias=bd[:, 0:1])
                    act.activation(w1[par][:], psf[SLOT["z"]], ACT.Sigmoid, bias=bd[:, 1:2], scale=-1.0
                                   ).then_inc(freed[SLOT["z"]], 1)
                    act.wait_ge(cs_ready, FLOOR + (n + 1))
                    act.activation(cs[:], cs[:], ACT.Sqrt).then_inc(dev_ready, 1)

                ch = Chain(act, achain)
                for k in range(KD):
                    act.wait_ge(reduced, FLOOR + (k + 1))
                    ch.link(act.activation(sinP[:, k, :], cosP[:, k, :], ACT.Sin))
                    ch.link(act.activation(cosP[:, k, :], cosP[:, k, :], ACT.Sin, scale=0.5))
                    ch.link(act.activation(cosP[:, k, :], cosP[:, k, :], ACT.Square))
                pre = ch.n
                act.wait_ge(ready0, FLOOR + 1)
                front(0, None, 0)
                with act.Fori(0, B // 2) as i:
                    for j in range(2):
                        turn = i * 2 + j
                        ch = Chain(act, achain, turn, 4)
                        ch.base = ch.base + pre
                        for mo in range(KD):
                            u = turn * 2 + mo
                            act.wait_ge(made, FLOOR + made_at(f"k{mo}", turn))
                            act.activation(th[:], psf[SLOT[f"k{mo}"]], ACT.Tanh, bias=col[:, 2 + mo:3 + mo]
                                           ).then_inc(freed[SLOT[f"k{mo}"]], 1)
                            taken(act, f"k{mo}", turn)
                            act.wait_ge(m_used, FLOOR + u)
                            act.wait_ge(kc_ready, FLOOR + u)
                            act.activation(ks[:, 1:], th[:], ACT.Sin, scale=PI_IN)
                            ch.link(act.activation(hs[:], th[:], ACT.Sin, scale=PI_IN / 2))
                            ch.link(act.activation(hs[:], hs[:], ACT.Square))
                            act.sem_inc(k_ready, 1)
                        ch.close()
                        front(turn + 1, turn, 1 - j)
                        for mo in range(KD):
                            act.wait_ge(cent, FLOOR + (turn * 2 + mo + 1))
                            act.activation(sq[:, mo, :], bl[:, mo, :], ACT.Square).then_inc(squared, 1)
                        act.wait_ge(made, FLOOR + made_at("var", turn))
                        act.wait_ge(ln_ready, FLOOR + turn * 2)
                        act.activation(vd[:], psf[SLOT["var"]], ACT.Sqrt, bias=eps[:, 0:1]).then_inc(freed[SLOT["var"]], 1)

            @block.vector
            def _(dve):
                STT = dve.scalar_tensor_tensor

                def weights(n, t, par, ch):
                    taken(dve, "gate", t)
                    ch.link(dve.tensor_tensor_scan(cs[:], ones[:], gt[par][:], 0.0, ALU.mult, ALU.add))
                    dve.tensor_scalar(cs[:], cs[:], 1.0, None, ALU.max).then_inc(cs_ready, 1)
                    dve.wait_ge(dev_ready, FLOOR + (n + 1))
                    ch.link(dve.reciprocal(cs[:], cs[:]))
                    taken(dve, "z", t)
                    ch.link(dve.tensor_tensor(w1[par][:], w1[par][:], cs[:], ALU.mult))

                dve.wait_ge(c_in, FLOOR + 16 * NC)
                ch = Chain(dve, chain)
                dve.memset(ones[:], 1.0)
                dve.memset(eps[:], LN_EPS)
                ch.link(dve.tensor_tensor(bd[:, 0:1], bb2_c[:, 0:1], bb2_c[:, 1:2], ALU.subtract))
                ch.link(dve.tensor_scalar(bd[:, 1:2], bd[:, 0:1], -1.0, None, ALU.mult))
                ch.link(dve.tensor_tensor(wb2_n[:], wb2_c[:, 0:1], wb2_c[:, 1:2], ALU.subtract))
                for k in range(KD):
                    ch.link(dve.tensor_copy(wg2_s[:, k, :], wg2_c[:, k:k + 1].broadcast_to([P, P])))
                ch.link(dve.tensor_copy(wbd_s[:], wb2_n[:, 0:1].broadcast_to([P, P])))
                for k in range(KD):
                    p = cosP[:, k, :]
                    ch.link(dve.tensor_scalar(a[:], p, 1.0 / (2 * PI), ROUND, ALU.mult, ALU.add))
                    ch.link(dve.tensor_scalar(a[:], a[:], -ROUND, None, ALU.add))
                    ch.link(STT(p, a[:], -TWO_PI_PARTS[0], p, ALU.mult, ALU.add))
                    ch.link(STT(p, a[:], -TWO_PI_PARTS[1], p, ALU.mult, ALU.add))
                    dve.tensor_scalar(p, p, PI_IN, -PI_IN, ALU.min, ALU.max).then_inc(reduced, 1)
                dve.wait_ge(achain, FLOOR + 3 * KD)
                dve.tensor_scalar(cosP[:], cosP[:], -2.0, 1.0, ALU.mult, ALU.add).then_inc(ready0, 1)
                dve.wait_ge(ready0, FLOOR + 1)
                weights(0, None, 0, ch)
                pre = ch.n
                with dve.Fori(0, B // 2) as i:
                    for j in range(2):
                        turn = i * 2 + j
                        ch = Chain(dve, chain, turn, 2 * 12 + 3 + 1 + 2)
                        ch.base = ch.base + pre
                        for mo in range(KD):
                            u = turn * 2 + mo
                            kv, pv = f"kv{mo}", f"pv{mo}"
                            dve.wait_ge(made, FLOOR + made_at(kv, turn))
                            dve.wait_ge(m_ready, FLOOR + u)
                            STT(kvg[:], psf[SLOT[kv]], col[:, 4 + mo:5 + mo], gt[j][:], ALU.add, ALU.mult
                                ).then_inc(freed[SLOT[kv]], 1)
                            dve.wait_ge(made, FLOOR + made_at(pv, turn))
                            ch.link(STT(a[:], psf[SLOT[pv]], col[:, mo:mo + 1], cosP[:, mo, :], ALU.add, ALU.mult))
                            STT(b_[:], psf[SLOT[pv]], col[:, mo:mo + 1], sinP[:, mo, :], ALU.add, ALU.mult
                                ).then_inc(freed[SLOT[pv]], 1)
                            taken(dve, pv, turn)
                            ch.link(dve.tensor_tensor_scan(sa[:], ones[:], a[:], 0.0, ALU.mult, ALU.add))
                            ch.link(dve.tensor_tensor_scan(sb_[:], ones[:], b_[:], 0.0, ALU.mult, ALU.add))
                            ch.link(dve.tensor_tensor(a[:], cosP[:, mo, :], sa[:], ALU.mult))
                            ch.link(dve.tensor_tensor(b_[:], sinP[:, mo, :], sb_[:], ALU.mult))
                            ch.link(dve.tensor_tensor(a[:], a[:], b_[:], ALU.add))
                            ch.link(dve.tensor_tensor(bl[:, mo, :], a[:], w0[j][:], ALU.mult))
                            dve.wait_ge(m_ready, FLOOR + (u + 1))
                            ch.link(dve.tensor_tensor_scan(sa[:], ones[:], mc[:], 0.0, ALU.mult, ALU.add))
                            ch.link(dve.tensor_tensor_scan(sb_[:], ones[:], ms[:], 0.0, ALU.mult, ALU.add))
                            ch.link(dve.tensor_tensor(a[:], kc[:, 1:], sa[:], ALU.mult))
                            dve.tensor_tensor(b_[:], ks[:, 1:], sb_[:], ALU.mult).then_inc(m_used, 1)
                            dve.wait_ge(m_used, FLOOR + (u + 1))
                            ch.link(dve.tensor_tensor(a[:], a[:], b_[:], ALU.add))
                            ch.link(dve.tensor_tensor(a[:], a[:], w1[j][:], ALU.mult))
                            dve.tensor_tensor(bl[:, mo, :], bl[:, mo, :], a[:], ALU.add).then_inc(blended, 1)
                            dve.wait_ge(blended, FLOOR + (u + 1))
                        weights(turn + 1, turn, 1 - j, ch)
                        dve.wait_ge(made, FLOOR + made_at("mean", turn))
                        for mo in range(KD):
                            STT(bl[:, mo, :], bl[:, mo, :], 1.0 / 16, psf[SLOT["mean"]], ALU.mult, ALU.subtract
                                ).then_inc(cent, 1)
                        dve.wait_ge(cent, FLOOR + (turn * 2 + 2))
                        dve.sem_inc(freed[SLOT["mean"]], 1)
                        taken(dve, "var", turn)
                        ch.link(dve.reciprocal(vd[:], vd[:]))
                        for mo in range(KD):
                            ch.link(dve.tensor_tensor(bl[:, mo, :], bl[:, mo, :], vd[:], ALU.mult))
                            dve.tensor_scalar(bl[:, mo, :], bl[:, mo, :], col[:, 8 + mo:9 + mo], col[:, 10 + mo:11 + mo],
                                              ALU.mult, ALU.add).then_inc(ln_ready, 1)
                        ch.close()
                        dve.wait_ge(base_ready, FLOOR + (turn + 1))
                        for hf, name in enumerate(("outA", "outB")):
                            dve.wait_ge(made, FLOOR + made_at(name, turn))
                            half = base[:, 4 * hf:4 * hf + 4, :].rearrange("p t n -> p (t n)")
                            dve.tensor_tensor(half, half, psf[SLOT[name]], ALU.add).then_inc(freed[SLOT[name]], 1)
def soft_slots(nc, xn_d, xnT_d, phi, W_d, b_d, y_d):
    CH = NP // P
    NE = P // SLOTS
    with Stage(nc, "sl") as st:
        xn = st.sb("xn", [P, TILES, D])
        xT = st.sb("xT", [P, KD, B * T])
        ph = st.sb("phi", [P, KD, NP])
        w = st.sb("w", [P, NE, KD, D])
        bias = st.sb("bias", [P, D])
        lg = [st.sb(f"lg{j}", [P, B, P]) for j in range(2)]
        mx = st.sb("mx", [P, P])
        sm = [st.sb(f"sm{j}", [P, P]) for j in range(2)]
        slT = st.sb("slT", [P, KD, B, P])
        y = st.sb("y", [P, B, D])
        lp = [st.ps(f"lp{j}", [P, B, P]) for j in range(2)]
        acc = st.ps("acc", [P, KD, B, P])
        yp = acc[:].rearrange("p k b n -> p (k b n)").rearrange("p (b n) -> p b n", n=D)
        c_in = st.sem("c_in")
        w_in = st.sem("w_in")
        logits = st.sem("logits")
        shifted = st.sem("shifted")
        chain = st.sem("chain")
        exped = st.sem("exped")
        inverted = st.sem("inverted")
        shared = st.sem("shared")
        slotted = st.sem("slotted")
        filled = st.sem("filled")
        slT_ready = st.sem("slT_ready")
        y_made = st.sem("y_made")
        y_ready = st.sem("y_ready")
        stored = st.sem("stored")
        with st.block() as block:

            @block.sync
            def _(sp):
                sp.dma_start(ph[:], phi.rearrange("(k p) n -> p k n", p=P)).then_inc(c_in, 16)
                for k in range(KD):
                    sp.dma_start(xT[:, k, :], xnT_d[k]).then_inc(c_in, 16)
                for b in range(B):
                    sp.dma_start(xn[:, b * NT:(b + 1) * NT, :],
                                 xn_d[b * T:(b + 1) * T, :].rearrange("(t p) d -> p t d", p=P)).then_inc(c_in, 16)
                with sp.Fori(0, CH) as c:
                    sp.wait_ge(y_made, FLOOR + c)
                    for e in range(NE):
                        sp.dma_start(w[:, e], W_d[c * NE + e, :, :].rearrange("(k p) n -> p k n", p=P)).then_inc(w_in, 16)
                    sp.wait_ge(y_ready, FLOOR + c)
                    for e in range(NE):
                        sp.dma_start(bias[e * SLOTS:(e + 1) * SLOTS, :],
                                     b_d[bass.ds(c * NE + e, 1), :].to_broadcast([SLOTS, D])).then_inc(w_in, 16)

            @block.gpsimd
            def _(pool):
                with pool.Fori(0, CH) as c:
                    for m in range(NT):
                        j = m % 2
                        pool.wait_ge(inverted, FLOOR + (c * NT + (m + 1)))
                        pool.tensor_tensor(lg[j][:], lg[j][:],
                                           sm[j][:].rearrange("p (a n) -> p a n", a=1).broadcast_to([P, B, P]), ALU.mult
                                           ).then_inc(shared, 1)

            @block.tensor
            def _(pe):
                def token_logits(c, u, m):
                    j = m % 2
                    pe.wait_ge(shifted, FLOOR + (max(u - 1, 0) if isinstance(u, int) else u - 1))
                    for b in range(B):
                        for k in range(KD):
                            ins = pe.matmul(lp[j][:, b, :], xT[:, k, b * T + m * P:b * T + (m + 1) * P],
                                            ph[:, k, bass.ds(c * P, P)], start=k == 0, stop=k == KD - 1)
                    ins.then_inc(logits, 1)

                pe.wait_ge(c_in, FLOOR + (16 * (1 + KD + B)))
                token_logits(0, 0, 0)
                with pe.Fori(0, CH) as c:
                    for m in range(NT):
                        j = m % 2
                        c1 = c if m < NT - 1 else (c + 1) % CH
                        token_logits(c1, c * NT + (m + 1), (m + 1) % NT)
                        pe.wait_ge(shared, FLOOR + (c * NT + (m + 1)))
                        if m == 0:
                            pe.wait_ge(y_ready, FLOOR + c)
                        for k in range(KD):
                            for b in range(B):
                                ins = pe.matmul(acc[:, k, b, :], xn[:, b * NT + m, k * P:(k + 1) * P], lg[j][:, b, :],
                                                start=m == 0 and b % 4 == 0, stop=m == NT - 1, skip_group_check=True)
                        ins.then_inc(slotted, 1)
                    pe.wait_ge(slT_ready, FLOOR + (c * 4 + 4))
                    pe.wait_ge(w_in, FLOOR + (c * 128 + 128))
                    for b in range(B):
                        for k in range(KD):
                            for e in range(NE):
                                ins = pe.matmul(yp[e * SLOTS:(e + 1) * SLOTS, b, :], slT[:, k, b, e * SLOTS:(e + 1) * SLOTS],
                                                w[:, e, k, :], start=k == 0, stop=k == KD - 1)
                    ins.then_inc(y_made, 1)

            @block.scalar
            def _(act):
                with act.Fori(0, CH) as c:
                    for m in range(NT):
                        j = m % 2
                        act.wait_ge(shifted, FLOOR + (c * NT + (m + 1)))
                        act.activation(lg[j][:], lg[j][:], ACT.Exp).then_inc(exped, 1)
                    act.wait_ge(slotted, FLOOR + (c * NT + NT))
                    act.wait_ge(y_made, FLOOR + c)
                    for k in range(KD):
                        for h in range(2):
                            act.activation(slT[:, k, 4 * h:4 * h + 4, :], acc[:, k, 4 * h:4 * h + 4, :], ACT.Copy
                                           ).then_inc(slT_ready, 1)
                    act.wait_ge(y_ready, FLOOR + (c + 1))
                    act.dma_start(y_d[:, bass.ds(c * P, P), :].rearrange("b p d -> p b d"), y[:]).then_inc(stored, 16)
                act.wait_ge(stored, FLOOR + 16 * CH)

            @block.vector
            def _(dve):
                with dve.Fori(0, CH) as c:
                    for m in range(NT):
                        j = m % 2
                        u = c * NT + m
                        ch = Chain(dve, chain, u, 2)
                        dve.wait_ge(logits, FLOOR + (u + 1))
                        if m >= 2:
                            dve.wait_ge(slotted, FLOOR + (u - 1))
                        else:
                            dve.wait_ge(slotted, FLOOR + c * NT)
                        ch.link(dve.tensor_reduce(mx[:], lp[j][:].rearrange("p b n -> p n b"), AX.X, ALU.max))
                        dve.tensor_tensor(lg[j][:], lp[j][:], mx[:].rearrange("p (a n) -> p a n", a=1).broadcast_to([P, B, P]),
                                          ALU.subtract).then_inc(shifted, 1)
                        dve.wait_ge(exped, FLOOR + (u + 1))
                        ch.link(dve.tensor_reduce(sm[j][:], lg[j][:].rearrange("p b n -> p n b"), AX.X, ALU.add))
                        ch.close()
                        dve.reciprocal(sm[j][:], sm[j][:]).then_inc(inverted, 1)
                    dve.wait_ge(y_made, FLOOR + (c + 1))
                    dve.wait_ge(stored, FLOOR + c * 16)
                    dve.wait_ge(w_in, FLOOR + (c * 128 + 128))
                    dve.tensor_tensor(y[:], yp, bias[:].rearrange("p (a n) -> p a n", a=1).broadcast_to([P, B, D]),
                                      ALU.add).then_inc(y_ready, 1)


def soft_combine(nc, xnT_d, phi, y_d, x_d, ident_d, out_d):
    SK = NP // P
    with Stage(nc, "cb") as st:
        ident = st.sb("ident", [P, P])
        ph = st.sb("phi", [P, KD, NP])
        y = st.sb("y", [P, 2, SK, D])
        xT = [st.sb(f"xT{j}", [P, KD, P]) for j in range(2)]
        x = [st.sb(f"x{j}", [P, D]) for j in range(2)]
        ex = [st.sb(f"ex{j}", [P, SK, P]) for j in range(2)]
        exT = [st.sb(f"exT{j}", [P, SK, P]) for j in range(2)]
        mx = [st.sb(f"mx{j}", [P, 1]) for j in range(2)]
        nm = [st.sb(f"nm{j}", [P, 1]) for j in range(2)]
        sm = [st.sb(f"sm{j}", [P, 1]) for j in range(2)]
        rs = [st.sb(f"rs{j}", [P, 1]) for j in range(2)]
        lp = st.ps("lp", [P, 4, 512])
        tr = [st.ps(f"tr{j}", [P, 4, P]) for j in range(2)]
        op = st.ps("op", [P, D])
        c_in = st.sem("c_in")
        y_in = st.sem("y_in")
        x_in = [st.sem(f"x_in{j}") for j in range(2)]
        logits = st.sem("logits")
        chain = st.sem("chain")
        neg_ready = st.sem("neg_ready")
        exped = st.sem("exped")
        turned = st.sem("turned")
        exT_ready = st.sem("exT_ready")
        made = st.sem("made")
        summed = st.sem("summed")
        inverted = st.sem("inverted")
        r_in = [st.sem(f"r_in{j}") for j in range(2)]
        stored = [st.sem(f"stored{j}") for j in range(2)]
        with st.block() as block:

            @block.sync
            def _(sp):
                sp.dma_start(ident[:], ident_d).then_inc(c_in, 16)
                sp.dma_start(ph[:], phi.rearrange("(k p) n -> p k n", p=P)).then_inc(c_in, 16)
                for j in range(2):
                    sp.dma_start(xT[j][:], xnT_d[:, :, j * P:(j + 1) * P].rearrange("k p t -> p k t")).then_inc(x_in[j], 16)
                sp.dma_start(y[:, 0], y_d[0].rearrange("(k p) d -> p k d", p=P)).then_inc(y_in, 16)
                with sp.Fori(0, B) as b:
                    sp.wait_ge(made, FLOOR + b * NT)
                    sp.wait_ge(y_in, FLOOR + (b * 16 + 16))
                    sp.dma_start(y[:, bass.ds((b + 1) % 2, 1)].rearrange("p a k d -> p (a k) d"),
                                 y_d[(b + 1) % B, :, :].rearrange("(k p) d -> p k d", p=P)).then_inc(y_in, 16)
                    for m in range(NT):
                        j = m % 2
                        t = b * NT + m
                        sp.wait_ge(logits, FLOOR + (t + 1))
                        sp.dma_start(xT[j][:], xnT_d[:, :, bass.ds(((t + 2) % TILES) * P, P)].rearrange("k p t -> p k t")
                                     ).then_inc(x_in[j], 16)
                        sp.wait_ge(summed, FLOOR + (t + 1))
                        sp.dma_start(out_d[bass.ds(t * P, P), :], x[j][:]).then_inc(stored[j], 16)
                for j in range(2):
                    sp.wait_ge(stored[j], FLOOR + 16 * TILES // 2)
                sp.wait_ge(y_in, FLOOR + (16 * (B + 1)))
                for j in range(2):
                    sp.wait_ge(x_in[j], FLOOR + (16 * (TILES // 2 + 1)))

            @block.tensor
            def _(pe):
                def token_logits(t, j, loads):
                    pe.wait_ge(x_in[j], FLOOR + loads * 16)
                    pe.wait_ge(exped, FLOOR + t)
                    for q in range(4):
                        for k in range(KD):
                            ins = pe.matmul(lp[:, q, :], xT[j][:, k, :], ph[:, k, q * 512:(q + 1) * 512],
                                            start=k == 0, stop=k == KD - 1)
                    ins.then_inc(logits, 1)

                pe.wait_ge(c_in, FLOOR + 32)
                token_logits(0, 0, 1)
                with pe.Fori(0, TILES // 2) as i:
                    for j in range(2):
                        t = i * 2 + j
                        pe.wait_ge(exped, FLOOR + (t + 1))
                        for q in range(4):
                            pe.wait_ge(exT_ready, FLOOR + (t * 4 + max(q - 1, 0)))
                            for s in range(4):
                                ins = pe.transpose(tr[q % 2][:, s, :], ex[j][:, 4 * q + s, :], ident[:])
                            ins.then_inc(turned, 1)
                        token_logits(t + 1, 1 - j, i + (1 + j))
                        pe.wait_ge(exT_ready, FLOOR + (t * 4 + 4))
                        pe.wait_ge(y_in, FLOOR + ((t // NT + 1) * 16))
                        pe.wait_ge(summed, FLOOR + t)
                        for k in range(SK):
                            ins = pe.matmul(op[:], exT[j][:, k, :],
                                            y[:, bass.ds((t // NT) % 2, 1), k, :].rearrange("p a d -> p (a d)"),
                                            start=k == 0, stop=k == SK - 1)
                        ins.then_inc(made, 1)

            @block.scalar
            def _(act):
                with act.Fori(0, TILES // 2) as i:
                    for j in range(2):
                        t = i * 2 + j
                        act.wait_ge(stored[j], FLOOR + i * 16)
                        act.dma_start(x[j][:], x_d[bass.ts(t, P), :]).then_inc(r_in[j], 16)
                        act.wait_ge(neg_ready, FLOOR + (t + 1))
                        act.wait_ge(summed, FLOOR + i * 2)
                        act.activation(ex[j][:].rearrange("p k n -> p (k n)"), lp[:].rearrange("p q n -> p (q n)"), ACT.Exp,
                                       bias=nm[j][:, 0:1], accum_out=sm[j][:, 0:1]).then_inc(exped, 1)
                        for q in range(0, 4, 2):
                            act.wait_ge(turned, FLOOR + (t * 4 + (q + 1)))
                            act.activation(exT[j][:, 4 * q:4 * q + 4, :], tr[q % 2][:], ACT.Copy).then_inc(exT_ready, 1)
                            act.wait_ge(turned, FLOOR + (t * 4 + (q + 2)))
                            act.activation(exT[j][:, 4 * q + 4:4 * q + 8, :], tr[q % 2 + 1][:], ACT.Copy
                                           ).then_inc(exT_ready, 1)

            @block.vector
            def _(dve):
                def neg_max(t, j):
                    dve.wait_ge(logits, FLOOR + (t + 1))
                    ch = Chain(dve, chain, t, 1)
                    ch.link(dve.tensor_reduce(mx[j][:], lp[:], AX.XY, ALU.max))
                    dve.tensor_scalar(nm[j][:], mx[j][:], -1.0, None, ALU.mult).then_inc(neg_ready, 1)

                neg_max(0, 0)
                with dve.Fori(0, TILES // 2) as i:
                    for j in range(2):
                        t = i * 2 + j
                        neg_max(t + 1, 1 - j)
                        dve.wait_ge(exped, FLOOR + (t + 1))
                        dve.reciprocal(rs[j][:], sm[j][:]).then_inc(inverted, 1)
                        dve.wait_ge(inverted, FLOOR + (t + 1))
                        dve.wait_ge(made, FLOOR + (t + 1))
                        dve.wait_ge(r_in[j], FLOOR + (i * 16 + 16))
                        dve.scalar_tensor_tensor(x[j][:], op[:], rs[j][:, 0:1], x[j][:], ALU.mult, ALU.add
                                                 ).then_inc(summed, 1)
def build_program(nc, a, out):
    def scratch(name, shape):
        return nc.dram_tensor(name, shape, F32, kind="Internal").ap()

    x0, ident = a["x"], a["ident"]
    xn, xnT = scratch("xn", (B * T, D)), scratch("xnT", (KD, P, B * T))
    qkv, ctx = scratch("qkv", (B * T, 3 * D)), scratch("ctx", (B * T, D))
    x1, x2, x3 = (scratch(n, (B * T, D)) for n in ("x1", "x2", "x3"))
    pos, aff = scratch("pos", (P, NT, B * E)), scratch("aff", (P, NT, B, E))
    y = scratch("y", (B, NP, D))

    normalise(nc, "n0", x0, xn, xnT, ident)
    qkv_rope(nc, xnT, *(a["L0_attn_" + n] for n in ("Wq", "Wk", "Wv", "bq", "bk", "bv")), a["cos"], a["sin"], qkv)
    attend(nc, qkv, ident, a["kaug"], ctx)
    project(nc, "pj", ctx, a["L0_attn_Wo"], a["L0_attn_bo"], x0, ident, x1)
    normalise(nc, "n1", x1, xn, xnT, ident)
    route(nc, xnT, a["L0_ffn_gate_w"], ident, pos, aff)
    experts(nc, xn, pos, aff, a["L0_ffn_Wg"], a["L0_ffn_Wu"], a["L0_ffn_Wd"], a["iota"], a["tok"], x1, x2)
    normalise(nc, "n2", x2, xn, xnT, ident)
    phases(nc, xn, xnT, x2, a["ppT"], *(a["L1_attn_" + n] for n in (
        "Wpv", "bpv", "Wk", "bk", "Wkv", "bkv", "Wg1", "bg1", "Wg2", "bg2", "Wb1", "bb1", "Wb2", "bb2",
        "ln_g", "ln_b", "Wo", "bo")), x3)
    normalise(nc, "n3", x3, xn, xnT, ident)
    soft_slots(nc, xn, xnT, a["phi"], a["L1_ffn_W"], a["L1_ffn_b"], y)
    soft_combine(nc, xnT, a["phi"], y, x3, ident, out)


def kernel(**inputs):
    import concourse.bacc as _bacc
    from concourse.bass_utils import run_bass_kernel_spmd as _run

    given = {k: np.asarray(v) for k, v in inputs.items()}
    arrays = {k: v for k, v in given.items() if k not in ("L0_attn_x", "L1_attn_pos_phases", "L1_ffn_phi")}
    arrays["x"] = given["L0_attn_x"].reshape(B * T, D)
    arrays["ppT"] = given["L1_attn_pos_phases"][:T].T
    arrays["phi"] = given["L1_ffn_phi"].reshape(D, NP)
    arrays.update(consts())
    nc = _bacc.Bacc("TRN2", target_bir_lowering=False, num_devices=1)
    sent, aps = {}, {}
    for name, v in arrays.items():
        sent[f"in_{name}"] = np.ascontiguousarray(v)
        aps[name] = nc.dram_tensor(f"in_{name}", v.shape, mybir.dt.from_np(v.dtype), kind="ExternalInput").ap()
    out = nc.dram_tensor("out", (B * T, D), F32, kind="ExternalOutput").ap()
    build_program(nc, aps, out)
    r = _run(nc, [sent], core_ids=[0])
    return r.results[0]["out"].reshape(B, T, D)
```

```python
from contextlib import ExitStack

import numpy as np
import concourse.bass as bass
from concourse import mybir

F32 = mybir.dt.float32
BF16 = mybir.dt.bfloat16
ALU = mybir.AluOpType
ACT = mybir.ActivationFunctionType
AX = mybir.AxisListType

P = 128
B, T, D = 8, 1024, 256
NT = T // P
TILES = B * NT
KD = D // P
H, HD = 16, 16
G = 4
HG = H // G
GW = HG * HD
E, I, CAP = 8, 512, 256
N_EXP, SLOTS = 64, 32
NP = N_EXP * SLOTS
LN_EPS = 1e-5
FLOOR = 1


class Chain:

    def __init__(self, eng, sem, turn=0, per=0):
        self.eng, self.sem, self.base, self.per, self.n = eng, sem, turn * per, per, 0

    def link(self, ins):
        ins.then_inc(self.sem, 1)
        self.n += 1
        self.eng.wait_ge(self.sem, FLOOR + (self.base + self.n))

    def close(self):
        assert self.n == self.per, (self.n, self.per)


class Stage:

    def __init__(self, nc, tag):
        self.nc, self.tag, self.ctx, self.sems = nc, tag, ExitStack(), []

    def __enter__(self):
        self.ctx.__enter__()
        self.mark = self.sem("mark")
        return self

    def settle(self, eng):
        eng.sem_inc(self.mark, 1)

    def __exit__(self, *a):
        if a[0] is None:
            self.nc.clear_and_free_semaphores(self.sems)
        return self.ctx.__exit__(*a)

    def block(self):
        for s in self.sems:
            self.nc.gpsimd.sem_inc(s, FLOOR)
        self.nc.all_engine_barrier()
        return self.nc.Block()

    def sb(self, name, shape, dt=F32):
        return self.ctx.enter_context(self.nc.sbuf_tensor(f"{self.tag}_{name}", shape, dt))

    def ps(self, name, shape, dt=F32):
        return self.ctx.enter_context(self.nc.psum_tensor(f"{self.tag}_{name}", shape, dt))

    def sem(self, name):
        self.sems.append(self.nc.alloc_semaphore(f"{self.tag}_{name}"))
        return self.sems[-1]


def col_bcast(vec, p=P):
    return vec.rearrange("(a n) -> a n", a=1).to_broadcast([p, vec.shape[0]])


def normalise(nc, tag, x_d, xn_d, xnT_d, ident_d):
    U = 4
    with Stage(nc, tag) as st:
        ident = st.sb("ident", [P, P])
        eps = st.sb("eps", [P, 1])
        x = [st.sb(f"x{j}", [P, NT, D]) for j in range(U)]
        stats = st.sb("stats", [P, NT, 6])
        mv = [st.sb(f"mv{j}", [P, NT, 2]) for j in range(2)]
        rstd = [st.sb(f"rstd{j}", [P, NT]) for j in range(2)]
        nmr = [st.sb(f"nmr{j}", [P, NT]) for j in range(2)]
        xn = [st.sb(f"xn{j}", [P, NT, D]) for j in range(2)]
        xnT = [st.sb(f"xnT{j}", [P, KD, T]) for j in range(2)]
        tr = [st.ps(f"tr{j}", [P, KD, 512]) for j in range(2)]
        x_in = [st.sem(f"x_in{j}") for j in range(U)]
        c_in = st.sem("c_in")
        chain = st.sem("chain")
        stats_ready = st.sem("stats_ready")
        eps_ready = st.sem("eps_ready")
        var_ready = st.sem("var_ready")
        dev_ready = st.sem("dev_ready")
        xn_ready = st.sem("xn_ready")
        turned = st.sem("turned")
        xnT_ready = st.sem("xnT_ready")
        xn_stored = [st.sem(f"xn_stored{j}") for j in range(2)]
        xnT_stored = [st.sem(f"xnT_stored{j}") for j in range(2)]
        with st.block() as block:

            @block.sync
            def _(sp):
                sp.dma_start(x[0][:], x_d[0:T, :].rearrange("(t p) d -> p t d", p=P)).then_inc(x_in[0], 16)
                sp.dma_start(ident[:], ident_d).then_inc(c_in, 16)
                for j in range(1, U):
                    sp.dma_start(x[j][:], x_d[j * T:(j + 1) * T, :].rearrange("(t p) d -> p t d", p=P)
                                 ).then_inc(x_in[j], 16)
                for b in range(U, B + 1):
                    j = b % U
                    sp.wait_ge(xn_ready, FLOOR + (b - U + 1))
                    rows = slice(b % B * T, (b % B + 1) * T)
                    sp.dma_start(x[j][:], x_d[rows, :].rearrange("(t p) d -> p t d", p=P)).then_inc(x_in[j], 16)

            @block.vector
            def _(dve):
                def statistics(n, u, loads):
                    dve.wait_ge(x_in[u], FLOOR + loads * 16)
                    dve.wait_ge(var_ready, FLOOR + n)
                    for t in range(NT):
                        ins = dve.bn_stats(stats[:, t, :], x[u][:, t, :])
                    ins.then_inc(stats_ready, 1)
                    dve.wait_ge(stats_ready, FLOOR + (n + 1))
                    st.settle(dve)
                    for t in range(NT):
                        ins = dve.bn_aggr(mv[u % 2][:, t, :], stats[:, t, :])
                    ins.then_inc(var_ready, 1)

                dve.memset(eps[:], LN_EPS).then_inc(eps_ready, 1)
                statistics(0, 0, 1)
                with dve.Fori(0, B // U) as i:
                    for u in range(U):
                        turn, j = i * U + u, u % 2
                        statistics(turn + 1, (u + 1) % U, i + (1 + (u + 1) // U))
                        ch = Chain(dve, chain, turn, 2)
                        dve.wait_ge(dev_ready, FLOOR + (turn + 1))
                        ch.link(dve.reciprocal(rstd[j][:], rstd[j][:]))
                        ch.link(dve.scalar_tensor_tensor(nmr[j][:], mv[j][:, :, 0], -1.0, rstd[j][:],
                                                         ALU.mult, ALU.mult))
                        ch.close()
                        dve.wait_ge(turned, FLOOR + (i * 2 * U + 2 * max(u - 1, 0)))
                        dve.wait_ge(xn_stored[j], FLOOR + (i * (U // 2) + u // 2) * 16)
                        for t in range(NT):
                            ins = dve.tensor_scalar(xn[j][:, t, :], x[u][:, t, :], rstd[j][:, t:t + 1],
                                                    nmr[j][:, t:t + 1], ALU.mult, ALU.add)
                        ins.then_inc(xn_ready, 1)

            @block.tensor
            def _(pe):
                pe.wait_ge(c_in, FLOOR + 16)
                with pe.Fori(0, B // 2) as i:
                    for j in range(2):
                        turn = i * 2 + j
                        pe.wait_ge(xn_ready, FLOOR + (turn + 1))
                        for half in range(2):
                            pe.wait_ge(xnT_ready, FLOOR + (turn * 4 + 2 * half))
                            for k in range(KD):
                                for t in range(NT // 2):
                                    ins = pe.transpose(tr[half][:, k, t * P:(t + 1) * P],
                                                       xn[j][:, half * NT // 2 + t, k * P:(k + 1) * P], ident[:])
                            ins.then_inc(turned, 1)

            @block.scalar
            def _(act):
                def deviation(n, j):
                    act.wait_ge(var_ready, FLOOR + (n + 1))
                    act.activation(rstd[j][:], mv[j][:, :, 1], ACT.Sqrt, bias=eps[:, 0:1]).then_inc(dev_ready, 1)

                act.wait_ge(eps_ready, FLOOR + 1)
                deviation(0, 0)
                with act.Fori(0, B // 2) as i:
                    for j in range(2):
                        turn = i * 2 + j
                        act.wait_ge(xn_ready, FLOOR + turn)
                        deviation(turn + 1, 1 - j)
                        act.wait_ge(xn_ready, FLOOR + (turn + 1))
                        act.dma_start(xn_d[bass.ts(turn, T), :].rearrange("(t p) d -> p t d", p=P),
                                      xn[j][:]).then_inc(xn_stored[j], 16)
                        act.wait_ge(xnT_stored[j], FLOOR + i * 32)
                        for half in range(2):
                            act.wait_ge(turned, FLOOR + (turn * 2 + half + 1))
                            for k in range(KD):
                                act.activation(xnT[j][:, k, half * 512:(half + 1) * 512], tr[half][:, k, :],
                                               ACT.Copy).then_inc(xnT_ready, 1)
                        act.wait_ge(xnT_ready, FLOOR + (turn * 4 + 4))
                        st.settle(act)
                        for k in range(KD):
                            act.dma_start(xnT_d[k, :, bass.ts(turn, T)], xnT[j][:, k, :]).then_inc(xnT_stored[j], 16)
                for j in range(2):
                    act.wait_ge(xn_stored[j], FLOOR + 16 * B // 2)
                    act.wait_ge(xnT_stored[j], FLOOR + 32 * B // 2)


def qkv_rope(nc, xnT_d, wq, wk, wv, bq, bk, bv, cos_d, sin_d, qkv_d):
    W = 3 * D
    NB = 4
    HT = NT // 2
    with Stage(nc, "qkv") as st:
        w = st.sb("w", [P, KD, G, 3, GW])
        bias = st.sb("bias", [P, G, 3, GW])
        cos = st.sb("cos", [P, NT, 8])
        sin = st.sb("sin", [P, NT, 8])
        xT = [st.sb(f"xT{h}", [P, KD, HT * P]) for h in range(2)]
        y = [st.sb(f"y{j}", [P, G, 3 * GW]) for j in range(NB)]
        by_cos = [st.sb(f"by_cos{j}", [P, G, 16, 8]) for j in range(2)]
        by_sin = [st.sb(f"by_sin{j}", [P, G, 16, 8]) for j in range(2)]
        mm = [st.ps(f"mm{j}", [P, 2, 512]) for j in range(NB)]
        c_in = st.sem("c_in")
        x_in = [st.sem(f"x_in{h}") for h in range(2)]
        made = st.sem("made")
        biased = st.sem("biased")
        cos_ready = st.sem("cos_ready")
        sin_ready = st.sem("sin_ready")
        first_ready = st.sem("first_ready")
        second_ready = st.sem("second_ready")
        stored = [st.sem(f"stored{j}") for j in range(NB)]
        heads = lambda j: y[j][:, :, 0:2 * GW].rearrange("p g (h e) -> p g h e", e=8)
        table = lambda tab, u: tab[:, u:u + 1, :].rearrange("p (a b) e -> p a b e", a=1).broadcast_to([P, G, 16, 8])
        with st.block() as block:

            @block.sync
            def _(sp):
                tokens = lambda t: xnT_d[:, :, bass.ds(t * P, HT * P)].rearrange("k p t -> p k t")
                sp.dma_start(xT[0][:], tokens(0)).then_inc(x_in[0], 16)
                for c, (wm, bm) in enumerate(((wq, bq), (wk, bk), (wv, bv))):
                    for k in range(KD):
                        sp.dma_start(w[:, k, :, c, :], wm[k * P:(k + 1) * P, :].rearrange("p (g n) -> p g n", g=G)
                                     ).then_inc(c_in, 16)
                    sp.dma_start(bias[:, :, c, :], col_bcast(bm).rearrange("p (g n) -> p g n", g=G)).then_inc(c_in, 16)
                sp.dma_start(cos[:], cos_d).then_inc(c_in, 16)
                sp.dma_start(sin[:], sin_d).then_inc(c_in, 16)
                with sp.Fori(0, B) as b:
                    sp.wait_ge(made, FLOOR + b * NT)
                    sp.dma_start(xT[1][:], tokens(b * NT + HT)).then_inc(x_in[1], 16)
                    sp.wait_ge(made, FLOOR + (b * NT + HT))
                    sp.dma_start(xT[0][:], tokens((b + 1) % B * NT)).then_inc(x_in[0], 16)
                sp.wait_ge(x_in[0], FLOOR + 16 * (B + 1))

            @block.tensor
            def _(pe):
                def product(t, u, half, loads):
                    j = u % NB
                    pe.wait_ge(x_in[half], FLOOR + loads * 16)
                    tile = slice(u % HT * P, (u % HT + 1) * P)
                    for n0, n1 in ((0, 512), (512, W)):
                        for k in range(KD):
                            ins = pe.matmul(mm[j][:, n0 // 512, 0:n1 - n0], xT[half][:, k, tile],
                                            w[:, k].rearrange("p g c n -> p (g c n)")[:, n0:n1],
                                            start=k == 0, stop=k == KD - 1)
                    ins.then_inc(made, 1)

                pe.wait_ge(c_in, FLOOR + 16 * 11)
                product(0, 0, 0, 1)
                with pe.Fori(0, B) as b:
                    for u in range(NT):
                        pe.wait_ge(biased, FLOOR + b * NT + max(u + 2 - NB, 0))
                        n = u + 1
                        product(b * NT + n, n, n % NT // HT, b + (1 + n // NT))

            @block.vector
            def _(dve):
                def first(t, u):
                    j = u % NB
                    dve.wait_ge(made, FLOOR + (t + 1))
                    dve.tensor_tensor(y[j][:].rearrange("p g n -> p (g n)"),
                                      mm[j][:].rearrange("p a n -> p (a n)")[:, 0:W],
                                      bias[:].rearrange("p g c n -> p (g c n)"), ALU.add).then_inc(biased, 1)
                    dve.wait_ge(biased, FLOOR + (t + 1))
                    dve.tensor_tensor(by_sin[u % 2][:], heads(j), table(sin, u % NT), ALU.mult).then_inc(sin_ready, 1)

                dve.wait_ge(c_in, FLOOR + 16 * 11)
                first(0, 0)
                with dve.Fori(0, B) as b:
                    for u in range(NT):
                        t = b * NT + u
                        n = u + 1
                        if n >= NB:
                            dve.wait_ge(stored[n % NB], FLOOR + (b * 2 + n // NB) * 16)
                        else:
                            dve.wait_ge(stored[n % NB], FLOOR + b * 32)
                        dve.wait_ge(first_ready, FLOOR + t)
                        first(t + 1, n)
                        dve.wait_ge(cos_ready, FLOOR + (t + 1))
                        dve.wait_ge(sin_ready, FLOOR + (t + 1))
                        dve.tensor_tensor(heads(u % NB)[:, :, 1::2, :], by_sin[u % 2][:, :, 0::2, :],
                                          by_cos[u % 2][:, :, 1::2, :], ALU.add).then_inc(second_ready, 1)

            @block.gpsimd
            def _(pool):
                pool.wait_ge(c_in, FLOOR + 16 * 11)
                with pool.Fori(0, B) as b:
                    for u in range(NT):
                        t = b * NT + u
                        pool.wait_ge(second_ready, FLOOR + b * NT + max(u - 1, 0))
                        pool.wait_ge(biased, FLOOR + (t + 1))
                        pool.tensor_tensor(by_cos[u % 2][:], heads(u % NB), table(cos, u), ALU.mult
                                           ).then_inc(cos_ready, 1)
                        pool.wait_ge(cos_ready, FLOOR + (t + 1))
                        pool.wait_ge(sin_ready, FLOOR + (t + 1))
                        pool.tensor_tensor(heads(u % NB)[:, :, 0::2, :], by_cos[u % 2][:, :, 0::2, :],
                                           by_sin[u % 2][:, :, 1::2, :], ALU.subtract).then_inc(first_ready, 1)

            @block.scalar
            def _(act):
                with act.Fori(0, B) as b:
                    for u in range(NT):
                        t = b * NT + u
                        act.wait_ge(first_ready, FLOOR + (t + 1))
                        act.wait_ge(second_ready, FLOOR + (t + 1))
                        act.dma_start(qkv_d[bass.ts(t, P), :], y[u % NB][:].rearrange("p g n -> p (g n)")
                                      ).then_inc(stored[u % NB], 16)
                for j in range(NB):
                    act.wait_ge(stored[j], FLOOR + 16 * TILES // NB)


def consts(nc_unused=None):
    pos = np.arange(T, dtype=np.float32)[:, None]
    inv = (np.float32(1.0) / np.float32(10000.0) ** (np.arange(8, dtype=np.float32) / np.float32(8))).astype(np.float32)
    ang = (pos * inv[None, :]).astype(np.float32)
    lay = lambda m: np.ascontiguousarray(m.astype(np.float32).reshape(NT, P, 8).transpose(1, 0, 2))
    kaug = np.zeros((32, HG), np.float32)
    for h in range(HG):
        kaug[3 * h:3 * h + 3, h] = 1.0
    tok = np.arange(T).reshape(NT, P).T
    iota = np.broadcast_to(np.arange(T, dtype=np.float32), (P, T)).copy()
    tok2 = np.stack([tok // 32 * 32, tok % 32], -1).astype(np.float32)
    return {"iota": iota, "tok": tok2, "kaug": kaug, "cos": lay(np.cos(ang)), "sin": lay(np.sin(ang)), "ident": np.eye(P, dtype=np.float32)}
def attend(nc, qkv_d, ident_d, kaug_d, ctx_d):
    NG = B * G
    S6 = 6
    ROWS = S6 * HD
    STEPS = 2 * (NT // 2)
    UNITS = 2 * HG * NT
    SINGLES = 64
    FIRST, PLACES = 5, 70
    Q_SLOT = {"h": (0, 1, 2), "m": (3, 4), "l": (5,)}
    K_SLOT = {"h": (0, 3, 5), "m": (1, 4), "l": (2,)}
    nc.disable_value_cache = True
    with Stage(nc, "att") as st:
        gin = [st.sb(f"gin{j}", [P, NT, 3 * GW]) for j in range(2)]
        hi = st.sb("hi", [P, NT, 2 * GW], BF16)
        mid = st.sb("mid", [P, NT, 2 * GW], BF16)
        low = st.sb("low", [P, NT, 2 * GW], BF16)
        rest = st.sb("rest", [P, NT, 2 * GW])
        nat = st.sb("nat", [P, NT, 2, HG, S6, HD], BF16)
        va = [st.sb(f"va{j}", [P, NT, HG, 32]) for j in range(2)]
        QT = [st.sb(f"QT{j}", [P, HG, T], BF16) for j in range(2)]
        KT = [st.sb(f"KT{j}", [P, HG, T], BF16) for j in range(2)]
        ident = st.sb("ident", [P, P])
        identb = st.sb("identb", [P, P], BF16)
        kaug = st.sb("kaug", [P, HG])
        mx2 = st.sb("mx2", [P, NT, HG, 2])
        mx = st.sb("mx", [P, NT, HG])
        mrest = st.sb("mrest", [P, NT, HG])
        naug = st.sb("naug", [P, NT, 32], BF16)
        pt = st.sb("pt", [P, 8, 2, 512])
        osb = st.sb("osb", [P, T])
        rec = st.sb("rec", [P, NT // 2, HG])
        ctx = [st.sb(f"ctx{j}", [P, NT, HG, HD]) for j in range(2)]
        s1 = st.ps("s1", [P, 3, 512])
        sT = st.ps("sT", [P, 3, 512])
        o = st.ps("o", [P, 512])
        tr = st.ps("tr", [P, 512])
        trb = tr[:].bitcast(BF16)
        c_in = st.sem("c_in")
        g_in = [st.sem(f"g_in{j}") for j in range(2)]
        ready0 = st.sem("ready0")
        chain = st.sem("chain")
        pchain = st.sem("pchain")
        nat_done = st.sem("nat_done")
        v_ready = st.sem("v_ready")
        turned = st.sem("turned")
        evac = st.sem("evac")
        scored = st.sem("scored")
        maxed = st.sem("maxed")
        naug_ready = st.sem("naug_ready")
        aug_turned = st.sem("aug_turned")
        aug_ready = st.sem("aug_ready")
        st_done = st.sem("st_done")
        exp_done = st.sem("exp_done")
        pv_done = st.sem("pv_done")
        o_evac = st.sem("o_evac")
        o_turned = st.sem("o_turned")
        rec_ready = st.sem("rec_ready")
        ctx_ready = st.sem("ctx_ready")
        stored = [st.sem(f"stored{j}") for j in range(2)]
        qkv_v = qkv_d.rearrange("(b t p) (g n) -> b p t g n", p=P, t=NT, g=G)
        ctx_v = ctx_d.rearrange("(b t p) (g n) -> b p t g n", p=P, t=NT, g=G)

        at_place = {FIRST + u * PLACES // UNITS: u for u in range(UNITS)}

        with st.block() as block:

            @block.sync
            def _(sp):
                sp.dma_start(ident[:], ident_d).then_inc(c_in, 16)
                sp.dma_start(kaug[96:P, :], kaug_d).then_inc(c_in, 16)
                sp.dma_start(gin[0][:], qkv_v[0, :, :, 0, :]).then_inc(g_in[0], 16)
                sp.dma_start(gin[1][:], qkv_v[0, :, :, 1, :]).then_inc(g_in[1], 16)
                with sp.Fori(0, NG // 2) as i:
                    for j in range(2):
                        g = i * 2 + j
                        n = (i * 2 + (j + 2)) % NG
                        sp.wait_ge(v_ready, FLOOR + (g + 1))
                        sp.dma_start(gin[j][:], qkv_v[n // G, :, :, n % G, :]).then_inc(g_in[j], 16)
                        sp.wait_ge(ctx_ready, FLOOR + (g * 2 + 2))
                        g_ = i * 2 + j
                        sp.dma_start(ctx_v[g_ // G, :, :, g_ % G, :],
                                     ctx[j][:].rearrange("p t h e -> p t (h e)")).then_inc(stored[j], 16)
                for j in range(2):
                    sp.wait_ge(g_in[j], FLOOR + (16 * (NG // 2 + 1)))
                    sp.wait_ge(stored[j], FLOOR + 16 * NG // 2)

            @block.gpsimd
            def _(pool):
                for j in range(2):
                    ins = pool.memset(va[j][:], 0.0)
                ins.then_inc(pchain, 1)
                pool.wait_ge(pchain, FLOOR + 1)
                for j in range(2):
                    pool.memset(va[j][:, :, :, HD:HD + 1], 1.0)

                def split(n, par, loads):
                    ch = Chain(pool, pchain, n, 4)
                    ch.base = ch.base + 1
                    pool.wait_ge(g_in[par], FLOOR + loads * 16)
                    qk = gin[par][:, :, 0:2 * GW]
                    pool.wait_ge(turned, FLOOR + n * 8)
                    st.settle(pool)
                    ch.link(pool.tensor_copy(hi[:], qk))
                    ch.link(pool.tensor_tensor(rest[:], qk, hi[:], ALU.subtract))
                    st.settle(pool)
                    ch.link(pool.tensor_copy(mid[:], rest[:]))
                    ch.link(pool.tensor_tensor(low[:], rest[:], mid[:], ALU.subtract))
                    ch.close()
                    st.settle(pool)
                    for part, src in (("h", hi), ("m", mid), ("l", low)):
                        for c, slots in enumerate((Q_SLOT[part], K_SLOT[part])):
                            for s in slots:
                                v = src[:, :, c * GW:(c + 1) * GW].rearrange("p t (h e) -> p t h e", h=HG)
                                ins = pool.tensor_copy(nat[:, :, c, :, s, :], v)
                    ins.then_inc(nat_done, 1)
                    if not isinstance(n, int):
                        pool.wait_ge(pv_done, FLOOR + (n * STEPS - STEPS))
                        st.settle(pool)
                    pool.tensor_copy(va[par][:, :, :, 0:HD],
                                     gin[par][:, :, 2 * GW:3 * GW].rearrange("p t (h e) -> p t h e", h=HG)
                                     ).then_inc(v_ready, 1)

                split(0, 0, 1)
                with pool.Fori(0, NG // 2) as i:
                    for j in range(2):
                        split(i * 2 + (j + 1), 1 - j, i + 1 + j)

            @block.tensor
            def _(pe):
                def turn_parts(n, par, c):
                    if c == 0:
                        pe.wait_ge(nat_done, FLOOR + (n + 1))
                        if not isinstance(n, int):
                            pe.wait_ge(ctx_ready, FLOOR + (n * 2 - 2))
                    pe.wait_ge(evac, FLOOR + (n * 8 + c))
                    h, w = c // 2, c % 2
                    for t in range(NT):
                        ins = pe.transpose(trb[0:ROWS, t * P:(t + 1) * P],
                                           nat[:, t, w, h].rearrange("p s e -> p (s e)"), identb[:])
                    ins.then_inc(turned, 1)

                def score_unit(n, par, u):
                    h, t, c = u // (2 * NT), u // 2 % NT, u % 2
                    if u % (2 * NT) == 0:
                        pe.wait_ge(evac, FLOOR + (n * 8 + (2 * h + 2)))
                    pe.wait_ge(maxed, FLOOR + (n * UNITS + max(u - 2, 0)))
                    pe.matmul(s1[:, u % 3, :], QT[par][0:ROWS, h, t * P:(t + 1) * P],
                              KT[par][0:ROWS, h, c * 512:(c + 1) * 512], start=True, stop=True).then_inc(scored, 1)

                def turn_max(n):
                    pe.wait_ge(naug_ready, FLOOR + (n + 1))
                    pe.wait_ge(evac, FLOOR + (n * 8 + 8))
                    for t in range(NT):
                        ins = pe.transpose(trb[96:P, t * P:(t + 1) * P], naug[:, t, :], identb[:])
                    ins.then_inc(aug_turned, 1)

                def score_T(g, par, s, c, h):
                    idx = (s * 2 + c) * HG + h
                    pe.wait_ge(exp_done, FLOOR + (g * SINGLES + max(idx - 2, 0)))
                    kt = s % 4 * 2 + c
                    pe.matmul(sT[:, idx % 3, :], KT[par][:, h, kt * P:(kt + 1) * P],
                              QT[par][:, h, s // 4 * 512:(s // 4 + 1) * 512], start=True, stop=True).then_inc(st_done, 1)

                def times_v(g, par, s, c):
                    kt = s % 4 * 2 + c
                    pe.wait_ge(exp_done, FLOOR + (g * SINGLES + (s * 2 + c + 1) * HG))
                    if s == 0 and c == 0:
                        pe.wait_ge(v_ready, FLOOR + (g + 1))
                    if kt == 0:
                        pe.wait_ge(o_evac, FLOOR + (g * 2 + s // 4))
                    for h in range(HG):
                        ins = pe.matmul(o[32 * h:32 * h + 32, :], va[par][:, kt, h, :],
                                        pt[:, (s % 2) * HG + h, c, :], start=kt == 0, stop=kt == NT - 1)
                    if c == 1:
                        ins.then_inc(pv_done, 1)

                pe.wait_ge(c_in, FLOOR + 32)
                pe.wait_ge(ready0, FLOOR + 1)
                for c in range(8):
                    turn_parts(0, 0, c)
                for u in range(UNITS):
                    score_unit(0, 0, u)
                turn_max(0)
                with pe.Fori(0, NG // 2) as i:
                    for j in range(2):
                        g, n, par = i * 2 + j, i * 2 + (j + 1), 1 - j
                        pe.wait_ge(aug_ready, FLOOR + (g + 1))
                        for k in range(SINGLES):
                            s, c, h = k // 8, k // HG % 2, k % HG
                            if k % 2 == 0 and k < 16:
                                turn_parts(n, par, k // 2)
                            score_T(g, j, s, c, h)
                            place = s * 10 + c * 5 + h
                            if place in at_place:
                                score_unit(n, par, at_place[place])
                            if h == HG - 1:
                                if s > 0:
                                    times_v(g, j, s - 1, c)
                                if place + 1 in at_place:
                                    score_unit(n, par, at_place[place + 1])
                        turn_max(n)
                        for c in range(2):
                            times_v(g, j, STEPS - 1, c)
                        for q in range(2):
                            pe.wait_ge(o_evac, FLOOR + (g * 2 + q + 1))
                            if q == 0:
                                pe.wait_ge(aug_ready, FLOOR + (n + 1))
                            else:
                                pe.wait_ge(ctx_ready, FLOOR + (g * 2 + 1))
                            for t in range(4):
                                ins = pe.transpose(tr[:, t * P:(t + 1) * P], osb[:, (q * 4 + t) * P:(q * 4 + t + 1) * P],
                                                   ident[:])
                            ins.then_inc(o_turned, 1)

            @block.scalar
            def _(act):
                def evacuate(n, par, c):
                    if c == 0:
                        act.wait_ge(st_done, FLOOR + (n * SINGLES - (SINGLES if not isinstance(n, int) else 0)))
                    act.wait_ge(turned, FLOOR + (n * 8 + c + 1))
                    dst = (QT, KT)[c % 2][par]
                    act.activation(dst[0:ROWS, c // 2, :], trb[0:ROWS, :], ACT.Copy).then_inc(evac, 1)

                for c in range(8):
                    evacuate(0, 0, c)
                with act.Fori(0, NG // 2) as i:
                    for j in range(2):
                        g = i * 2 + j
                        for s in range(STEPS):
                            act.wait_ge(pv_done, FLOOR + (g * STEPS + max(s - 1, 0)))
                            for q in range(2 * HG):
                                c, h = q // HG, q % HG
                                k = s * 2 * HG + q
                                if k % 2 == 0 and k < 16:
                                    evacuate(i * 2 + (j + 1), 1 - j, k // 2)
                                act.wait_ge(st_done, FLOOR + (g * SINGLES + (k + 1)))
                                act.activation(pt[:, (s % 2) * HG + h, c], sT[:, k % 3, :], ACT.Exp,
                                               scale=HD ** -0.5).then_inc(exp_done, 1)

            @block.vector
            def _(dve):
                dve.wait_ge(c_in, FLOOR + 32)
                for j in range(2):
                    for h in range(HG):
                        dve.tensor_copy(KT[j][96:P, h, :], kaug[96:P, h:h + 1].broadcast_to([32, T]))
                dve.memset(naug[:], 0.0)
                dve.tensor_copy(identb[:], ident[:]).then_inc(ready0, 1)

                def take_max(n, u):
                    dve.wait_ge(scored, FLOOR + (n * UNITS + u + 1))
                    h, t, c = u // (2 * NT), u // 2 % NT, u % 2
                    dve.tensor_reduce(mx2[:, t, h, c:c + 1], s1[:, u % 3, :], AX.X, ALU.max).then_inc(maxed, 1)

                def split_max(n):
                    ch = Chain(dve, chain, n, 5)
                    dve.wait_ge(maxed, FLOOR + (n * UNITS + UNITS))
                    dve.wait_ge(aug_turned, FLOOR + n)
                    ch.link(dve.tensor_tensor(mx[:], mx2[:, :, :, 0], mx2[:, :, :, 1], ALU.max))
                    ch.link(dve.tensor_scalar(naug[:, :, 0:12:3], mx[:], -1.0, None, ALU.mult))
                    ch.link(dve.scalar_tensor_tensor(mrest[:], mx[:], -1.0, naug[:, :, 0:12:3], ALU.mult, ALU.subtract))
                    ch.link(dve.tensor_copy(naug[:, :, 1:12:3], mrest[:]))
                    dve.tensor_tensor(naug[:, :, 2:12:3], mrest[:], naug[:, :, 1:12:3], ALU.subtract
                                      ).then_inc(naug_ready, 1)
                    return ch

                def place_max(n, par, ch):
                    dve.wait_ge(aug_turned, FLOOR + (n + 1))
                    ch.link(dve.tensor_copy(QT[par][96:P, 0, :], trb[96:P, :]))
                    ch.close()
                    for h in range(1, HG):
                        ins = dve.tensor_copy(QT[par][96:P, h, :], QT[par][96:P, 0, :])
                    ins.then_inc(aug_ready, 1)

                for u in range(UNITS):
                    take_max(0, u)
                place_max(0, 0, split_max(0))
                with dve.Fori(0, NG // 2) as i:
                    for j in range(2):
                        g, n, par = i * 2 + j, i * 2 + (j + 1), 1 - j

                        def o_out(q):
                            dve.wait_ge(pv_done, FLOOR + (g * STEPS + 4 * q + 4))
                            dve.wait_ge(o_turned, FLOOR + g * 2)
                            dve.tensor_copy(osb[:, q * 512:(q + 1) * 512], o[:]).then_inc(o_evac, 1)

                        for place in range(STEPS * 10):
                            if place in at_place:
                                take_max(n, at_place[place])
                            if place == 50:
                                o_out(0)
                        place_max(n, par, split_max(n))
                        o_out(1)
                        dve.wait_ge(stored[j], FLOOR + i * 16)
                        trv = tr[:].rearrange("p (t h e) -> p t h e", t=4, h=HG)
                        for q in range(2):
                            dve.wait_ge(o_turned, FLOOR + (g * 2 + q + 1))
                            dve.reciprocal(rec[:], trv[:, :, :, HD]).then_inc(rec_ready, 1)
                            dve.wait_ge(rec_ready, FLOOR + (g * 2 + q + 1))
                            dve.tensor_tensor(ctx[j][:, 4 * q:4 * q + 4], trv[:, :, :, 0:HD],
                                              rec[:].rearrange("p t (h a) -> p t h a", a=1).broadcast_to([P, 4, HG, HD]),
                                              ALU.mult).then_inc(ctx_ready, 1)
    nc.disable_value_cache = False
def project(nc, tag, ctx_d, w_d, b_d, x_d, ident_d, out_d):
    TC = 4
    TURNS = TILES // TC
    U = 4
    N = TC * P
    rows = lambda d, t: d[bass.ds(t * N, N), :].rearrange("(t p) d -> p t d", p=P)
    with Stage(nc, tag) as st:
        w = st.sb("w", [P, KD, D])
        bias = st.sb("bias", [P, D])
        ident = st.sb("ident", [P, P])
        c = [st.sb(f"c{j}", [P, TC, D]) for j in range(U)]
        x = [st.sb(f"x{j}", [P, TC, D]) for j in range(U)]
        cT = [st.sb(f"cT{j}", [P, TC, KD, P]) for j in range(2)]
        tr = [st.ps(f"tr{j}", [P, TC, KD, P]) for j in range(2)]
        mm = [st.ps(f"mm{j}", [P, TC, D]) for j in range(2)]
        w_in = st.sem("w_in")
        ctx_in = [st.sem(f"ctx_in{j}") for j in range(U)]
        x_in = [st.sem(f"x_in{j}") for j in range(U)]
        turned = st.sem("turned")
        cT_ready = st.sem("cT_ready")
        biased = st.sem("biased")
        made = st.sem("made")
        summed = st.sem("summed")
        stored = [st.sem(f"stored{j}") for j in range(U)]
        with st.block() as block:

            @block.sync
            def _(sp):
                sp.dma_start(ident[:], ident_d).then_inc(w_in, 16)
                sp.dma_start(c[0][:], rows(ctx_d, 0)).then_inc(ctx_in[0], 16)
                sp.dma_start(w[:], w_d.rearrange("(k p) n -> p k n", p=P)).then_inc(w_in, 16)
                sp.dma_start(bias[:], col_bcast(b_d)).then_inc(w_in, 16)
                sp.dma_start(c[1][:], rows(ctx_d, 1)).then_inc(ctx_in[1], 16)
                with sp.Fori(0, TURNS // U) as i:
                    for j in range(U):
                        t = i * U + j
                        sp.wait_ge(stored[j], FLOOR + i * 16)
                        sp.dma_start(x[j][:], rows(x_d, t)).then_inc(x_in[j], 16)
                        sp.wait_ge(turned, FLOOR + i * U + max(j - 1, 0))
                        sp.dma_start(c[(j + 2) % U][:], rows(ctx_d, (t + 2) % TURNS)).then_inc(ctx_in[(j + 2) % U], 16)
                for j in range(2):
                    sp.wait_ge(ctx_in[j], FLOOR + 16 * (TURNS // U + 1))

            @block.tensor
            def _(pe):
                def turn_context(j, u, loads):
                    pe.wait_ge(ctx_in[u], FLOOR + loads * 16)
                    for q in range(TC):
                        for k in range(KD):
                            ins = pe.transpose(tr[j][:, q, k, :], c[u][:, q, k * P:(k + 1) * P], ident[:])
                    ins.then_inc(turned, 1)

                pe.wait_ge(w_in, FLOOR + 48)
                turn_context(0, 0, 1)
                with pe.Fori(0, TURNS // U) as i:
                    for u in range(U):
                        t, j = i * U + u, u % 2
                        pe.wait_ge(cT_ready, FLOOR + t)
                        turn_context(1 - j, (u + 1) % U, i + (1 + (u + 1) // U))
                        pe.wait_ge(cT_ready, FLOOR + (t + 1))
                        pe.wait_ge(summed, FLOOR + i * U + max(u - 1, 0))
                        for q in range(TC):
                            for k in range(KD):
                                ins = pe.matmul(mm[j][:, q, :], cT[j][:, q, k, :], w[:, k, :],
                                                start=k == 0, stop=k == KD - 1)
                        ins.then_inc(made, 1)

            @block.scalar
            def _(act):
                act.wait_ge(turned, FLOOR + 1)
                act.activation(cT[0][:], tr[0][:], ACT.Copy).then_inc(cT_ready, 1)
                with act.Fori(0, TURNS // U) as i:
                    for u in range(U):
                        t, j = i * U + u, u % 2
                        act.wait_ge(turned, FLOOR + (t + 2))
                        act.wait_ge(made, FLOOR + t)
                        act.activation(cT[1 - j][:], tr[1 - j][:], ACT.Copy).then_inc(cT_ready, 1)
                        act.wait_ge(summed, FLOOR + (t + 1))
                        act.dma_start(rows(out_d, t), x[u][:]).then_inc(stored[u], 16)
                for u in range(U):
                    act.wait_ge(stored[u], FLOOR + 16 * TURNS // U)

            @block.vector
            def _(dve):
                with dve.Fori(0, TURNS // U) as i:
                    for u in range(U):
                        t, j = i * U + u, u % 2
                        dve.wait_ge(biased, FLOOR + (t + 1))
                        dve.wait_ge(made, FLOOR + (t + 1))
                        dve.tensor_tensor(x[u][:], x[u][:], mm[j][:], ALU.add).then_inc(summed, 1)

            @block.gpsimd
            def _(pool):
                pool.wait_ge(w_in, FLOOR + 48)
                with pool.Fori(0, TURNS // U) as i:
                    for j in range(U):
                        pool.wait_ge(x_in[j], FLOOR + (i * 16 + 16))
                        pool.tensor_tensor(x[j][:], x[j][:],
                                           bias[:].rearrange("p (a n) -> p a n", a=1).broadcast_to([P, TC, D]),
                                           ALU.add).then_inc(biased, 1)


def route(nc, xnT_d, gate_d, ident_d, pos_d, aff_d):
    with Stage(nc, "rt") as st:
        ident = st.sb("ident", [P, P])
        gw = st.sb("gw", [P, KD, E])
        xT = [st.sb(f"xT{j}", [P, KD, T]) for j in range(2)]
        lg = st.sb("lg", [P, NT, E])
        ex = st.sb("ex", [P, NT, E])
        mx = st.sb("mx", [P, NT])
        sm = st.sb("sm", [P, NT])
        aff = st.sb("aff", [P, NT, B, E])
        work = st.sb("work", [B * E, T])
        sel = st.sb("sel", [B * E, T])
        ones = st.sb("ones", [B * E, T])
        pos = st.sb("pos", [B * E, T])
        m8 = st.sb("m8", [B * E, 8])
        posT = st.sb("posT", [P, NT, B * E])
        lp = [st.ps(f"lp{j}", [P, NT, E]) for j in range(2)]
        rows = st.ps("rows", [B * E, T])
        cols = st.ps("cols", [P, NT, B * E])
        c_in = st.sem("c_in")
        x_in = [st.sem(f"x_in{j}") for j in range(2)]
        made = st.sem("made")
        read = st.sem("read")
        shifted = st.sem("shifted")
        exped = st.sem("exped")
        chain = st.sem("chain")
        aff_ready = st.sem("aff_ready")
        turned = st.sem("turned")
        pos_ready = st.sem("pos_ready")
        turned_back = st.sem("turned_back")
        posT_ready = st.sem("posT_ready")
        stored = st.sem("stored")
        PER = 6
        with st.block() as block:

            @block.sync
            def _(sp):
                sp.dma_start(ident[:], ident_d).then_inc(c_in, 16)
                sp.dma_start(gw[:], gate_d.rearrange("(k p) e -> p k e", p=P)).then_inc(c_in, 16)
                with sp.Fori(0, B // 2) as i:
                    for j in range(2):
                        b = i * 2 + j
                        sp.wait_ge(made, FLOOR + i * 2)
                        sp.dma_start(xT[j][:], xnT_d[:, :, bass.ts(b, T)].rearrange("k p t -> p k t")
                                     ).then_inc(x_in[j], 16)
                sp.wait_ge(aff_ready, FLOOR + 1)
                sp.dma_start(aff_d, aff[:]).then_inc(stored, 16)
                sp.wait_ge(posT_ready, FLOOR + 1)
                sp.dma_start(pos_d, posT[:]).then_inc(stored, 16)
                sp.wait_ge(stored, FLOOR + 32)

            @block.tensor
            def _(pe):
                pe.wait_ge(c_in, FLOOR + 32)
                with pe.Fori(0, B // 2) as i:
                    for j in range(2):
                        pe.wait_ge(x_in[j], FLOOR + (i * 16 + 16))
                        pe.wait_ge(read, FLOOR + i * 2)
                        for t in range(NT):
                            for k in range(KD):
                                ins = pe.matmul(lp[j][:, t, :], xT[j][:, k, t * P:(t + 1) * P], gw[:, k, :],
                                                start=k == 0, stop=k == KD - 1)
                        ins.then_inc(made, 1)
                pe.wait_ge(aff_ready, FLOOR + 1)
                for t in range(NT):
                    ins = pe.transpose(rows[:, t * P:(t + 1) * P], aff[:, t].rearrange("p b e -> p (b e)"), ident[:])
                ins.then_inc(turned, 1)
                pe.wait_ge(pos_ready, FLOOR + 1)
                for t in range(NT):
                    ins = pe.transpose(cols[:, t, :], pos[:, t * P:(t + 1) * P], ident[0:B * E, 0:B * E])
                ins.then_inc(turned_back, 1)

            @block.scalar
            def _(act):
                with act.Fori(0, B) as b:
                    act.wait_ge(shifted, FLOOR + (b + 1))
                    act.activation(ex[:], lg[:], ACT.Exp).then_inc(exped, 1)

            @block.vector
            def _(dve):
                dve.memset(ones[:], 1.0)
                with dve.Fori(0, B // 2) as i:
                    for j in range(2):
                        b = i * 2 + j
                        ch = Chain(dve, chain, b, 4)
                        dve.wait_ge(made, FLOOR + (b + 1))
                        ch.link(dve.tensor_reduce(mx[:], lp[j][:], AX.X, ALU.max))
                        dve.tensor_tensor(lg[:], lp[j][:], mx[:].rearrange("p (t a) -> p t a", a=1).broadcast_to([P, NT, E]),
                                          ALU.subtract).then_inc(shifted, 1)
                        dve.wait_ge(shifted, FLOOR + (b + 1))
                        dve.wait_ge(exped, FLOOR + (b + 1))
                        ch.link(dve.tensor_reduce(sm[:], ex[:], AX.X, ALU.add))
                        ch.link(dve.reciprocal(sm[:], sm[:]))
                        ch.link(dve.tensor_tensor(aff[:, :, b, :], ex[:],
                                                  sm[:].rearrange("p (t a) -> p t a", a=1).broadcast_to([P, NT, E]),
                                                  ALU.mult))
                        ch.close()
                        dve.sem_inc(read, 1)
                dve.sem_inc(aff_ready, 1)
                dve.wait_ge(turned, FLOOR + 1)
                ch = Chain(dve, chain)
                ch.base = 4 * B
                ch.link(dve.tensor_copy(work[:], rows[:]))
                with dve.Fori(0, CAP // 8) as r:
                    cr = Chain(dve, chain, r, 2)
                    cr.base = cr.base + (4 * B + 1)
                    cr.link(dve.max(m8[:], work[:]))
                    st.settle(dve)
                    cr.link(dve.match_replace(work[:], m8[:], work[:], -1.0))
                ch.base += 2 * CAP // 8
                ch.link(dve.tensor_scalar(sel[:], work[:], 0.0, None, ALU.is_lt))
                ch.link(dve.tensor_tensor_scan(pos[:], ones[:], sel[:], 0.0, ALU.mult, ALU.add))
                ch.link(dve.tensor_tensor(pos[:], pos[:], sel[:], ALU.mult))
                dve.tensor_scalar(pos[:], pos[:], -1.0, None, ALU.add).then_inc(pos_ready, 1)
                dve.wait_ge(turned_back, FLOOR + 1)
                dve.tensor_copy(posT[:], cols[:]).then_inc(posT_ready, 1)


def experts(nc, xn_d, pos_d, aff_d, wg_d, wu_d, wd_d, iota_d, tok_d, x_d, out_d):
    NB = 4
    NI = I // P
    NS = CAP // P
    WAY = (B // NB) * E
    xn_v = xn_d.rearrange("(b t p) d -> b p t d", p=P, t=NT)
    x_v = x_d.rearrange("(b t p) d -> b p t d", p=P, t=NT)
    out_v = out_d.rearrange("(b t p) d -> b p t d", p=P, t=NT)
    with Stage(nc, "moe") as st:
        iota = st.sb("iota", [P, T])
        iotab = st.sb("iotab", [P, CAP], BF16)
        posT = st.sb("posT", [P, NT, B * E])
        aff = st.sb("aff", [P, NT, B * E])
        arest = st.sb("arest", [P, NT, B * E])
        affs = st.sb("affs", [P, NT, B * E, 5], BF16)
        tok = st.sb("tok", [P, NT, 2])
        stage = st.sb("stage", [P, NT, D])
        xs = [st.sb(f"xs{b}", [P, NT, 3, D], BF16) for b in range(NB)]
        acc = [st.sb(f"acc{b}", [P, NT, D]) for b in range(NB)]
        wg = st.sb("wg", [P, KD, I])
        wu = st.sb("wu", [P, KD, I])
        wd = st.sb("wd", [P, NI, D])
        onehot = st.sb("onehot", [P, NT, CAP], BF16)
        onehotT = st.sb("onehotT", [P, NS, T])
        gi = st.sb("gi", [P, NS, 5])
        gate = st.sb("gate", [P, NS])
        idx = st.sb("idx", [P, NS])
        xsel = st.sb("xsel", [P, KD, CAP])
        sg = st.sb("sg", [P, NI, CAP])
        hT = st.sb("hT", [P, NI, CAP])
        y = st.sb("y", [P, NS, D])
        pg = st.ps("pg", [P, KD, CAP])
        pi = st.ps("pi", [P, NS, 5])
        gp = st.ps("gp", [P, NI, CAP])
        up = st.ps("up", [P, NI, CAP])
        yp = st.ps("yp", [P, NS, D])
        sp_ = st.ps("sp", [P, 2, D])
        c_in = st.sem("c_in")
        w_in = st.sem("w_in")
        wd_in = st.sem("wd_in")
        stage_in = st.sem("stage_in")
        acc_in = [st.sem(f"acc_in{b}") for b in range(NB)]
        acc_out = [st.sem(f"acc_out{b}") for b in range(NB)]
        ready0 = st.sem("ready0")
        split = st.sem("split")
        pchain = st.sem("pchain")
        chain = st.sem("chain")
        hot_ready = st.sem("hot_ready")
        gathered = st.sem("gathered")
        xsel_ready = st.sem("xsel_ready")
        hotT_ready = st.sem("hotT_ready")
        gu_done = st.sem("gu_done")
        silued = st.sem("silued")
        h_ready = st.sem("h_ready")
        down = st.sem("down")
        y_ready = st.sem("y_ready")
        scat = st.sem("scat")
        added = st.sem("added")
        with st.block() as block:

            @block.sync
            def _(sp):
                sp.dma_start(iota[:], iota_d).then_inc(c_in, 16)
                sp.dma_start(posT[:], pos_d).then_inc(c_in, 16)
                sp.dma_start(aff[:], aff_d.rearrange("p t b e -> p t (b e)")).then_inc(c_in, 16)
                sp.dma_start(tok[:], tok_d).then_inc(c_in, 16)
                def weights(i, e):
                    sp.wait_ge(gu_done, FLOOR + i * NB)
                    sp.dma_start(wg[:], wg_d[e, :, :].rearrange("(k p) n -> p k n", p=P)).then_inc(w_in, 16)
                    sp.dma_start(wu[:], wu_d[e, :, :].rearrange("(k p) n -> p k n", p=P)).then_inc(w_in, 16)
                    sp.wait_ge(down, FLOOR + i * NB)
                    sp.dma_start(wd[:], wd_d[e, :, :].rearrange("(k p) n -> p k n", p=P)).then_inc(wd_in, 16)

                with sp.Fori(0, E) as i:
                    weights(i, i)
                for b in range(NB):
                    sp.wait_ge(split, FLOOR + (NB + b))
                    sp.dma_start(stage[:], xn_v[NB + b]).then_inc(stage_in, 16)
                weights(E, 0)
                for b in range(NB):
                    sp.wait_ge(added, FLOOR + (4 * (NB * (E - 1) + b + 1)))
                    sp.dma_start(out_v[b], acc[b][:]).then_inc(acc_out[b], 16)
                for b in range(NB):
                    sp.wait_ge(acc_out[b], FLOOR + 16)
                    sp.dma_start(acc[b][:], x_v[NB + b]).then_inc(acc_in[b], 16)
                with sp.Fori(E + 1, 2 * E) as i:
                    weights(i, i - E)
                for b in range(NB):
                    sp.wait_ge(added, FLOOR + (4 * (NB * (2 * E - 1) + b + 1)))
                    sp.dma_start(out_v[NB + b], acc[b][:]).then_inc(acc_out[b], 16)
                for b in range(NB):
                    sp.wait_ge(acc_out[b], FLOOR + 32)

            @block.scalar
            def _(act):
                for b in range(NB):
                    act.wait_ge(split, FLOOR + b) if b else None
                    act.dma_start(stage[:], xn_v[b]).then_inc(stage_in, 16)
                    act.dma_start(acc[b][:], x_v[b]).then_inc(acc_in[b], 16)
                with act.Fori(0, WAY) as i:
                    for b in range(NB):
                        turn = i * NB + b
                        act.wait_ge(gathered, FLOOR + (turn + 1))
                        act.activation(xsel[:], pg[:], ACT.Copy).then_inc(xsel_ready, 1)
                        act.wait_ge(gu_done, FLOOR + (turn + 1))
                        act.activation(sg[:], gp[:], ACT.Silu).then_inc(silued, 1)
                        act.wait_ge(down, FLOOR + (turn + 1))
                        act.wait_ge(scat, FLOOR + turn * 4)
                        for s in range(NS):
                            act.activation(y[:, s, :], yp[:, s, :], ACT.Copy, scale=gate[:, s:s + 1]
                                           ).then_inc(y_ready, 1)

            @block.gpsimd
            def _(pool):
                ch = Chain(pool, pchain)

                def split_batch(b):
                    ch.link(pool.tensor_copy(xs[b][:, :, 0, :], stage[:]))
                    ch.link(pool.tensor_tensor(stage[:], stage[:], xs[b][:, :, 0, :], ALU.subtract))
                    ch.link(pool.tensor_copy(xs[b][:, :, 1, :], stage[:]))
                    pool.tensor_tensor(xs[b][:, :, 2, :], stage[:], xs[b][:, :, 1, :], ALU.subtract).then_inc(split, 1)

                for b in range(NB):
                    pool.wait_ge(stage_in, FLOOR + (16 * (b + 1)))
                    split_batch(b)
                for b in range(NB):
                    pool.wait_ge(gathered, FLOOR + (NB * (E - 1) + b + 1))
                    pool.wait_ge(stage_in, FLOOR + (16 * (NB + b + 1)))
                    split_batch(b)

            @block.vector
            def _(dve):
                ch0 = Chain(dve, chain)
                dve.wait_ge(c_in, FLOOR + 64)
                ch0.link(dve.tensor_copy(iotab[:], iota[:, 0:CAP]))
                ch0.link(dve.tensor_copy(affs[:, :, :, 0], aff[:]))
                ch0.link(dve.tensor_tensor(arest[:], aff[:], affs[:, :, :, 0], ALU.subtract))
                ch0.link(dve.tensor_copy(affs[:, :, :, 1], arest[:]))
                ch0.link(dve.tensor_tensor(affs[:, :, :, 2], arest[:], affs[:, :, :, 1], ALU.subtract))
                for c in range(2):
                    ch0.link(dve.tensor_copy(affs[:, :, :, 3 + c], tok[:, :, c:c + 1].broadcast_to([P, NT, B * E])))
                N0 = ch0.n

                def make_onehot(n, col):
                    dve.wait_ge(gathered, FLOOR + n)
                    for t in range(NT):
                        ins = dve.tensor_scalar(onehot[:, t, :], iotab[:], posT[:, t, bass.ds(col, 1)], None, ALU.is_equal)
                    ins.then_inc(hot_ready, 1)

                make_onehot(0, 0)
                with dve.Fori(0, WAY) as i:
                    for b in range(NB):
                        turn = i * NB + b
                        ch = Chain(dve, chain, turn, 4)
                        ch.base = ch.base + N0
                        dve.wait_ge(gathered, FLOOR + (turn + 1))
                        ch.link(dve.tensor_copy(gi[:], pi[:]))
                        dve.wait_ge(y_ready, FLOOR + turn * NS)
                        ch.link(dve.tensor_tensor(gate[:], gi[:, :, 0], gi[:, :, 1], ALU.add))
                        ch.link(dve.tensor_tensor(gate[:], gate[:], gi[:, :, 2], ALU.add))
                        ch.link(dve.tensor_tensor(idx[:], gi[:, :, 3], gi[:, :, 4], ALU.add))
                        ch.close()
                        dve.wait_ge(scat, FLOOR + turn * 4)
                        for s in range(NS):
                            ins = dve.tensor_scalar(onehotT[:, s, :], iota[:], idx[:, s:s + 1], None, ALU.is_equal)
                        ins.then_inc(hotT_ready, 1)
                        n = turn + 1
                        if b < NB - 1:
                            col = ((i // E) * NB + (b + 1)) * E + i % E
                        else:
                            i1 = (i + 1) % WAY
                            col = ((i1 // E) * NB) * E + i1 % E
                        make_onehot(n, col)
                        dve.wait_ge(silued, FLOOR + (turn + 1))
                        dve.wait_ge(down, FLOOR + turn)
                        dve.tensor_tensor(hT[:], sg[:], up[:], ALU.mult).then_inc(h_ready, 1)
                        dve.wait_ge(acc_in[b], FLOOR + ((i // E + 1) * 16))
                        for q in range(4):
                            dve.wait_ge(scat, FLOOR + (turn * 4 + (q + 1)))
                            dve.tensor_tensor(acc[b][:, 2 * q:2 * q + 2, :], acc[b][:, 2 * q:2 * q + 2, :], sp_[:],
                                              ALU.add).then_inc(added, 1)

            @block.tensor
            def _(pe):
                def gather(n, b, col, need):
                    pe.wait_ge(hot_ready, FLOOR + (n + 1))
                    pe.wait_ge(split, FLOOR + need)
                    pe.wait_ge(xsel_ready, FLOOR + n)
                    for k in range(KD):
                        for t in range(NT):
                            for part in range(3):
                                pe.matmul(pg[:, k, :], xs[b][:, t, part, k * P:(k + 1) * P], onehot[:, t, :],
                                          start=t == 0 and part == 0, stop=t == NT - 1 and part == 2)
                    pe.wait_ge(hotT_ready, FLOOR + n)
                    for s in range(NS):
                        for t in range(NT):
                            ins = pe.matmul(pi[:, s, :], onehot[:, t, s * P:(s + 1) * P],
                                            affs[:, t, bass.ds(col, 1), :].rearrange("p a c -> p (a c)"),
                                            start=t == 0, stop=t == NT - 1)
                    ins.then_inc(gathered, 1)

                gather(0, 0, 0, 1)
                with pe.Fori(0, WAY) as i:
                    for b in range(NB):
                        turn = i * NB + b
                        if b == 0:
                            pe.wait_ge(w_in, FLOOR + (i * 32 + 32))
                            pe.wait_ge(wd_in, FLOOR + (i * 16 + 16))
                        pe.wait_ge(xsel_ready, FLOOR + (turn + 1))
                        pe.wait_ge(h_ready, FLOOR + turn)
                        for w_, o_ in ((wg, gp), (wu, up)):
                            for m in range(NI):
                                for k in range(KD):
                                    ins = pe.matmul(o_[:, m, :], w_[:, k, m * P:(m + 1) * P], xsel[:, k, :],
                                                    start=k == 0, stop=k == KD - 1)
                        ins.then_inc(gu_done, 1)
                        if b < NB - 1:
                            gather(turn + 1, b + 1, ((i // E) * NB + (b + 1)) * E + i % E, (i // E) * NB + (b + 2))
                        else:
                            i1 = (i + 1) % WAY
                            gather(turn + 1, 0, ((i1 // E) * NB) * E + i1 % E, (i1 // E) * NB + 1)
                        pe.wait_ge(h_ready, FLOOR + (turn + 1))
                        pe.wait_ge(y_ready, FLOOR + turn * NS)
                        for s in range(NS):
                            for m in range(NI):
                                ins = pe.matmul(yp[:, s, :], hT[:, m, s * P:(s + 1) * P], wd[:, m, :],
                                                start=m == 0, stop=m == NI - 1)
                        ins.then_inc(down, 1)
                        pe.wait_ge(y_ready, FLOOR + (turn * NS + NS))
                        pe.wait_ge(hotT_ready, FLOOR + (turn + 1))
                        for q in range(4):
                            pe.wait_ge(added, FLOOR + (turn * 4 + q))
                            for t in range(2):
                                for s in range(NS):
                                    ins = pe.matmul(sp_[:, t, :], onehotT[:, s, (2 * q + t) * P:(2 * q + t + 1) * P],
                                                    y[:, s, :], start=s == 0, stop=s == NS - 1)
                            ins.then_inc(scat, 1)
PI = 3.14159265358979
TWO_PI_PARTS = (6.28125, 0.0019353071795864769)
PI_IN = 3.1415925
ROUND = 12582912.0


def phases(nc, xn_d, xnT_d, x_d, ppT_d, wpv, bpv, wk, bk, wkv, bkv, wg1, bg1, wg2, bg2, wb1, bb1, wb2, bb2,
           ln_g, ln_b, wo, bo, out_d):
    C = 2
    NAMES = ["k0", "kv0", "pv0", "k1", "kv1", "pv1", "gh0", "gh1", "bh", "gate", "z", "mean", "var", "outA", "outB"]
    FRONT = NAMES[6:11]
    NPROD, NPRE = len(NAMES), len(FRONT)
    SLOT = {n: q % 4 for q, n in enumerate(NAMES)}

    def made_at(name, turn):
        if turn is None:
            return FRONT.index(name) + 1
        return turn * NPROD + (NPRE + NAMES.index(name) + 1)

    def before(name, turn):
        s = SLOT[name]
        if turn is None:
            return [n for n in FRONT if SLOT[n] == s].index(name)
        mates = [n for n in NAMES if SLOT[n] == s]
        return turn * len(mates) + (len([n for n in FRONT if SLOT[n] == s]) + mates.index(name))

    with Stage(nc, "ph") as st:
        cosP = st.sb("cosP", [P, KD, T])
        sinP = st.sb("sinP", [P, KD, T])
        wpv_s, wk_s, wkv_s, wo_s = [st.sb(n, [P, KD, D]) for n in ("wpv", "wk", "wkv", "wo")]
        wg1_s = st.sb("wg1", [P, 2 * KD, D])
        wb1_s = st.sb("wb1", [P, KD, P])
        wg2_c = st.sb("wg2c", [P, KD])
        wb2_c = st.sb("wb2c", [P, 2])
        wb2_n = st.sb("wb2n", [P, 1])
        wg2_s = st.sb("wg2", [P, KD, P])
        wbd_s = st.sb("wbd", [P, P])
        col = st.sb("col", [P, 12])
        bb1_c = st.sb("bb1", [P, 1])
        bg2_c = st.sb("bg2", [P, 1])
        bb2_c = st.sb("bb2", [P, 2])
        bd = st.sb("bd", [P, 2])
        bo_r = st.sb("bo", [P, D])
        ones = st.sb("ones", [P, T])
        avg = st.sb("avg", [P, P])
        avg16 = st.sb("avg16", [P, P])
        xT = [st.sb(f"xT{j}", [P, KD, 1 + T]) for j in range(2)]
        gh = st.sb("gh", [P, KD, T])
        bh = st.sb("bh", [P, T])
        gt = [st.sb(f"gt{j}", [P, T]) for j in range(2)]
        w0 = [st.sb(f"w0{j}", [P, T]) for j in range(2)]
        w1 = [st.sb(f"w1{j}", [P, T]) for j in range(2)]
        th = st.sb("th", [P, T])
        hs = st.sb("hs", [P, T])
        kc = st.sb("kc", [P, 1 + T])
        ks = st.sb("ks", [P, 1 + T])
        kvg = st.sb("kvg", [P, T])
        a = st.sb("a", [P, T])
        b_ = st.sb("b", [P, T])
        sa = st.sb("sa", [P, T])
        sb_ = st.sb("sb", [P, T])
        mc = st.sb("mc", [P, T])
        ms = st.sb("ms", [P, T])
        bl = st.sb("bl", [P, KD, T])
        sq = st.sb("sq", [P, KD, T])
        cs = st.sb("cs", [P, T])
        vd = st.sb("vd", [P, T])
        eps = st.sb("eps", [P, 1])
        base = st.sb("base", [P, NT, D])
        xnat = st.sb("xnat", [P, NT, D])
        ps = [st.ps(f"ps{s}", [P, C, 512]) for s in range(4)]
        psf = [q[:].rearrange("p c n -> p (c n)") for q in ps]
        c_in = st.sem("c_in")
        x_in = [st.sem(f"x_in{j}") for j in range(2)]
        nat_in = st.sem("nat_in")
        made = st.sem("made")
        freed = [st.sem(f"freed{s}") for s in range(4)]
        ready0 = st.sem("ready0")
        zeroed = st.sem("zeroed")
        chain = st.sem("chain")
        achain = st.sem("achain")
        pchain = st.sem("pchain")
        cs_ready = st.sem("cs_ready")
        dev_ready = st.sem("dev_ready")
        reduced = st.sem("reduced")
        k_ready = st.sem("k_ready")
        kc_ready = st.sem("kc_ready")
        m_ready = st.sem("m_ready")
        m_used = st.sem("m_used")
        blended = st.sem("blended")
        cent = st.sem("cent")
        squared = st.sem("squared")
        ln_ready = st.sem("ln_ready")
        base_ready = st.sem("base_ready")
        stored = st.sem("stored")

        def taken(eng, name, turn):
            eng.wait_ge(freed[SLOT[name]], FLOOR + (before(name, turn) + 1))

        with st.block() as block:

            @block.sync
            def _(sp):
                for dst, src in ((wpv_s, wpv), (wk_s, wk), (wkv_s, wkv), (wo_s, wo), (wg1_s, wg1), (wb1_s, wb1)):
                    sp.dma_start(dst[:], src.rearrange("(k p) n -> p k n", p=P)).then_inc(c_in, 16)
                sp.dma_start(wg2_c[:], wg2.rearrange("(k p) a -> p (k a)", p=P), allow_slow_non_contiguous=True).then_inc(c_in, 16)
                sp.dma_start(wb2_c[:], wb2).then_inc(c_in, 16)
                for q, v in enumerate((bpv, bk, bkv, bg1, ln_g, ln_b)):
                    sp.dma_start(col[:, 2 * q:2 * q + 2], v.rearrange("(k p) -> p k", p=P),
                                 allow_slow_non_contiguous=True).then_inc(c_in, 16)
                sp.dma_start(bb1_c[:], bb1.rearrange("(p a) -> p a", a=1)).then_inc(c_in, 16)
                sp.dma_start(bg2_c[:], col_bcast(bg2)).then_inc(c_in, 16)
                sp.dma_start(bb2_c[:], col_bcast(bb2)).then_inc(c_in, 16)
                sp.dma_start(bo_r[:], col_bcast(bo)).then_inc(c_in, 16)
                sp.dma_start(cosP[:], ppT_d.rearrange("(k p) t -> p k t", p=P)).then_inc(c_in, 16)
                sp.wait_ge(zeroed, FLOOR + 1)
                for k in range(KD):
                    sp.dma_start(xT[0][:, k, 1:], xnT_d[k, :, 0:T]).then_inc(x_in[0], 16)
                with sp.Fori(0, B // 2) as i:
                    for j in range(2):
                        turn, n = i * 2 + j, i * 2 + (j + 1)
                        sp.wait_ge(made, FLOOR + turn * NPROD)
                        for k in range(KD):
                            sp.dma_start(xT[1 - j][:, k, 1:], xnT_d[k, :, bass.ds((n % B) * T, T)]).then_inc(x_in[1 - j], 16)
                        sp.wait_ge(stored, FLOOR + turn * 16)
                        sp.dma_start(base[:], x_d[bass.ds(turn * T, T), :].rearrange("(t p) d -> p t d", p=P)).then_inc(nat_in, 16)
                        sp.wait_ge(base_ready, FLOOR + turn)
                        sp.dma_start(xnat[:], xn_d[bass.ds(turn * T, T), :].rearrange("(t p) d -> p t d", p=P)).then_inc(nat_in, 16)
                        taken(sp, "outA", turn)
                        st.settle(sp)
                        taken(sp, "outB", turn)
                        st.settle(sp)
                        sp.dma_start(out_d[bass.ds(turn * T, T), :].rearrange("(t p) d -> p t d", p=P), base[:]).then_inc(stored, 16)
                sp.wait_ge(stored, FLOOR + 16 * B)
                sp.wait_ge(x_in[0], FLOOR + (32 * (B // 2 + 1)))

            NC = 19

            @block.gpsimd
            def _(pool):
                for j in range(2):
                    pool.memset(xT[j][:, :, 0:1], 0.0)
                pool.memset(kc[:, 0:1], 0.0)
                pool.memset(ks[:, 0:1], 0.0).then_inc(zeroed, 1)
                pool.memset(avg[:], 1.0 / D)
                pool.memset(avg16[:], 1.0 / D / 16).then_inc(zeroed, 1)
                pool.wait_ge(c_in, FLOOR + 16 * NC)
                with pool.Fori(0, B) as i:
                    ch = Chain(pool, pchain, i, 1)
                    pool.wait_ge(nat_in, FLOOR + (i * 32 + 32))
                    ch.link(pool.tensor_tensor(base[:], base[:], xnat[:], ALU.add))
                    pool.tensor_tensor(base[:], base[:], bo_r[:].rearrange("p (a n) -> p a n", a=1).broadcast_to([P, NT, D]),
                                       ALU.add).then_inc(base_ready, 1)
                    for mo in range(KD):
                        u = i * 2 + mo
                        pool.wait_ge(k_ready, FLOOR + (u + 1))
                        pool.wait_ge(m_used, FLOOR + u)
                        st.settle(pool)
                        pool.tensor_scalar(kc[:, 1:], hs[:], -2.0, 1.0, ALU.mult, ALU.add).then_inc(kc_ready, 1)
                        pool.wait_ge(kc_ready, FLOOR + (u + 1))
                        taken(pool, f"kv{mo}", i)
                        pool.tensor_tensor(mc[:], kvg[:], kc[:, 0:T], ALU.mult)
                        pool.tensor_tensor(ms[:], kvg[:], ks[:, 0:T], ALU.mult).then_inc(m_ready, 1)
                    ch.close()

            @block.tensor
            def _(pe):
                def product(name, turn, lhs, rhs, nk):
                    pe.wait_ge(freed[SLOT[name]], FLOOR + before(name, turn))
                    for c in range(C):
                        for k in range(nk):
                            ins = pe.matmul(ps[SLOT[name]][:, c, :], lhs(k), rhs(k, c), start=k == 0, stop=k == nk - 1)
                    ins.then_inc(made, 1)

                def front(n, par, loads):
                    pe.wait_ge(x_in[par], FLOOR + loads)
                    for mo in range(KD):
                        product(f"gh{mo}", n, lambda k: wg1_s[:, k, mo * P:(mo + 1) * P],
                                lambda k, c: xT[par][:, k % KD, 1 - k // KD + c * 512:1 - k // KD + (c + 1) * 512], 2 * KD)
                    product("bh", n, lambda k: wb1_s[:, k, :], lambda k, c: xT[par][:, k, 1 + c * 512:1 + (c + 1) * 512], KD)
                    taken(pe, "gh0", n)
                    taken(pe, "gh1", n)
                    product("gate", n, lambda k: wg2_s[:, k, :], lambda k, c: gh[:, k, c * 512:(c + 1) * 512], KD)
                    taken(pe, "bh", n)
                    product("z", n, lambda k: wbd_s[:], lambda k, c: bh[:, c * 512:(c + 1) * 512], 1)

                pe.wait_ge(c_in, FLOOR + 16 * NC)
                pe.wait_ge(zeroed, FLOOR + 2)
                pe.wait_ge(ready0, FLOOR + 1)
                front(None, 0, 32)
                with pe.Fori(0, B // 2) as i:
                    for j in range(2):
                        turn = i * 2 + j
                        for mo in range(KD):
                            for nm, w_ in (("k", wk_s), ("kv", wkv_s), ("pv", wpv_s)):
                                product(f"{nm}{mo}", turn, lambda k: w_[:, k, mo * P:(mo + 1) * P],
                                        lambda k, c: xT[j][:, k, 1 + c * 512:1 + (c + 1) * 512], KD)
                        front(turn, 1 - j, (i + (1 + j)) * 32)
                        pe.wait_ge(blended, FLOOR + (turn * 2 + 2))
                        product("mean", turn, lambda k: avg16[:], lambda k, c: bl[:, k, c * 512:(c + 1) * 512], KD)
                        pe.wait_ge(squared, FLOOR + (turn * 2 + 2))
                        product("var", turn, lambda k: avg[:], lambda k, c: sq[:, k, c * 512:(c + 1) * 512], KD)
                        pe.wait_ge(ln_ready, FLOOR + (turn * 2 + 2))
                        for hf, name in enumerate(("outA", "outB")):
                            pe.wait_ge(freed[SLOT[name]], FLOOR + before(name, turn))
                            pv = psf[SLOT[name]].rearrange("p (t n) -> p t n", n=D)
                            for t in range(4):
                                for k in range(KD):
                                    tt = hf * 4 + t
                                    ins = pe.matmul(pv[:, t, :], bl[:, k, tt * P:(tt + 1) * P], wo_s[:, k, :],
                                                    start=k == 0, stop=k == KD - 1)
                            ins.then_inc(made, 1)

            @block.scalar
            def _(act):
                def front(n, t, par):
                    for name, dst, bias in (("gh0", gh[:, 0, :], col[:, 6:7]), ("gh1", gh[:, 1, :], col[:, 7:8]),
                                            ("bh", bh[:], bb1_c[:, 0:1])):
                        act.wait_ge(made, FLOOR + made_at(name, t))
                        act.activation(dst, psf[SLOT[name]], ACT.Gelu, bias=bias).then_inc(freed[SLOT[name]], 1)
                    if t is not None:
                        act.wait_ge(blended, FLOOR + t * 2)
                    act.wait_ge(made, FLOOR + made_at("gate", t))
                    act.activation(gt[par][:], psf[SLOT["gate"]], ACT.Sigmoid, bias=bg2_c[:, 0:1]
                                   ).then_inc(freed[SLOT["gate"]], 1)
                    act.wait_ge(made, FLOOR + made_at("z", t))
                    act.activation(w0[par][:], psf[SLOT["z"]], ACT.Sigmoid, bias=bd[:, 0:1])
                    act.activation(w1[par][:], psf[SLOT["z"]], ACT.Sigmoid, bias=bd[:, 1:2], scale=-1.0
                                   ).then_inc(freed[SLOT["z"]], 1)
                    act.wait_ge(cs_ready, FLOOR + (n + 1))
                    act.activation(cs[:], cs[:], ACT.Sqrt).then_inc(dev_ready, 1)

                ch = Chain(act, achain)
                for k in range(KD):
                    act.wait_ge(reduced, FLOOR + (k + 1))
                    ch.link(act.activation(sinP[:, k, :], cosP[:, k, :], ACT.Sin))
                    ch.link(act.activation(cosP[:, k, :], cosP[:, k, :], ACT.Sin, scale=0.5))
                    ch.link(act.activation(cosP[:, k, :], cosP[:, k, :], ACT.Square))
                pre = ch.n
                act.wait_ge(ready0, FLOOR + 1)
                front(0, None, 0)
                with act.Fori(0, B // 2) as i:
                    for j in range(2):
                        turn = i * 2 + j
                        ch = Chain(act, achain, turn, 4)
                        ch.base = ch.base + pre
                        for mo in range(KD):
                            u = turn * 2 + mo
                            act.wait_ge(made, FLOOR + made_at(f"k{mo}", turn))
                            act.activation(th[:], psf[SLOT[f"k{mo}"]], ACT.Tanh, bias=col[:, 2 + mo:3 + mo]
                                           ).then_inc(freed[SLOT[f"k{mo}"]], 1)
                            taken(act, f"k{mo}", turn)
                            act.wait_ge(m_used, FLOOR + u)
                            act.wait_ge(kc_ready, FLOOR + u)
                            act.activation(ks[:, 1:], th[:], ACT.Sin, scale=PI_IN)
                            ch.link(act.activation(hs[:], th[:], ACT.Sin, scale=PI_IN / 2))
                            ch.link(act.activation(hs[:], hs[:], ACT.Square))
                            act.sem_inc(k_ready, 1)
                        ch.close()
                        front(turn + 1, turn, 1 - j)
                        for mo in range(KD):
                            act.wait_ge(cent, FLOOR + (turn * 2 + mo + 1))
                            act.activation(sq[:, mo, :], bl[:, mo, :], ACT.Square).then_inc(squared, 1)
                        act.wait_ge(made, FLOOR + made_at("var", turn))
                        act.wait_ge(ln_ready, FLOOR + turn * 2)
                        act.activation(vd[:], psf[SLOT["var"]], ACT.Sqrt, bias=eps[:, 0:1]).then_inc(freed[SLOT["var"]], 1)

            @block.vector
            def _(dve):
                STT = dve.scalar_tensor_tensor

                def weights(n, t, par, ch):
                    taken(dve, "gate", t)
                    ch.link(dve.tensor_tensor_scan(cs[:], ones[:], gt[par][:], 0.0, ALU.mult, ALU.add))
                    dve.tensor_scalar(cs[:], cs[:], 1.0, None, ALU.max).then_inc(cs_ready, 1)
                    dve.wait_ge(dev_ready, FLOOR + (n + 1))
                    ch.link(dve.reciprocal(cs[:], cs[:]))
                    taken(dve, "z", t)
                    ch.link(dve.tensor_tensor(w1[par][:], w1[par][:], cs[:], ALU.mult))

                dve.wait_ge(c_in, FLOOR + 16 * NC)
                ch = Chain(dve, chain)
                dve.memset(ones[:], 1.0)
                dve.memset(eps[:], LN_EPS)
                ch.link(dve.tensor_tensor(bd[:, 0:1], bb2_c[:, 0:1], bb2_c[:, 1:2], ALU.subtract))
                ch.link(dve.tensor_scalar(bd[:, 1:2], bd[:, 0:1], -1.0, None, ALU.mult))
                ch.link(dve.tensor_tensor(wb2_n[:], wb2_c[:, 0:1], wb2_c[:, 1:2], ALU.subtract))
                for k in range(KD):
                    ch.link(dve.tensor_copy(wg2_s[:, k, :], wg2_c[:, k:k + 1].broadcast_to([P, P])))
                ch.link(dve.tensor_copy(wbd_s[:], wb2_n[:, 0:1].broadcast_to([P, P])))
                for k in range(KD):
                    p = cosP[:, k, :]
                    ch.link(dve.tensor_scalar(a[:], p, 1.0 / (2 * PI), ROUND, ALU.mult, ALU.add))
                    ch.link(dve.tensor_scalar(a[:], a[:], -ROUND, None, ALU.add))
                    ch.link(STT(p, a[:], -TWO_PI_PARTS[0], p, ALU.mult, ALU.add))
                    ch.link(STT(p, a[:], -TWO_PI_PARTS[1], p, ALU.mult, ALU.add))
                    dve.tensor_scalar(p, p, PI_IN, -PI_IN, ALU.min, ALU.max).then_inc(reduced, 1)
                dve.wait_ge(achain, FLOOR + 3 * KD)
                dve.tensor_scalar(cosP[:], cosP[:], -2.0, 1.0, ALU.mult, ALU.add).then_inc(ready0, 1)
                dve.wait_ge(ready0, FLOOR + 1)
                weights(0, None, 0, ch)
                pre = ch.n
                with dve.Fori(0, B // 2) as i:
                    for j in range(2):
                        turn = i * 2 + j
                        ch = Chain(dve, chain, turn, 2 * 12 + 3 + 1 + 2)
                        ch.base = ch.base + pre
                        for mo in range(KD):
                            u = turn * 2 + mo
                            kv, pv = f"kv{mo}", f"pv{mo}"
                            dve.wait_ge(made, FLOOR + made_at(kv, turn))
                            dve.wait_ge(m_ready, FLOOR + u)
                            STT(kvg[:], psf[SLOT[kv]], col[:, 4 + mo:5 + mo], gt[j][:], ALU.add, ALU.mult
                                ).then_inc(freed[SLOT[kv]], 1)
                            dve.wait_ge(made, FLOOR + made_at(pv, turn))
                            ch.link(STT(a[:], psf[SLOT[pv]], col[:, mo:mo + 1], cosP[:, mo, :], ALU.add, ALU.mult))
                            STT(b_[:], psf[SLOT[pv]], col[:, mo:mo + 1], sinP[:, mo, :], ALU.add, ALU.mult
                                ).then_inc(freed[SLOT[pv]], 1)
                            taken(dve, pv, turn)
                            ch.link(dve.tensor_tensor_scan(sa[:], ones[:], a[:], 0.0, ALU.mult, ALU.add))
                            ch.link(dve.tensor_tensor_scan(sb_[:], ones[:], b_[:], 0.0, ALU.mult, ALU.add))
                            ch.link(dve.tensor_tensor(a[:], cosP[:, mo, :], sa[:], ALU.mult))
                            ch.link(dve.tensor_tensor(b_[:], sinP[:, mo, :], sb_[:], ALU.mult))
                            ch.link(dve.tensor_tensor(a[:], a[:], b_[:], ALU.add))
                            ch.link(dve.tensor_tensor(bl[:, mo, :], a[:], w0[j][:], ALU.mult))
                            dve.wait_ge(m_ready, FLOOR + (u + 1))
                            ch.link(dve.tensor_tensor_scan(sa[:], ones[:], mc[:], 0.0, ALU.mult, ALU.add))
                            ch.link(dve.tensor_tensor_scan(sb_[:], ones[:], ms[:], 0.0, ALU.mult, ALU.add))
                            ch.link(dve.tensor_tensor(a[:], kc[:, 1:], sa[:], ALU.mult))
                            dve.tensor_tensor(b_[:], ks[:, 1:], sb_[:], ALU.mult).then_inc(m_used, 1)
                            dve.wait_ge(m_used, FLOOR + (u + 1))
                            ch.link(dve.tensor_tensor(a[:], a[:], b_[:], ALU.add))
                            ch.link(dve.tensor_tensor(a[:], a[:], w1[j][:], ALU.mult))
                            dve.tensor_tensor(bl[:, mo, :], bl[:, mo, :], a[:], ALU.add).then_inc(blended, 1)
                            dve.wait_ge(blended, FLOOR + (u + 1))
                        weights(turn + 1, turn, 1 - j, ch)
                        dve.wait_ge(made, FLOOR + made_at("mean", turn))
                        for mo in range(KD):
                            STT(bl[:, mo, :], bl[:, mo, :], 1.0 / 16, psf[SLOT["mean"]], ALU.mult, ALU.subtract
                                ).then_inc(cent, 1)
                        dve.wait_ge(cent, FLOOR + (turn * 2 + 2))
                        dve.sem_inc(freed[SLOT["mean"]], 1)
                        taken(dve, "var", turn)
                        ch.link(dve.reciprocal(vd[:], vd[:]))
                        for mo in range(KD):
                            ch.link(dve.tensor_tensor(bl[:, mo, :], bl[:, mo, :], vd[:], ALU.mult))
                            dve.tensor_scalar(bl[:, mo, :], bl[:, mo, :], col[:, 8 + mo:9 + mo], col[:, 10 + mo:11 + mo],
                                              ALU.mult, ALU.add).then_inc(ln_ready, 1)
                        ch.close()
                        dve.wait_ge(base_ready, FLOOR + (turn + 1))
                        for hf, name in enumerate(("outA", "outB")):
                            dve.wait_ge(made, FLOOR + made_at(name, turn))
                            half = base[:, 4 * hf:4 * hf + 4, :].rearrange("p t n -> p (t n)")
                            dve.tensor_tensor(half, half, psf[SLOT[name]], ALU.add).then_inc(freed[SLOT[name]], 1)
def soft_slots(nc, xn_d, xnT_d, phi, W_d, b_d, ident_d, y_d, nm_d):
    CH = NP // P
    NE = P // SLOTS
    HB = B // 2
    AHEAD = 2
    with Stage(nc, "sl") as st:
        xn = st.sb("xn", [P, TILES, D])
        xT = st.sb("xT", [P, KD, B * T])
        ph = st.sb("phi", [P, KD, NP])
        w = st.sb("w", [P, NE, KD, D])
        bias = st.sb("bias", [P, D])
        ident = st.sb("ident", [P, P])
        lg = [st.sb(f"lg{j}", [P, B, P]) for j in range(4)]
        mx = st.sb("mx", [P, P])
        sm = [st.sb(f"sm{j}", [P, P]) for j in range(2)]
        slT = st.sb("slT", [P, KD, B, P])
        y = st.sb("y", [P, B, D])
        tmax = st.sb("tmax", [P, CH, B, NT])
        rest = st.sb("rest", [P, B * NT])
        part_b = st.sb("part_b", [P, 3, B * NT], BF16)
        part = st.sb("part", [P, 3, B * NT])
        part_r = [st.sb(f"part_r{h}", [P, P], BF16) for h in range(2)]
        lp = [st.ps(f"lp{j}", [P, B, P]) for j in range(2)]
        yp = [q[:].rearrange("p b n -> p (b n)").rearrange("p (b n) -> p b n", n=D) for q in lp[::-1]]
        acc = st.ps("acc", [P, KD, B, P])
        c_in = st.sem("c_in")
        n_in = st.sem("n_in")
        w_in = st.sem("w_in")
        bias_in = st.sem("bias_in")
        logits = st.sem("logits")
        shifted = st.sem("shifted")
        lp_read = st.sem("lp_read")
        chain = st.sem("chain")
        exped = st.sem("exped")
        inverted = st.sem("inverted")
        shared = st.sem("shared")
        slotted = st.sem("slotted")
        slT_ready = st.sem("slT_ready")
        y_made = st.sem("y_made")
        y_ready = st.sem("y_ready")
        stored = st.sem("stored")
        parts_ready = st.sem("parts_ready")
        parts_turned = st.sem("parts_turned")
        rows_ready = st.sem("rows_ready")
        parts_stored = st.sem("parts_stored")
        with st.block() as block:

            @block.sync
            def _(sp):
                sp.dma_start(ph[:], phi.rearrange("(k p) n -> p k n", p=P)).then_inc(c_in, 16)
                for k in range(KD):
                    sp.dma_start(xT[:, k, :], xnT_d[k]).then_inc(c_in, 16)
                sp.dma_start(ident[:], ident_d).then_inc(n_in, 16)
                for b in range(B):
                    sp.dma_start(xn[:, b * NT:(b + 1) * NT, :],
                                 xn_d[b * T:(b + 1) * T, :].rearrange("(t p) d -> p t d", p=P)).then_inc(n_in, 16)

                def weights(c):
                    for e in range(NE):
                        sp.dma_start(w[:, e], W_d[c * NE + e, :, :].rearrange("(k p) n -> p k n", p=P)).then_inc(w_in, 16)

                def biases(c):
                    for e in range(NE):
                        row = b_d[c * NE + e:c * NE + e + 1, :] if isinstance(c, int) else b_d[bass.ds(c * NE + e, 1), :]
                        sp.dma_start(bias[e * SLOTS:(e + 1) * SLOTS, :], row.to_broadcast([SLOTS, D])
                                     ).then_inc(bias_in, 16)

                weights(0)
                biases(0)
                with sp.Fori(0, CH) as c:
                    sp.wait_ge(y_made, FLOOR + (c * 2 + 2))
                    weights((c + 1) % CH)
                    sp.wait_ge(y_ready, FLOOR + (c * 2 + 2))
                    sp.dma_start(y_d[:, bass.ds(c * P, P), :].rearrange("b p d -> p b d"), y[:]).then_inc(stored, 16)
                    biases((c + 1) % CH)
                sp.wait_ge(stored, FLOOR + 16 * CH)
                sp.wait_ge(w_in, FLOOR + 64 * (CH + 1))
                sp.wait_ge(bias_in, FLOOR + 64 * (CH + 1))
                for h in range(2):
                    sp.wait_ge(rows_ready, FLOOR + h + 1)
                    n = 2 - h
                    sp.dma_start(nm_d[2 * h:2 * h + n, :].rearrange("q (t p) -> (q t) p", p=P),
                                 part_r[h][0:n * TILES, :]).then_inc(parts_stored, 16)
                sp.wait_ge(parts_stored, FLOOR + 32)

            @block.gpsimd
            def _(pool):
                with pool.Fori(0, CH) as c:
                    for m in range(NT):
                        j = m % 2
                        pool.wait_ge(inverted, FLOOR + (c * NT + (m + 1)))
                        for half in range(2):
                            part_ = lg[m % 4][:, half * HB:(half + 1) * HB, :]
                            pool.tensor_tensor(part_, part_,
                                               sm[j][:].rearrange("p (a n) -> p a n", a=1).broadcast_to([P, HB, P]),
                                               ALU.mult).then_inc(shared, 1)

            @block.tensor
            def _(pe):
                def token_logits(c, m):
                    j = m % 2
                    for b in range(B):
                        for k in range(KD):
                            ins = pe.matmul(lp[j][:, b, :], xT[:, k, b * T + m * P:b * T + (m + 1) * P],
                                            ph[:, k, bass.ds(c * P, P)], start=k == 0, stop=k == KD - 1)
                    ins.then_inc(logits, 1)

                def through_experts(c, read):
                    pe.wait_ge(w_in, FLOOR + (c * 64 + 64))
                    for h in range(2):
                        if read is not None:
                            pe.wait_ge(lp_read, FLOOR + (read + h))
                        for b in range(HB):
                            for k in range(KD):
                                for e in range(NE):
                                    ins = pe.matmul(yp[h][e * SLOTS:(e + 1) * SLOTS, b, :],
                                                    slT[:, k, h * HB + b, e * SLOTS:(e + 1) * SLOTS],
                                                    w[:, e, k, :], start=k == 0, stop=k == KD - 1)
                        ins.then_inc(y_made, 1)

                def turn(c, first):
                    for m in range(NT):
                        u = c * NT + m
                        pe.wait_ge(lp_read, FLOOR + (u + 1))
                        if m in (1, 2) and not first:
                            pe.wait_ge(y_ready, FLOOR + (c * 2 + (m - 2)))
                        token_logits(c if m < NT - AHEAD else (c + 1) % CH, (m + AHEAD) % NT)
                        for half in range(2):
                            pe.wait_ge(shared, FLOOR + (u * 2 + half + 1))
                            if m == 0 and half == 0 and not first:
                                pe.wait_ge(slT_ready, FLOOR + c * 4)
                            for k in range(KD):
                                for b in range(half * HB, (half + 1) * HB):
                                    ins = pe.matmul(acc[:, k, b, :], xn[:, b * NT + m, k * P:(k + 1) * P],
                                                    lg[m % 4][:, b, :], start=m == 0 and b % 4 == 0,
                                                    stop=m == NT - 1, skip_group_check=True)
                        ins.then_inc(slotted, 1)
                        if m == 0 and not first:
                            through_experts(c - 1, c * NT + 2)

                pe.wait_ge(c_in, FLOOR + (16 * (1 + KD)))
                for m in range(AHEAD):
                    token_logits(0, m)
                pe.wait_ge(n_in, FLOOR + (16 * (1 + B)))
                turn(0, True)
                with pe.Fori(1, CH) as c:
                    turn(c, False)
                pe.wait_ge(slT_ready, FLOOR + CH * 4)
                through_experts(CH - 1, None)
                pe.wait_ge(parts_ready, FLOOR + 1)
                parts = part[:].rearrange("p q t -> p (q t)")
                for h in range(2):
                    n = (2 - h) * TILES
                    pe.transpose(acc[0:n, 0, 4 * h, :], parts[:, h * P:h * P + n], ident[:]).then_inc(parts_turned, 1)

            @block.scalar
            def _(act):
                def exponential(c, m):
                    act.wait_ge(shifted, FLOOR + (c * NT + (m + 1)))
                    act.activation(lg[m % 4][:], lg[m % 4][:], ACT.Exp).then_inc(exped, 1)

                def slots_out(c):
                    act.wait_ge(slotted, FLOOR + (c * NT + NT))
                    act.wait_ge(y_made, FLOOR + c * 2)
                    for k in range(KD):
                        for h in range(2):
                            act.activation(slT[:, k, 4 * h:4 * h + 4, :], acc[:, k, 4 * h:4 * h + 4, :], ACT.Copy
                                           ).then_inc(slT_ready, 1)

                for m in range(AHEAD):
                    exponential(0, m)
                with act.Fori(0, CH - 1) as c:
                    for m in range(AHEAD, NT + AHEAD):
                        exponential(c, m)
                    slots_out(c)
                for m in range(AHEAD, NT):
                    exponential(CH - 1, m)
                slots_out(CH - 1)

            @block.vector
            def _(dve):
                def add_bias(c, h):
                    dve.wait_ge(y_made, FLOOR + (c * 2 + h + 1))
                    dve.wait_ge(stored, FLOOR + c * 16)
                    dve.wait_ge(bias_in, FLOOR + (c * 64 + 64))
                    dve.tensor_tensor(y[:, h * HB:(h + 1) * HB, :], yp[h],
                                      bias[:].rearrange("p (a n) -> p a n", a=1).broadcast_to([P, HB, D]),
                                      ALU.add).then_inc(y_ready, 1)

                def turn(c, first):
                    for m in range(NT):
                        j, l = m % 2, m % 4
                        u = c * NT + m
                        ch = Chain(dve, chain, u, 2)
                        dve.wait_ge(logits, FLOOR + (u + 1))
                        ch.link(dve.tensor_reduce(mx[:], lp[j][:].rearrange("p b n -> p n b"), AX.X, ALU.max))
                        if m >= 4 or not first:
                            dve.wait_ge(slotted, FLOOR + (u - 3))
                        dve.tensor_tensor(lg[l][:], lp[j][:], mx[:].rearrange("p (a n) -> p a n", a=1).broadcast_to([P, B, P]),
                                          ALU.subtract).then_inc(shifted, 1)
                        dve.tensor_reduce(tmax[:, bass.ds(c, 1), :, m].rearrange("p c b -> p (c b)"), lp[j][:],
                                          AX.X, ALU.max).then_inc(lp_read, 1)
                        if m == 2 and not first:
                            for h in range(2):
                                add_bias(c - 1, h)
                        dve.wait_ge(exped, FLOOR + (u + 1))
                        if m >= 2 or not first:
                            dve.wait_ge(shared, FLOOR + (u - 1) * 2)
                        ch.link(dve.tensor_reduce(sm[j][:], lg[l][:].rearrange("p b n -> p n b"), AX.X, ALU.add))
                        ch.close()
                        dve.reciprocal(sm[j][:], sm[j][:]).then_inc(inverted, 1)

                turn(0, True)
                with dve.Fori(1, CH) as c:
                    turn(c, False)
                ch = Chain(dve, chain)
                ch.base = 2 * CH * NT
                ch.link(dve.tensor_reduce(rest[:], tmax[:].rearrange("p c b m -> p (b m) c"), AX.X, ALU.max))
                ch.link(dve.tensor_scalar(rest[:], rest[:], -1.0, None, ALU.mult))
                for q in range(3):
                    ch.link(dve.tensor_copy(part_b[:, q, :], rest[:]))
                    ch.link(dve.tensor_tensor(rest[:], rest[:], part_b[:, q, :], ALU.subtract))
                dve.tensor_copy(part[:], part_b[:]).then_inc(parts_ready, 1)
                for h in range(2):
                    add_bias(CH - 1, h)
                for h in range(2):
                    n = (2 - h) * TILES
                    dve.wait_ge(parts_turned, FLOOR + h + 1)
                    dve.tensor_copy(part_r[h][0:n, :], acc[0:n, 0, 4 * h, :]).then_inc(rows_ready, 1)


def soft_combine(nc, xnT_d, phi, y_d, nm_d, x_d, out_d):
    SK = NP // P
    GT = 4
    GN = GT * P
    LAG = 3
    with Stage(nc, "cb") as st:
        ph = st.sb("phi", [P, KD, NP])
        y = st.sb("y", [P, 2, SK, D + 1])
        nm = st.sb("nm", [3, B * T], BF16)
        ones = st.sb("ones", [3, P], BF16)
        xT = [st.sb(f"xT{h}", [P, KD, GN]) for h in range(2)]
        x = [st.sb(f"x{h}", [P, GT, D]) for h in range(2)]
        ex = [st.sb(f"ex{j}", [P, GN]) for j in range(4)]
        rs = [st.sb(f"rs{h}", [P, GT]) for h in range(2)]
        lp = [st.ps(f"lp{j}", [P, GN]) for j in range(4)]
        op = st.ps("op", [P, GT, 512])
        c_in = st.sem("c_in")
        y_in = st.sem("y_in")
        ones_ready = st.sem("ones_ready")
        x_in = [st.sem(f"x_in{h}") for h in range(2)]
        r_in = [st.sem(f"r_in{h}") for h in range(2)]
        logits = st.sem("logits")
        exped = st.sem("exped")
        used = st.sem("used")
        inverted = st.sem("inverted")
        read = st.sem("read")
        stored = [st.sem(f"stored{h}") for h in range(2)]
        with st.block() as block:

            @block.sync
            def _(sp):
                tokens = lambda n0: xnT_d[:, :, bass.ds(n0, GN)].rearrange("k p t -> p k t")
                slots = lambda b: y_d[b, :, :].rearrange("(k p) d -> p k d", p=P)
                sp.dma_start(ph[:], phi.rearrange("(k p) n -> p k n", p=P)).then_inc(c_in, 16)
                sp.dma_start(nm[:], nm_d).then_inc(c_in, 16)
                sp.dma_start(xT[0][:], tokens(0)).then_inc(x_in[0], 16)
                sp.dma_start(y[:, 0, :, 0:D], slots(0)).then_inc(y_in, 16)
                with sp.Fori(0, B) as b:
                    for h in range(2):
                        g = b * 2 + h
                        sp.wait_ge(used, FLOOR + g * SK)
                        if h == 0:
                            sp.dma_start(xT[1][:], tokens(b * T + GN)).then_inc(x_in[1], 16)
                            sp.wait_ge(y_in, FLOOR + (b * 16 + 16))
                            sp.dma_start(y[:, bass.ds((b + 1) % 2, 1), :, 0:D].rearrange("p a k d -> p (a k) d"),
                                         slots((b + 1) % B)).then_inc(y_in, 16)
                        else:
                            sp.dma_start(xT[0][:], tokens((b + 1) % B * T)).then_inc(x_in[0], 16)
                        sp.wait_ge(stored[h], FLOOR + b * 16)
                        sp.dma_start(x[h][:], x_d[bass.ds(g * GN, GN), :].rearrange("(t p) d -> p t d", p=P)
                                     ).then_inc(r_in[h], 16)
                        sp.wait_ge(read, FLOOR + (g * GT + GT))
                        sp.dma_start(out_d[bass.ds(g * GN, GN), :].rearrange("(t p) d -> p t d", p=P), x[h][:]
                                     ).then_inc(stored[h], 16)
                for h in range(2):
                    sp.wait_ge(stored[h], FLOOR + 16 * B)
                sp.wait_ge(y_in, FLOOR + 16 * (B + 1))
                sp.wait_ge(x_in[0], FLOOR + 16 * (B + 1))

            @block.tensor
            def _(pe):
                def slot_logits(g, n0, h, s, loads):
                    j = s % 4
                    if s == 0:
                        pe.wait_ge(x_in[h], FLOOR + loads * 16)
                    for k in range(KD):
                        pe.matmul(lp[j][:], ph[:, k, s * P:(s + 1) * P], xT[h][:, k, :], start=k == 0, stop=False)
                    pe.matmul(lp[j][:], ones[:], nm[:, bass.ds(n0, GN)], start=False, stop=True).then_inc(logits, 1)

                pe.wait_ge(c_in, FLOOR + 32)
                pe.wait_ge(ones_ready, FLOOR + 2)
                for s in range(LAG):
                    slot_logits(0, 0, 0, s, 1)
                with pe.Fori(0, B) as b:
                    for h in range(2):
                        g = b * 2 + h
                        for s in range(SK):
                            pe.wait_ge(exped, FLOOR + (g * SK + (s + 1)))
                            ahead = s + LAG
                            if ahead < SK:
                                slot_logits(g, b * T + h * GN, h, ahead, 0)
                            else:
                                slot_logits(g + 1, (b * T + (h + 1) * GN) if h == 0 else (b + 1) % B * T,
                                            1 - h, ahead - SK, b + 1 + h)
                            if s == 0:
                                pe.wait_ge(y_in, FLOOR + (b * 16 + 16))
                                pe.wait_ge(read, FLOOR + g * GT)
                            for q in range(GT):
                                ins = pe.matmul(op[:, q, 0:D + 1], ex[s % 4][:, q * P:(q + 1) * P],
                                                y[:, bass.ds(b % 2, 1), s, :].rearrange("p a d -> p (a d)"),
                                                start=s == 0, stop=s == SK - 1)
                            ins.then_inc(used, 1)

            @block.scalar
            def _(act):
                with act.Fori(0, B) as b:
                    for h in range(2):
                        g = b * 2 + h
                        for s in range(SK):
                            act.wait_ge(used, FLOOR + (g * SK + max(s - 3, 0)))
                            act.wait_ge(logits, FLOOR + (g * SK + s + 1))
                            act.activation(ex[s % 4][:], lp[s % 4][:], ACT.Exp).then_inc(exped, 1)

            @block.vector
            def _(dve):
                dve.memset(ones[:], 1.0).then_inc(ones_ready, 1)
                dve.memset(y[:, :, :, D:D + 1], 1.0).then_inc(ones_ready, 1)
                with dve.Fori(0, B) as b:
                    for h in range(2):
                        g = b * 2 + h
                        dve.wait_ge(used, FLOOR + (g * SK + SK))
                        dve.reciprocal(rs[h][:], op[:, :, D]).then_inc(inverted, 1)
                        dve.wait_ge(inverted, FLOOR + (g + 1))
                        dve.wait_ge(r_in[h], FLOOR + (b * 16 + 16))
                        for q in range(GT):
                            dve.scalar_tensor_tensor(x[h][:, q, :], op[:, q, 0:D], rs[h][:, q:q + 1], x[h][:, q, :],
                                                     ALU.mult, ALU.add).then_inc(read, 1)
def build_program(nc, a, out):
    def scratch(name, shape):
        return nc.dram_tensor(name, shape, F32, kind="Internal").ap()

    x0, ident = a["x"], a["ident"]
    xn, xnT = scratch("xn", (B * T, D)), scratch("xnT", (KD, P, B * T))
    qkv, ctx = scratch("qkv", (B * T, 3 * D)), scratch("ctx", (B * T, D))
    x1, x2, x3 = (scratch(n, (B * T, D)) for n in ("x1", "x2", "x3"))
    pos, aff = scratch("pos", (P, NT, B * E)), scratch("aff", (P, NT, B, E))
    y = scratch("y", (B, NP, D))
    nm = nc.dram_tensor("nm", (3, B * T), BF16, kind="Internal").ap()

    normalise(nc, "n0", x0, xn, xnT, ident)
    qkv_rope(nc, xnT, *(a["L0_attn_" + n] for n in ("Wq", "Wk", "Wv", "bq", "bk", "bv")), a["cos"], a["sin"], qkv)
    attend(nc, qkv, ident, a["kaug"], ctx)
    project(nc, "pj", ctx, a["L0_attn_Wo"], a["L0_attn_bo"], x0, ident, x1)
    normalise(nc, "n1", x1, xn, xnT, ident)
    route(nc, xnT, a["L0_ffn_gate_w"], ident, pos, aff)
    experts(nc, xn, pos, aff, a["L0_ffn_Wg"], a["L0_ffn_Wu"], a["L0_ffn_Wd"], a["iota"], a["tok"], x1, x2)
    normalise(nc, "n2", x2, xn, xnT, ident)
    phases(nc, xn, xnT, x2, a["ppT"], *(a["L1_attn_" + n] for n in (
        "Wpv", "bpv", "Wk", "bk", "Wkv", "bkv", "Wg1", "bg1", "Wg2", "bg2", "Wb1", "bb1", "Wb2", "bb2",
        "ln_g", "ln_b", "Wo", "bo")), x3)
    normalise(nc, "n3", x3, xn, xnT, ident)
    soft_slots(nc, xn, xnT, a["phi"], a["L1_ffn_W"], a["L1_ffn_b"], ident, y, nm)
    soft_combine(nc, xnT, a["phi"], y, nm, x3, out)


def kernel(**inputs):
    import concourse.bacc as _bacc
    from concourse.bass_utils import run_bass_kernel_spmd as _run

    given = {k: np.asarray(v) for k, v in inputs.items()}
    arrays = {k: v for k, v in given.items() if k not in ("L0_attn_x", "L1_attn_pos_phases", "L1_ffn_phi")}
    arrays["x"] = given["L0_attn_x"].reshape(B * T, D)
    arrays["ppT"] = given["L1_attn_pos_phases"][:T].T
    arrays["phi"] = given["L1_ffn_phi"].reshape(D, NP)
    arrays.update(consts())
    nc = _bacc.Bacc("TRN2", target_bir_lowering=False, num_devices=1)
    sent, aps = {}, {}
    for name, v in arrays.items():
        sent[f"in_{name}"] = np.ascontiguousarray(v)
        aps[name] = nc.dram_tensor(f"in_{name}", v.shape, mybir.dt.from_np(v.dtype), kind="ExternalInput").ap()
    out = nc.dram_tensor("out", (B * T, D), F32, kind="ExternalOutput").ap()
    build_program(nc, aps, out)
    r = _run(nc, [sent], core_ids=[0])
    return r.results[0]["out"].reshape(B, T, D)
```

```python
from contextlib import ExitStack

import numpy as np
import concourse.bass as bass
from concourse import mybir

F32 = mybir.dt.float32
BF16 = mybir.dt.bfloat16
ALU = mybir.AluOpType
ACT = mybir.ActivationFunctionType
AX = mybir.AxisListType

P = 128
B, T, D = 8, 1024, 256
NT = T // P
TILES = B * NT
KD = D // P
H, HD = 16, 16
G = 4
HG = H // G
GW = HG * HD
E, I, CAP = 8, 512, 256
N_EXP, SLOTS = 64, 32
NP = N_EXP * SLOTS
LN_EPS = 1e-5
FLOOR = 1


class Chain:

    def __init__(self, eng, sem, turn=0, per=0):
        self.eng, self.sem, self.base, self.per, self.n = eng, sem, turn * per, per, 0

    def link(self, ins):
        ins.then_inc(self.sem, 1)
        self.n += 1
        self.eng.wait_ge(self.sem, FLOOR + (self.base + self.n))

    def close(self):
        assert self.n == self.per, (self.n, self.per)


class Stage:

    def __init__(self, nc, tag):
        self.nc, self.tag, self.ctx, self.sems = nc, tag, ExitStack(), []

    def __enter__(self):
        self.ctx.__enter__()
        self.mark = self.sem("mark")
        return self

    def settle(self, eng):
        eng.sem_inc(self.mark, 1)

    def __exit__(self, *a):
        if a[0] is None:
            self.nc.clear_and_free_semaphores(self.sems)
        return self.ctx.__exit__(*a)

    def block(self):
        for s in self.sems:
            self.nc.gpsimd.sem_inc(s, FLOOR)
        self.nc.all_engine_barrier()
        return self.nc.Block()

    def sb(self, name, shape, dt=F32):
        return self.ctx.enter_context(self.nc.sbuf_tensor(f"{self.tag}_{name}", shape, dt))

    def ps(self, name, shape, dt=F32):
        return self.ctx.enter_context(self.nc.psum_tensor(f"{self.tag}_{name}", shape, dt))

    def sem(self, name):
        self.sems.append(self.nc.alloc_semaphore(f"{self.tag}_{name}"))
        return self.sems[-1]


def col_bcast(vec, p=P):
    return vec.rearrange("(a n) -> a n", a=1).to_broadcast([p, vec.shape[0]])


def normalise(nc, tag, x_d, xn_d, xnT_d, ident_d):
    U = 4
    with Stage(nc, tag) as st:
        ident = st.sb("ident", [P, P])
        eps = st.sb("eps", [P, 1])
        x = [st.sb(f"x{j}", [P, NT, D]) for j in range(U)]
        stats = st.sb("stats", [P, NT, 6])
        mv = [st.sb(f"mv{j}", [P, NT, 2]) for j in range(2)]
        rstd = [st.sb(f"rstd{j}", [P, NT]) for j in range(2)]
        nmr = [st.sb(f"nmr{j}", [P, NT]) for j in range(2)]
        xn = [st.sb(f"xn{j}", [P, NT, D]) for j in range(2)]
        xnT = [st.sb(f"xnT{j}", [P, KD, T]) for j in range(2)]
        tr = [st.ps(f"tr{j}", [P, KD, 512]) for j in range(2)]
        x_in = [st.sem(f"x_in{j}") for j in range(U)]
        c_in = st.sem("c_in")
        chain = st.sem("chain")
        stats_ready = st.sem("stats_ready")
        eps_ready = st.sem("eps_ready")
        var_ready = st.sem("var_ready")
        dev_ready = st.sem("dev_ready")
        xn_ready = st.sem("xn_ready")
        turned = st.sem("turned")
        xnT_ready = st.sem("xnT_ready")
        xn_stored = [st.sem(f"xn_stored{j}") for j in range(2)]
        xnT_stored = [st.sem(f"xnT_stored{j}") for j in range(2)]
        with st.block() as block:

            @block.sync
            def _(sp):
                sp.dma_start(x[0][:], x_d[0:T, :].rearrange("(t p) d -> p t d", p=P)).then_inc(x_in[0], 16)
                sp.dma_start(ident[:], ident_d).then_inc(c_in, 16)
                for j in range(1, U):
                    sp.dma_start(x[j][:], x_d[j * T:(j + 1) * T, :].rearrange("(t p) d -> p t d", p=P)
                                 ).then_inc(x_in[j], 16)
                for b in range(U, B + 1):
                    j = b % U
                    sp.wait_ge(xn_ready, FLOOR + (b - U + 1))
                    rows = slice(b % B * T, (b % B + 1) * T)
                    sp.dma_start(x[j][:], x_d[rows, :].rearrange("(t p) d -> p t d", p=P)).then_inc(x_in[j], 16)

            @block.vector
            def _(dve):
                def statistics(n, u, loads):
                    dve.wait_ge(x_in[u], FLOOR + loads * 16)
                    dve.wait_ge(var_ready, FLOOR + n)
                    for t in range(NT):
                        ins = dve.bn_stats(stats[:, t, :], x[u][:, t, :])
                    ins.then_inc(stats_ready, 1)
                    dve.wait_ge(stats_ready, FLOOR + (n + 1))
                    st.settle(dve)
                    for t in range(NT):
                        ins = dve.bn_aggr(mv[u % 2][:, t, :], stats[:, t, :])
                    ins.then_inc(var_ready, 1)

                dve.memset(eps[:], LN_EPS).then_inc(eps_ready, 1)
                statistics(0, 0, 1)
                with dve.Fori(0, B // U) as i:
                    for u in range(U):
                        turn, j = i * U + u, u % 2
                        statistics(turn + 1, (u + 1) % U, i + (1 + (u + 1) // U))
                        ch = Chain(dve, chain, turn, 2)
                        dve.wait_ge(dev_ready, FLOOR + (turn + 1))
                        ch.link(dve.reciprocal(rstd[j][:], rstd[j][:]))
                        ch.link(dve.scalar_tensor_tensor(nmr[j][:], mv[j][:, :, 0], -1.0, rstd[j][:],
                                                         ALU.mult, ALU.mult))
                        ch.close()
                        dve.wait_ge(turned, FLOOR + (i * 2 * U + 2 * max(u - 1, 0)))
                        if xn_d is not None:
                            dve.wait_ge(xn_stored[j], FLOOR + (i * (U // 2) + u // 2) * 16)
                        for t in range(NT):
                            ins = dve.tensor_scalar(xn[j][:, t, :], x[u][:, t, :], rstd[j][:, t:t + 1],
                                                    nmr[j][:, t:t + 1], ALU.mult, ALU.add)
                        ins.then_inc(xn_ready, 1)

            @block.tensor
            def _(pe):
                pe.wait_ge(c_in, FLOOR + 16)
                with pe.Fori(0, B // 2) as i:
                    for j in range(2):
                        turn = i * 2 + j
                        pe.wait_ge(xn_ready, FLOOR + (turn + 1))
                        for half in range(2):
                            pe.wait_ge(xnT_ready, FLOOR + (turn * 4 + 2 * half))
                            for k in range(KD):
                                for t in range(NT // 2):
                                    ins = pe.transpose(tr[half][:, k, t * P:(t + 1) * P],
                                                       xn[j][:, half * NT // 2 + t, k * P:(k + 1) * P], ident[:])
                            ins.then_inc(turned, 1)

            @block.scalar
            def _(act):
                def deviation(n, j):
                    act.wait_ge(var_ready, FLOOR + (n + 1))
                    act.activation(rstd[j][:], mv[j][:, :, 1], ACT.Sqrt, bias=eps[:, 0:1]).then_inc(dev_ready, 1)

                act.wait_ge(eps_ready, FLOOR + 1)
                deviation(0, 0)
                with act.Fori(0, B // 2) as i:
                    for j in range(2):
                        turn = i * 2 + j
                        act.wait_ge(xn_ready, FLOOR + turn)
                        deviation(turn + 1, 1 - j)
                        act.wait_ge(xn_ready, FLOOR + (turn + 1))
                        if xn_d is not None:
                            act.dma_start(xn_d[bass.ts(turn, T), :].rearrange("(t p) d -> p t d", p=P),
                                          xn[j][:]).then_inc(xn_stored[j], 16)
                        act.wait_ge(xnT_stored[j], FLOOR + i * 32)
                        for half in range(2):
                            act.wait_ge(turned, FLOOR + (turn * 2 + half + 1))
                            for k in range(KD):
                                act.activation(xnT[j][:, k, half * 512:(half + 1) * 512], tr[half][:, k, :],
                                               ACT.Copy).then_inc(xnT_ready, 1)
                        act.wait_ge(xnT_ready, FLOOR + (turn * 4 + 4))
                        st.settle(act)
                        for k in range(KD):
                            act.dma_start(xnT_d[k, :, bass.ts(turn, T)], xnT[j][:, k, :]).then_inc(xnT_stored[j], 16)
                for j in range(2):
                    if xn_d is not None:
                        act.wait_ge(xn_stored[j], FLOOR + 16 * B // 2)
                    act.wait_ge(xnT_stored[j], FLOOR + 32 * B // 2)


def qkv_rope(nc, xnT_d, wq, wk, wv, bq, bk, bv, cos_d, sin_d, qkv_d):
    W = 3 * D
    NB = 4
    HT = NT // 2
    with Stage(nc, "qkv") as st:
        w = st.sb("w", [P, KD, G, 3, GW])
        bias = st.sb("bias", [P, G, 3, GW])
        cos = st.sb("cos", [P, NT, 8])
        sin = st.sb("sin", [P, NT, 8])
        xT = [st.sb(f"xT{h}", [P, KD, HT * P]) for h in range(2)]
        y = [st.sb(f"y{j}", [P, G, 3 * GW]) for j in range(NB)]
        by_cos = [st.sb(f"by_cos{j}", [P, G, 16, 8]) for j in range(2)]
        by_sin = [st.sb(f"by_sin{j}", [P, G, 16, 8]) for j in range(2)]
        mm = [st.ps(f"mm{j}", [P, 2, 512]) for j in range(NB)]
        c_in = st.sem("c_in")
        x_in = [st.sem(f"x_in{h}") for h in range(2)]
        made = st.sem("made")
        biased = st.sem("biased")
        cos_ready = st.sem("cos_ready")
        sin_ready = st.sem("sin_ready")
        first_ready = st.sem("first_ready")
        second_ready = st.sem("second_ready")
        stored = [st.sem(f"stored{j}") for j in range(NB)]
        heads = lambda j: y[j][:, :, 0:2 * GW].rearrange("p g (h e) -> p g h e", e=8)
        table = lambda tab, u: tab[:, u:u + 1, :].rearrange("p (a b) e -> p a b e", a=1).broadcast_to([P, G, 16, 8])
        with st.block() as block:

            @block.sync
            def _(sp):
                tokens = lambda t: xnT_d[:, :, bass.ds(t * P, HT * P)].rearrange("k p t -> p k t")
                sp.dma_start(xT[0][:], tokens(0)).then_inc(x_in[0], 16)
                for c, (wm, bm) in enumerate(((wq, bq), (wk, bk), (wv, bv))):
                    for k in range(KD):
                        sp.dma_start(w[:, k, :, c, :], wm[k * P:(k + 1) * P, :].rearrange("p (g n) -> p g n", g=G)
                                     ).then_inc(c_in, 16)
                    sp.dma_start(bias[:, :, c, :], col_bcast(bm).rearrange("p (g n) -> p g n", g=G)).then_inc(c_in, 16)
                sp.dma_start(cos[:], cos_d).then_inc(c_in, 16)
                sp.dma_start(sin[:], sin_d).then_inc(c_in, 16)
                with sp.Fori(0, B) as b:
                    sp.wait_ge(made, FLOOR + b * NT)
                    sp.dma_start(xT[1][:], tokens(b * NT + HT)).then_inc(x_in[1], 16)
                    sp.wait_ge(made, FLOOR + (b * NT + HT))
                    sp.dma_start(xT[0][:], tokens((b + 1) % B * NT)).then_inc(x_in[0], 16)
                sp.wait_ge(x_in[0], FLOOR + 16 * (B + 1))

            @block.tensor
            def _(pe):
                def product(t, u, half, loads):
                    j = u % NB
                    pe.wait_ge(x_in[half], FLOOR + loads * 16)
                    tile = slice(u % HT * P, (u % HT + 1) * P)
                    for n0, n1 in ((0, 512), (512, W)):
                        for k in range(KD):
                            ins = pe.matmul(mm[j][:, n0 // 512, 0:n1 - n0], xT[half][:, k, tile],
                                            w[:, k].rearrange("p g c n -> p (g c n)")[:, n0:n1],
                                            start=k == 0, stop=k == KD - 1)
                    ins.then_inc(made, 1)

                pe.wait_ge(c_in, FLOOR + 16 * 11)
                product(0, 0, 0, 1)
                with pe.Fori(0, B) as b:
                    for u in range(NT):
                        pe.wait_ge(biased, FLOOR + b * NT + max(u + 2 - NB, 0))
                        n = u + 1
                        product(b * NT + n, n, n % NT // HT, b + (1 + n // NT))

            @block.vector
            def _(dve):
                def first(t, u):
                    j = u % NB
                    dve.wait_ge(made, FLOOR + (t + 1))
                    dve.tensor_tensor(y[j][:].rearrange("p g n -> p (g n)"),
                                      mm[j][:].rearrange("p a n -> p (a n)")[:, 0:W],
                                      bias[:].rearrange("p g c n -> p (g c n)"), ALU.add).then_inc(biased, 1)
                    dve.wait_ge(biased, FLOOR + (t + 1))
                    dve.tensor_tensor(by_sin[u % 2][:], heads(j), table(sin, u % NT), ALU.mult).then_inc(sin_ready, 1)

                dve.wait_ge(c_in, FLOOR + 16 * 11)
                first(0, 0)
                with dve.Fori(0, B) as b:
                    for u in range(NT):
                        t = b * NT + u
                        n = u + 1
                        if n >= NB:
                            dve.wait_ge(stored[n % NB], FLOOR + (b * 2 + n // NB) * 16)
                        else:
                            dve.wait_ge(stored[n % NB], FLOOR + b * 32)
                        dve.wait_ge(first_ready, FLOOR + t)
                        first(t + 1, n)
                        dve.wait_ge(cos_ready, FLOOR + (t + 1))
                        dve.wait_ge(sin_ready, FLOOR + (t + 1))
                        dve.tensor_tensor(heads(u % NB)[:, :, 1::2, :], by_sin[u % 2][:, :, 0::2, :],
                                          by_cos[u % 2][:, :, 1::2, :], ALU.add).then_inc(second_ready, 1)

            @block.gpsimd
            def _(pool):
                pool.wait_ge(c_in, FLOOR + 16 * 11)
                with pool.Fori(0, B) as b:
                    for u in range(NT):
                        t = b * NT + u
                        pool.wait_ge(second_ready, FLOOR + b * NT + max(u - 1, 0))
                        pool.wait_ge(biased, FLOOR + (t + 1))
                        pool.tensor_tensor(by_cos[u % 2][:], heads(u % NB), table(cos, u), ALU.mult
                                           ).then_inc(cos_ready, 1)
                        pool.wait_ge(cos_ready, FLOOR + (t + 1))
                        pool.wait_ge(sin_ready, FLOOR + (t + 1))
                        pool.tensor_tensor(heads(u % NB)[:, :, 0::2, :], by_cos[u % 2][:, :, 0::2, :],
                                           by_sin[u % 2][:, :, 1::2, :], ALU.subtract).then_inc(first_ready, 1)

            @block.scalar
            def _(act):
                with act.Fori(0, B) as b:
                    for u in range(NT):
                        t = b * NT + u
                        act.wait_ge(first_ready, FLOOR + (t + 1))
                        act.wait_ge(second_ready, FLOOR + (t + 1))
                        act.dma_start(qkv_d[bass.ts(t, P), :], y[u % NB][:].rearrange("p g n -> p (g n)")
                                      ).then_inc(stored[u % NB], 16)
                for j in range(NB):
                    act.wait_ge(stored[j], FLOOR + 16 * TILES // NB)


def consts():
    pos = np.arange(T, dtype=np.float32)[:, None]
    inv = (np.float32(1.0) / np.float32(10000.0) ** (np.arange(8, dtype=np.float32) / np.float32(8))).astype(np.float32)
    ang = (pos * inv[None, :]).astype(np.float32)
    lay = lambda m: np.ascontiguousarray(m.astype(np.float32).reshape(NT, P, 8).transpose(1, 0, 2))
    kaug = np.zeros((32, HG), np.float32)
    for h in range(HG):
        kaug[3 * h:3 * h + 3, h] = 1.0
    tok = np.arange(T).reshape(NT, P).T
    iota = np.broadcast_to(np.arange(T, dtype=np.float32), (P, T)).copy()
    tok2 = np.stack([tok // 32 * 32, tok % 32], -1).astype(np.float32)
    return {"iota": iota, "tok": tok2, "kaug": kaug, "cos": lay(np.cos(ang)), "sin": lay(np.sin(ang)), "ident": np.eye(P, dtype=np.float32)}
def attend(nc, qkv_d, ident_d, kaug_d, ctx_d):
    NG = B * G
    S6 = 6
    ROWS = S6 * HD
    STEPS = 2 * (NT // 2)
    UNITS = 2 * HG * NT
    SINGLES = 64
    FIRST, PLACES = 8, 66
    PART_AT = {k: c for c, k in enumerate((4, 6, 10, 14, 18, 22, 26, 30))}
    VPARTS = 2
    CTX0 = 46
    Q_SLOT = {"h": (0, 1, 2), "m": (3, 4), "l": (5,)}
    K_SLOT = {"h": (0, 3, 5), "m": (1, 4), "l": (2,)}
    nc.disable_value_cache = True
    with Stage(nc, "att") as st:
        gin = [st.sb(f"gin{j}", [P, NT, 3 * GW]) for j in range(2)]
        hi = st.sb("hi", [P, NT, 2 * GW], BF16)
        mid = st.sb("mid", [P, NT, 2 * GW], BF16)
        low = st.sb("low", [P, NT, 2 * GW], BF16)
        rest = st.sb("rest", [P, NT, 2 * GW])
        nat = st.sb("nat", [P, NT, 2, HG, S6, HD], BF16)
        va = [st.sb(f"va{j}", [P, NT, HG, 32]) for j in range(2)]
        QT = [st.sb(f"QT{j}", [P, HG, T], BF16) for j in range(2)]
        KT = [st.sb(f"KT{j}", [P, HG, T], BF16) for j in range(2)]
        ident = st.sb("ident", [P, P])
        identb = st.sb("identb", [P, P], BF16)
        kaug = st.sb("kaug", [P, HG])
        mx2 = st.sb("mx2", [P, NT, HG, 2])
        mx = st.sb("mx", [P, NT, HG])
        mrest = st.sb("mrest", [P, NT, HG])
        naug = st.sb("naug", [P, NT, 32], BF16)
        pt = st.sb("pt", [P, 8, 2, 512])
        osb = st.sb("osb", [P, T])
        rec = st.sb("rec", [P, NT // 2, HG])
        ctx = [st.sb(f"ctx{j}", [P, NT, HG, HD]) for j in range(2)]
        s1 = st.ps("s1", [P, 3, 512])
        sT = st.ps("sT", [P, 3, 512])
        o = st.ps("o", [P, 512])
        tr = st.ps("tr", [P, 512])
        trb = tr[:].bitcast(BF16)
        c_in = st.sem("c_in")
        g_in = [st.sem(f"g_in{j}") for j in range(2)]
        ready0 = st.sem("ready0")
        chain = st.sem("chain")
        pchain = st.sem("pchain")
        nat_done = st.sem("nat_done")
        v_ready = st.sem("v_ready")
        turned = st.sem("turned")
        evac = st.sem("evac")
        scored = st.sem("scored")
        maxed = st.sem("maxed")
        naug_ready = st.sem("naug_ready")
        aug_turned = st.sem("aug_turned")
        aug_ready = st.sem("aug_ready")
        st_done = st.sem("st_done")
        exp_done = st.sem("exp_done")
        pv_done = st.sem("pv_done")
        o_evac = st.sem("o_evac")
        o_turned = st.sem("o_turned")
        rec_ready = st.sem("rec_ready")
        ctx_ready = st.sem("ctx_ready")
        stored = [st.sem(f"stored{j}") for j in range(2)]
        qkv_v = qkv_d.rearrange("(b t p) (g n) -> b p t g n", p=P, t=NT, g=G)
        ctx_v = ctx_d.rearrange("(b t p) (g n) -> b p t g n", p=P, t=NT, g=G)

        at_place = {FIRST + u * PLACES // UNITS: u for u in range(UNITS)}

        with st.block() as block:

            @block.sync
            def _(sp):
                sp.dma_start(ident[:], ident_d).then_inc(c_in, 16)
                sp.dma_start(kaug[96:P, :], kaug_d).then_inc(c_in, 16)
                sp.dma_start(gin[0][:], qkv_v[0, :, :, 0, :]).then_inc(g_in[0], 16)
                sp.dma_start(gin[1][:], qkv_v[0, :, :, 1, :]).then_inc(g_in[1], 16)
                with sp.Fori(0, NG // 2) as i:
                    for j in range(2):
                        g = i * 2 + j
                        n = (i * 2 + (j + 2)) % NG
                        sp.wait_ge(v_ready, FLOOR + (g + 1))
                        sp.dma_start(gin[j][:], qkv_v[n // G, :, :, n % G, :]).then_inc(g_in[j], 16)
                        sp.wait_ge(ctx_ready, FLOOR + (g * 2 + 2))
                        g_ = i * 2 + j
                        sp.dma_start(ctx_v[g_ // G, :, :, g_ % G, :],
                                     ctx[j][:].rearrange("p t h e -> p t (h e)")).then_inc(stored[j], 16)
                for j in range(2):
                    sp.wait_ge(g_in[j], FLOOR + (16 * (NG // 2 + 1)))
                    sp.wait_ge(stored[j], FLOOR + 16 * NG // 2)

            @block.gpsimd
            def _(pool):
                for j in range(2):
                    ins = pool.memset(va[j][:], 0.0)
                ins.then_inc(pchain, 1)
                pool.wait_ge(pchain, FLOOR + 1)
                for j in range(2):
                    pool.memset(va[j][:, :, :, HD:HD + 1], 1.0)

                def split(n, par, loads):
                    ch = Chain(pool, pchain, n, 4)
                    ch.base = ch.base + 1
                    pool.wait_ge(g_in[par], FLOOR + loads * 16)
                    qk = gin[par][:, :, 0:2 * GW]
                    pool.wait_ge(nat_done, FLOOR + n)
                    st.settle(pool)
                    ch.link(pool.tensor_copy(hi[:], qk))
                    ch.link(pool.tensor_tensor(rest[:], qk, hi[:], ALU.subtract))
                    st.settle(pool)
                    ch.link(pool.tensor_copy(mid[:], rest[:]))
                    ch.link(pool.tensor_tensor(low[:], rest[:], mid[:], ALU.subtract))
                    ch.close()
                    pool.wait_ge(turned, FLOOR + n * 8)
                    st.settle(pool)
                    for part, src in (("h", hi), ("m", mid), ("l", low)):
                        for c, slots in enumerate((Q_SLOT[part], K_SLOT[part])):
                            for s in slots:
                                v = src[:, :, c * GW:(c + 1) * GW].rearrange("p t (h e) -> p t h e", h=HG)
                                ins = pool.tensor_copy(nat[:, :, c, :, s, :], v)
                    ins.then_inc(nat_done, 1)
                    if not isinstance(n, int):
                        pool.wait_ge(pv_done, FLOOR + (n * STEPS - STEPS))
                        st.settle(pool)
                    pool.tensor_copy(va[par][:, :, :, 0:HD],
                                     gin[par][:, :, 2 * GW:3 * GW].rearrange("p t (h e) -> p t h e", h=HG)
                                     ).then_inc(v_ready, 1)

                split(0, 0, 1)
                with pool.Fori(0, NG // 2) as i:
                    for j in range(2):
                        split(i * 2 + (j + 1), 1 - j, i + 1 + j)

            @block.tensor
            def _(pe):
                def turn_parts(n, par, c):
                    if c == 0:
                        pe.wait_ge(nat_done, FLOOR + (n + 1))
                        if not isinstance(n, int):
                            pe.wait_ge(ctx_ready, FLOOR + (n * 2 - 2))
                    pe.wait_ge(evac, FLOOR + (n * 8 + c))
                    h, w = c // 2, c % 2
                    for t in range(NT):
                        ins = pe.transpose(trb[0:ROWS, t * P:(t + 1) * P],
                                           nat[:, t, w, h].rearrange("p s e -> p (s e)"), identb[:])
                    ins.then_inc(turned, 1)

                def score_unit(n, par, u):
                    h, t, c = u // (2 * NT), u // 2 % NT, u % 2
                    if u % (2 * NT) == 0:
                        pe.wait_ge(evac, FLOOR + (n * 8 + (2 * h + 2)))
                    pe.wait_ge(maxed, FLOOR + (n * UNITS + max(u - 2, 0)))
                    pe.matmul(s1[:, u % 3, :], QT[par][0:ROWS, h, t * P:(t + 1) * P],
                              KT[par][0:ROWS, h, c * 512:(c + 1) * 512], start=True, stop=True).then_inc(scored, 1)

                def turn_ctx(g, n, q):
                    pe.wait_ge(o_evac, FLOOR + (g * 2 + q + 1))
                    if q == 0:
                        pe.wait_ge(evac, FLOOR + (n * 8 + 8))
                    else:
                        pe.wait_ge(aug_ready, FLOOR + (n * HG + 1))
                    for t in range(4):
                        ins = pe.transpose(tr[:, t * P:(t + 1) * P], osb[:, (q * 4 + t) * P:(q * 4 + t + 1) * P], ident[:])
                    ins.then_inc(o_turned, 1)

                def turn_max(n, g=None):
                    pe.wait_ge(naug_ready, FLOOR + (n + 1))
                    pe.wait_ge(evac, FLOOR + (n * 8 + 8))
                    if g is not None:
                        pe.wait_ge(ctx_ready, FLOOR + (g * 2 + 1))
                    for t in range(NT):
                        ins = pe.transpose(trb[96:P, t * P:(t + 1) * P], naug[:, t, :], identb[:])
                    ins.then_inc(aug_turned, 1)

                def score_T(g, par, s, c, h):
                    idx = (s * 2 + c) * HG + h
                    pe.wait_ge(exp_done, FLOOR + (g * SINGLES + max(idx - 2, 0)))
                    kt = s % 4 * 2 + c
                    pe.matmul(sT[:, idx % 3, :], KT[par][:, h, kt * P:(kt + 1) * P],
                              QT[par][:, h, s // 4 * 512:(s // 4 + 1) * 512], start=True, stop=True).then_inc(st_done, 1)

                def times_v(g, par, s, c):
                    kt = s % 4 * 2 + c
                    pe.wait_ge(exp_done, FLOOR + (g * SINGLES + (s * 2 + c + 1) * HG))
                    if s == 0 and c == 0:
                        pe.wait_ge(v_ready, FLOOR + (g + 1))
                    if kt == 0:
                        pe.wait_ge(o_evac, FLOOR + (g * 2 + s // 4))
                    for h in range(HG):
                        ins = pe.matmul(o[32 * h:32 * h + 32, :], va[par][:, kt, h, :],
                                        pt[:, (s % 2) * HG + h, c, :], start=kt == 0, stop=kt == NT - 1)
                    if c == 1:
                        ins.then_inc(pv_done, 1)

                pe.wait_ge(c_in, FLOOR + 32)
                pe.wait_ge(ready0, FLOOR + 1)
                for c in range(8):
                    turn_parts(0, 0, c)
                for u in range(UNITS):
                    score_unit(0, 0, u)
                turn_max(0)
                with pe.Fori(0, NG // 2) as i:
                    for j in range(2):
                        g, n, par = i * 2 + j, i * 2 + (j + 1), 1 - j
                        for k in range(SINGLES):
                            s, c, h = k // 8, k // HG % 2, k % HG
                            if k < HG:
                                pe.wait_ge(aug_ready, FLOOR + (g * HG + h + 1))
                            if k in PART_AT:
                                turn_parts(n, par, PART_AT[k])
                            if k == CTX0:
                                turn_ctx(g, n, 0)
                            score_T(g, j, s, c, h)
                            place = s * 10 + c * 5 + h
                            if place in at_place:
                                score_unit(n, par, at_place[place])
                            if h == HG - 1:
                                if s > 0:
                                    times_v(g, j, s - 1, c)
                                if place + 1 in at_place:
                                    score_unit(n, par, at_place[place + 1])
                        times_v(g, j, STEPS - 1, 0)
                        turn_max(n, g)
                        times_v(g, j, STEPS - 1, 1)
                        turn_ctx(g, n, 1)

            @block.scalar
            def _(act):
                def evacuate(n, par, c):
                    if not isinstance(n, int) and c == VPARTS:
                        act.wait_ge(st_done, FLOOR + (n * SINGLES - SINGLES))
                    act.wait_ge(turned, FLOOR + (n * 8 + c + 1))
                    dst = (QT, KT)[c % 2][par]
                    act.activation(dst[0:ROWS, c // 2, :], trb[0:ROWS, :], ACT.Copy).then_inc(evac, 1)

                for c in range(8):
                    evacuate(0, 0, c)
                with act.Fori(0, NG // 2) as i:
                    for j in range(2):
                        g = i * 2 + j
                        for s in range(STEPS):
                            act.wait_ge(pv_done, FLOOR + (g * STEPS + max(s - 1, 0)))
                            for q in range(2 * HG):
                                c, h = q // HG, q % HG
                                k = s * 2 * HG + q
                                if PART_AT.get(k, 0) >= VPARTS:
                                    evacuate(i * 2 + (j + 1), 1 - j, PART_AT[k])
                                act.wait_ge(st_done, FLOOR + (g * SINGLES + (k + 1)))
                                act.activation(pt[:, (s % 2) * HG + h, c], sT[:, k % 3, :], ACT.Exp,
                                               scale=HD ** -0.5).then_inc(exp_done, 1)
                        act.wait_ge(pv_done, FLOOR + (g * STEPS + STEPS))
                        act.wait_ge(o_turned, FLOOR + g * 2)
                        act.activation(osb[:, 512:T], o[:], ACT.Copy).then_inc(o_evac, 1)

            @block.vector
            def _(dve):
                dve.wait_ge(c_in, FLOOR + 32)
                for j in range(2):
                    for h in range(HG):
                        dve.tensor_copy(KT[j][96:P, h, :], kaug[96:P, h:h + 1].broadcast_to([32, T]))
                dve.memset(naug[:], 0.0)
                dve.tensor_copy(identb[:], ident[:]).then_inc(ready0, 1)

                def take_max(n, u):
                    dve.wait_ge(scored, FLOOR + (n * UNITS + u + 1))
                    h, t, c = u // (2 * NT), u // 2 % NT, u % 2
                    dve.tensor_reduce(mx2[:, t, h, c:c + 1], s1[:, u % 3, :], AX.X, ALU.max).then_inc(maxed, 1)

                def split_max(n):
                    ch = Chain(dve, chain, n, 4)
                    dve.wait_ge(maxed, FLOOR + (n * UNITS + UNITS))
                    dve.wait_ge(aug_turned, FLOOR + n)
                    ch.link(dve.tensor_tensor(mx[:], mx2[:, :, :, 0], mx2[:, :, :, 1], ALU.max))
                    ch.link(dve.tensor_scalar(naug[:, :, 0:12:3], mx[:], -1.0, None, ALU.mult))
                    ch.link(dve.scalar_tensor_tensor(mrest[:], mx[:], -1.0, naug[:, :, 0:12:3], ALU.mult, ALU.subtract))
                    ch.link(dve.tensor_copy(naug[:, :, 1:12:3], mrest[:]))
                    dve.tensor_tensor(naug[:, :, 2:12:3], mrest[:], naug[:, :, 1:12:3], ALU.subtract
                                      ).then_inc(naug_ready, 1)
                    ch.close()

                def place_max(n, par):
                    dve.wait_ge(aug_turned, FLOOR + (n + 1))
                    dve.tensor_copy(QT[par][96:P, 0, :], trb[96:P, :]).then_inc(aug_ready, 1)
                    dve.wait_ge(aug_ready, FLOOR + (n * HG + 1))
                    for h in range(1, HG):
                        dve.tensor_copy(QT[par][96:P, h, :], QT[par][96:P, 0, :]).then_inc(aug_ready, 1)

                for u in range(UNITS):
                    take_max(0, u)
                split_max(0)
                place_max(0, 0)
                with dve.Fori(0, NG // 2) as i:
                    for j in range(2):
                        g, n, par = i * 2 + j, i * 2 + (j + 1), 1 - j

                        def divide(q):
                            dve.wait_ge(o_turned, FLOOR + (g * 2 + q + 1))
                            dve.reciprocal(rec[:], trv[:, :, :, HD]).then_inc(rec_ready, 1)
                            dve.wait_ge(rec_ready, FLOOR + (g * 2 + q + 1))
                            dve.tensor_tensor(ctx[j][:, 4 * q:4 * q + 4], trv[:, :, :, 0:HD],
                                              rec[:].rearrange("p t (h a) -> p t h a", a=1).broadcast_to([P, 4, HG, HD]),
                                              ALU.mult).then_inc(ctx_ready, 1)

                        trv = tr[:].rearrange("p (t h e) -> p t h e", t=4, h=HG)
                        part_places = [k // 8 * 10 + k // HG % 2 * 5 + k % HG
                                       for k in PART_AT][:VPARTS]
                        for place in range(STEPS * 10):
                            if place in part_places:
                                c = part_places.index(place)
                                if c == 0:
                                    dve.wait_ge(st_done, FLOOR + g * SINGLES)
                                dve.wait_ge(turned, FLOOR + (n * 8 + c + 1))
                                dve.tensor_copy((QT, KT)[c % 2][par][0:ROWS, c // 2, :], trb[0:ROWS, :]).then_inc(evac, 1)
                            if place in at_place:
                                take_max(n, at_place[place])
                            if place == 50:
                                dve.wait_ge(pv_done, FLOOR + (g * STEPS + 4))
                                dve.wait_ge(o_turned, FLOOR + g * 2)
                                dve.tensor_copy(osb[:, 0:512], o[:]).then_inc(o_evac, 1)
                            if place == 64:
                                dve.wait_ge(stored[j], FLOOR + i * 16)
                                divide(0)
                        split_max(n)
                        place_max(n, par)
                        divide(1)
    nc.disable_value_cache = False
def project(nc, tag, ctx_d, w_d, b_d, x_d, ident_d, out_d):
    TC = 4
    TURNS = TILES // TC
    U = 4
    N = TC * P
    rows = lambda d, t: d[bass.ds(t * N, N), :].rearrange("(t p) d -> p t d", p=P)
    with Stage(nc, tag) as st:
        w = st.sb("w", [P, KD, D])
        bias = st.sb("bias", [P, D])
        ident = st.sb("ident", [P, P])
        c = [st.sb(f"c{j}", [P, TC, D]) for j in range(U)]
        x = [st.sb(f"x{j}", [P, TC, D]) for j in range(U)]
        cT = [st.sb(f"cT{j}", [P, TC, KD, P]) for j in range(2)]
        tr = [st.ps(f"tr{j}", [P, TC, KD, P]) for j in range(2)]
        mm = [st.ps(f"mm{j}", [P, TC, D]) for j in range(2)]
        w_in = st.sem("w_in")
        ctx_in = [st.sem(f"ctx_in{j}") for j in range(U)]
        x_in = [st.sem(f"x_in{j}") for j in range(U)]
        turned = st.sem("turned")
        cT_ready = st.sem("cT_ready")
        biased = st.sem("biased")
        made = st.sem("made")
        summed = st.sem("summed")
        stored = [st.sem(f"stored{j}") for j in range(U)]
        with st.block() as block:

            @block.sync
            def _(sp):
                sp.dma_start(ident[:], ident_d).then_inc(w_in, 16)
                sp.dma_start(c[0][:], rows(ctx_d, 0)).then_inc(ctx_in[0], 16)
                sp.dma_start(w[:], w_d.rearrange("(k p) n -> p k n", p=P)).then_inc(w_in, 16)
                sp.dma_start(bias[:], col_bcast(b_d)).then_inc(w_in, 16)
                sp.dma_start(c[1][:], rows(ctx_d, 1)).then_inc(ctx_in[1], 16)
                with sp.Fori(0, TURNS // U) as i:
                    for j in range(U):
                        t = i * U + j
                        sp.wait_ge(stored[j], FLOOR + i * 16)
                        sp.dma_start(x[j][:], rows(x_d, t)).then_inc(x_in[j], 16)
                        sp.wait_ge(turned, FLOOR + i * U + max(j - 1, 0))
                        sp.dma_start(c[(j + 2) % U][:], rows(ctx_d, (t + 2) % TURNS)).then_inc(ctx_in[(j + 2) % U], 16)
                for j in range(2):
                    sp.wait_ge(ctx_in[j], FLOOR + 16 * (TURNS // U + 1))

            @block.tensor
            def _(pe):
                def turn_context(j, u, loads):
                    pe.wait_ge(ctx_in[u], FLOOR + loads * 16)
                    for q in range(TC):
                        for k in range(KD):
                            ins = pe.transpose(tr[j][:, q, k, :], c[u][:, q, k * P:(k + 1) * P], ident[:])
                    ins.then_inc(turned, 1)

                pe.wait_ge(w_in, FLOOR + 48)
                turn_context(0, 0, 1)
                with pe.Fori(0, TURNS // U) as i:
                    for u in range(U):
                        t, j = i * U + u, u % 2
                        pe.wait_ge(cT_ready, FLOOR + t)
                        turn_context(1 - j, (u + 1) % U, i + (1 + (u + 1) // U))
                        pe.wait_ge(cT_ready, FLOOR + (t + 1))
                        pe.wait_ge(summed, FLOOR + i * U + max(u - 1, 0))
                        for q in range(TC):
                            for k in range(KD):
                                ins = pe.matmul(mm[j][:, q, :], cT[j][:, q, k, :], w[:, k, :],
                                                start=k == 0, stop=k == KD - 1)
                        ins.then_inc(made, 1)

            @block.scalar
            def _(act):
                act.wait_ge(turned, FLOOR + 1)
                act.activation(cT[0][:], tr[0][:], ACT.Copy).then_inc(cT_ready, 1)
                with act.Fori(0, TURNS // U) as i:
                    for u in range(U):
                        t, j = i * U + u, u % 2
                        act.wait_ge(turned, FLOOR + (t + 2))
                        act.wait_ge(made, FLOOR + t)
                        act.activation(cT[1 - j][:], tr[1 - j][:], ACT.Copy).then_inc(cT_ready, 1)
                        act.wait_ge(summed, FLOOR + (t + 1))
                        act.dma_start(rows(out_d, t), x[u][:]).then_inc(stored[u], 16)
                for u in range(U):
                    act.wait_ge(stored[u], FLOOR + 16 * TURNS // U)

            @block.vector
            def _(dve):
                with dve.Fori(0, TURNS // U) as i:
                    for u in range(U):
                        t, j = i * U + u, u % 2
                        dve.wait_ge(biased, FLOOR + (t + 1))
                        dve.wait_ge(made, FLOOR + (t + 1))
                        dve.tensor_tensor(x[u][:], x[u][:], mm[j][:], ALU.add).then_inc(summed, 1)

            @block.gpsimd
            def _(pool):
                pool.wait_ge(w_in, FLOOR + 48)
                with pool.Fori(0, TURNS // U) as i:
                    for j in range(U):
                        pool.wait_ge(x_in[j], FLOOR + (i * 16 + 16))
                        pool.tensor_tensor(x[j][:], x[j][:],
                                           bias[:].rearrange("p (a n) -> p a n", a=1).broadcast_to([P, TC, D]),
                                           ALU.add).then_inc(biased, 1)


def route(nc, xnT_d, gate_d, ident_d, pos_d, aff_d):
    U = 4
    with Stage(nc, "rt") as st:
        ident = st.sb("ident", [P, P])
        gw = st.sb("gw", [P, KD, E])
        xT = [st.sb(f"xT{u}", [P, KD, T]) for u in range(U)]
        lg = st.sb("lg", [P, NT, E])
        ex = st.sb("ex", [P, NT, E])
        mx = st.sb("mx", [P, NT])
        sm = st.sb("sm", [P, NT])
        aff = st.sb("aff", [P, NT, B, E])
        work = st.sb("work", [B * E, T])
        sel = st.sb("sel", [B * E, T])
        ones = st.sb("ones", [B * E, T])
        pos = st.sb("pos", [B * E, T])
        m8 = st.sb("m8", [B * E, 8])
        posT = st.sb("posT", [P, NT, B * E])
        lp = [st.ps(f"lp{j}", [P, NT, E]) for j in range(2)]
        rows = st.ps("rows", [B * E, T])
        cols = st.ps("cols", [P, NT, B * E])
        c_in = st.sem("c_in")
        x_in = [st.sem(f"x_in{u}") for u in range(U)]
        made = st.sem("made")
        read = st.sem("read")
        shifted = st.sem("shifted")
        exped = st.sem("exped")
        chain = st.sem("chain")
        aff_ready = st.sem("aff_ready")
        turned = st.sem("turned")
        pos_ready = st.sem("pos_ready")
        turned_back = st.sem("turned_back")
        posT_ready = st.sem("posT_ready")
        stored = st.sem("stored")
        with st.block() as block:

            @block.sync
            def _(sp):
                sp.dma_start(ident[:], ident_d).then_inc(c_in, 16)
                sp.dma_start(gw[:], gate_d.rearrange("(k p) e -> p k e", p=P)).then_inc(c_in, 16)
                for b in range(B):
                    if b >= U:
                        sp.wait_ge(made, FLOOR + (b - U + 1))
                    sp.dma_start(xT[b % U][:], xnT_d[:, :, b * T:(b + 1) * T].rearrange("k p t -> p k t")
                                 ).then_inc(x_in[b % U], 16)
                sp.wait_ge(aff_ready, FLOOR + 1)
                sp.dma_start(aff_d, aff[:]).then_inc(stored, 16)
                sp.wait_ge(posT_ready, FLOOR + 1)
                sp.dma_start(pos_d, posT[:]).then_inc(stored, 16)
                sp.wait_ge(stored, FLOOR + 32)

            @block.tensor
            def _(pe):
                pe.wait_ge(c_in, FLOOR + 32)
                with pe.Fori(0, B // U) as i:
                    for u in range(U):
                        j = u % 2
                        pe.wait_ge(x_in[u], FLOOR + (i * 16 + 16))
                        pe.wait_ge(read, FLOOR + (i * U + max(u - 1, 0)))
                        for t in range(NT):
                            for k in range(KD):
                                ins = pe.matmul(lp[j][:, t, :], xT[u][:, k, t * P:(t + 1) * P], gw[:, k, :],
                                                start=k == 0, stop=k == KD - 1)
                        ins.then_inc(made, 1)
                pe.wait_ge(aff_ready, FLOOR + 1)
                for t in range(NT):
                    ins = pe.transpose(rows[:, t * P:(t + 1) * P], aff[:, t].rearrange("p b e -> p (b e)"), ident[:])
                ins.then_inc(turned, 1)
                pe.wait_ge(pos_ready, FLOOR + 1)
                for t in range(NT):
                    ins = pe.transpose(cols[:, t, :], pos[:, t * P:(t + 1) * P], ident[0:B * E, 0:B * E])
                ins.then_inc(turned_back, 1)

            @block.scalar
            def _(act):
                with act.Fori(0, B) as b:
                    act.wait_ge(shifted, FLOOR + (b + 1))
                    act.activation(ex[:], lg[:], ACT.Exp).then_inc(exped, 1)

            @block.vector
            def _(dve):
                dve.memset(ones[:], 1.0)
                with dve.Fori(0, B // 2) as i:
                    for j in range(2):
                        b = i * 2 + j
                        ch = Chain(dve, chain, b, 4)
                        dve.wait_ge(made, FLOOR + (b + 1))
                        ch.link(dve.tensor_reduce(mx[:], lp[j][:], AX.X, ALU.max))
                        dve.tensor_tensor(lg[:], lp[j][:], mx[:].rearrange("p (t a) -> p t a", a=1).broadcast_to([P, NT, E]),
                                          ALU.subtract).then_inc(shifted, 1)
                        dve.wait_ge(shifted, FLOOR + (b + 1))
                        dve.wait_ge(exped, FLOOR + (b + 1))
                        ch.link(dve.tensor_reduce(sm[:], ex[:], AX.X, ALU.add))
                        ch.link(dve.reciprocal(sm[:], sm[:]))
                        ch.link(dve.tensor_tensor(aff[:, :, b, :], ex[:],
                                                  sm[:].rearrange("p (t a) -> p t a", a=1).broadcast_to([P, NT, E]),
                                                  ALU.mult))
                        ch.close()
                        dve.sem_inc(read, 1)
                dve.sem_inc(aff_ready, 1)
                dve.wait_ge(turned, FLOOR + 1)
                ch = Chain(dve, chain)
                ch.base = 4 * B
                ch.link(dve.tensor_copy(work[:], rows[:]))
                with dve.Fori(0, CAP // 8) as r:
                    cr = Chain(dve, chain, r, 2)
                    cr.base = cr.base + (4 * B + 1)
                    cr.link(dve.max(m8[:], work[:]))
                    st.settle(dve)
                    cr.link(dve.match_replace(work[:], m8[:], work[:], -1.0))
                ch.base += 2 * CAP // 8
                ch.link(dve.tensor_scalar(sel[:], work[:], 0.0, None, ALU.is_lt))
                ch.link(dve.tensor_tensor_scan(pos[:], ones[:], sel[:], 0.0, ALU.mult, ALU.add))
                ch.link(dve.tensor_tensor(pos[:], pos[:], sel[:], ALU.mult))
                dve.tensor_scalar(pos[:], pos[:], -1.0, None, ALU.add).then_inc(pos_ready, 1)
                dve.wait_ge(turned_back, FLOOR + 1)
                dve.tensor_copy(posT[:], cols[:]).then_inc(posT_ready, 1)


def experts(nc, xn_d, pos_d, aff_d, wg_d, wu_d, wd_d, iota_d, tok_d, x_d, out_d):
    NB = 4
    NI = I // P
    NS = CAP // P
    WAY = (B // NB) * E
    xn_v = xn_d.rearrange("(b t p) d -> b p t d", p=P, t=NT)
    x_v = x_d.rearrange("(b t p) d -> b p t d", p=P, t=NT)
    out_v = out_d.rearrange("(b t p) d -> b p t d", p=P, t=NT)
    with Stage(nc, "moe") as st:
        iota = st.sb("iota", [P, T])
        iotab = st.sb("iotab", [P, CAP], BF16)
        posT = st.sb("posT", [P, NT, B * E])
        aff = st.sb("aff", [P, NT, B * E])
        arest = st.sb("arest", [P, NT, B * E])
        affs = st.sb("affs", [P, NT, B * E, 5], BF16)
        tok = st.sb("tok", [P, NT, 2])
        stage = [st.sb(f"stage{j}", [P, NT, D]) for j in range(2)]
        xs = [st.sb(f"xs{b}", [P, NT, 3, D], BF16) for b in range(NB)]
        acc = [st.sb(f"acc{b}", [P, NT, D]) for b in range(NB)]
        wg = st.sb("wg", [P, KD, I])
        wu = st.sb("wu", [P, KD, I])
        wd = st.sb("wd", [P, NI, D])
        onehot = st.sb("onehot", [P, NT, CAP], BF16)
        onehotT = st.sb("onehotT", [P, NS, T], BF16)
        gi = st.sb("gi", [P, NS, 5])
        gate = [st.sb(f"gate{j}", [P, NS]) for j in range(2)]
        idx = [st.sb(f"idx{j}", [P, NS]) for j in range(2)]
        xsel = st.sb("xsel", [P, KD, CAP])
        sg = st.sb("sg", [P, NI, CAP])
        hT = st.sb("hT", [P, NI, CAP])
        y = st.sb("y", [P, 3, NS, D], BF16)
        rest = st.sb("rest", [P, NS, D])
        pg = st.ps("pg", [P, KD, CAP])
        gp = st.ps("gp", [P, NI, CAP])
        up = st.ps("up", [P, NI, CAP])
        yp = st.ps("yp", [P, NS, D])
        pi = yp[:, 0, 0:NS * 5].rearrange("p (s c) -> p s c", c=5)
        back = [st.ps(f"back{j}", [P, 2, D]) for j in range(2)]
        c_in = st.sem("c_in")
        w_in = st.sem("w_in")
        wd_in = st.sem("wd_in")
        stage_in = [st.sem(f"stage_in{j}") for j in range(2)]
        part_made = st.sem("part_made")
        part_off = st.sem("part_off")
        acc_in = [st.sem(f"acc_in{b}") for b in range(NB)]
        acc_out = [st.sem(f"acc_out{b}") for b in range(NB)]
        zeroed = st.sem("zeroed")
        split = st.sem("split")
        pchain = st.sem("pchain")
        chain = st.sem("chain")
        hot_ready = st.sem("hot_ready")
        gathered = st.sem("gathered")
        xsel_ready = st.sem("xsel_ready")
        hotT_ready = st.sem("hotT_ready")
        gu_done = st.sem("gu_done")
        silued = st.sem("silued")
        h_ready = st.sem("h_ready")
        down = st.sem("down")
        gi_read = st.sem("gi_read")
        high_ready = st.sem("high_ready")
        rest_ready = st.sem("rest_ready")
        mid_ready = st.sem("mid_ready")
        y_ready = st.sem("y_ready")
        scat = st.sem("scat")
        added = st.sem("added")
        with st.block() as block:

            @block.sync
            def _(sp):
                sp.dma_start(iota[:], iota_d).then_inc(c_in, 16)
                sp.dma_start(posT[:], pos_d).then_inc(c_in, 16)
                sp.dma_start(aff[:], aff_d.rearrange("p t b e -> p t (b e)")).then_inc(c_in, 16)
                sp.dma_start(tok[:], tok_d).then_inc(c_in, 16)
                def weights(i, e):
                    sp.wait_ge(gu_done, FLOOR + i * NB)
                    sp.dma_start(wg[:], wg_d[e, :, :].rearrange("(k p) n -> p k n", p=P)).then_inc(w_in, 16)
                    sp.dma_start(wu[:], wu_d[e, :, :].rearrange("(k p) n -> p k n", p=P)).then_inc(w_in, 16)
                    sp.wait_ge(down, FLOOR + i * NB)
                    sp.dma_start(wd[:], wd_d[e, :, :].rearrange("(k p) n -> p k n", p=P)).then_inc(wd_in, 16)

                with sp.Fori(0, E) as i:
                    weights(i, i)
                for b in range(NB):
                    sp.wait_ge(split, FLOOR + (NB + b - 1))
                    sp.dma_start(stage[b % 2][:], xn_v[NB + b]).then_inc(stage_in[b % 2], 16)
                weights(E, 0)
                for b in range(NB):
                    sp.wait_ge(added, FLOOR + (4 * (NB * (E - 1) + b + 2)))
                    sp.dma_start(out_v[b], acc[b][:]).then_inc(acc_out[b], 16)
                for b in range(NB):
                    sp.wait_ge(acc_out[b], FLOOR + 16)
                    sp.dma_start(acc[b][:], x_v[NB + b]).then_inc(acc_in[b], 16)
                with sp.Fori(E + 1, 2 * E) as i:
                    weights(i, i - E)
                for b in range(NB):
                    sp.wait_ge(added, FLOOR + (4 * (NB * (2 * E - 1) + b + 2)))
                    sp.dma_start(out_v[NB + b], acc[b][:]).then_inc(acc_out[b], 16)
                for b in range(NB):
                    sp.wait_ge(acc_out[b], FLOOR + 32)

            @block.scalar
            def _(act):
                def split_batch(b):
                    act.wait_ge(stage_in[b % 2], FLOOR + 16 * (b // 2 + 1))
                    act.activation(xs[b][:, :, 0, :], stage[b % 2][:], ACT.Copy).then_inc(part_made, 1)
                    act.wait_ge(part_off, FLOOR + (b + 1))
                    act.activation(xs[b][:, :, 1, :], stage[b % 2][:], ACT.Copy).then_inc(part_made, 1)
                    if b + 2 < NB:
                        act.wait_ge(split, FLOOR + (b + 1))
                        act.dma_start(stage[b % 2][:], xn_v[b + 2]).then_inc(stage_in[b % 2], 16)

                for b in range(2):
                    act.dma_start(stage[b][:], xn_v[b]).then_inc(stage_in[b], 16)
                split_batch(0)
                for b in range(NB):
                    act.dma_start(acc[b][:], x_v[b]).then_inc(acc_in[b], 16)
                split_batch(1)
                act.wait_ge(gathered, FLOOR + 1)
                act.activation(xsel[:], pg[:], ACT.Copy).then_inc(xsel_ready, 1)
                split_batch(2)
                split_batch(3)
                with act.Fori(0, WAY) as i:
                    for b in range(NB):
                        turn = i * NB + b
                        act.wait_ge(gu_done, FLOOR + (turn + 1))
                        act.activation(sg[:], gp[:], ACT.Silu).then_inc(silued, 1)
                        act.wait_ge(gathered, FLOOR + (turn + 2))
                        act.activation(xsel[:], pg[:], ACT.Copy).then_inc(xsel_ready, 1)
                        act.wait_ge(down, FLOOR + (turn + 1))
                        act.wait_ge(scat, FLOOR + (turn * 4 + 4))
                        for s in range(NS):
                            act.activation(y[:, 0, s, :], yp[:, s, :], ACT.Copy, scale=gate[b % 2][:, s:s + 1]
                                           ).then_inc(high_ready, 1)

            @block.gpsimd
            def _(pool):
                ch = Chain(pool, pchain)

                def split_batch(b):
                    part, whole = xs[b], stage[b % 2]
                    ch.link(pool.tensor_copy(part[:, :, 0, :], whole[:]))
                    ch.link(pool.tensor_tensor(whole[:], whole[:], part[:, :, 0, :], ALU.subtract))
                    ch.link(pool.tensor_copy(part[:, :, 1, :], whole[:]))
                    pool.tensor_tensor(part[:, :, 2, :], whole[:], part[:, :, 1, :], ALU.subtract).then_inc(split, 1)

                def lower_parts(turn):
                    pool.wait_ge(rest_ready, FLOOR + (turn + 1))
                    pool.wait_ge(scat, FLOOR + (turn * 4 + 4))
                    st.settle(pool)
                    pool.tensor_copy(y[:, 1], rest[:]).then_inc(mid_ready, 1)
                    pool.wait_ge(mid_ready, FLOOR + (turn + 1))
                    pool.tensor_tensor(y[:, 2], rest[:], y[:, 1], ALU.subtract).then_inc(y_ready, 1)

                pool.memset(y[:], 0.0).then_inc(y_ready, 1)
                with pool.Fori(0, NB * (E - 1)) as turn:
                    lower_parts(turn)
                for b in range(NB):
                    lower_parts(NB * (E - 1) + b)
                    pool.wait_ge(gathered, FLOOR + (NB * (E - 1) + b + 1))
                    pool.wait_ge(stage_in[b % 2], FLOOR + (32 + 16 * (b // 2 + 1)))
                    split_batch(b)
                with pool.Fori(NB * E, NB * WAY) as turn:
                    lower_parts(turn)

            @block.vector
            def _(dve):
                ch0 = Chain(dve, chain)
                dve.wait_ge(c_in, FLOOR + 64)
                ch0.link(dve.tensor_copy(iotab[:], iota[:, 0:CAP]))
                ch0.link(dve.tensor_copy(affs[:, :, :, 0], aff[:]))
                ch0.link(dve.tensor_tensor(arest[:], aff[:], affs[:, :, :, 0], ALU.subtract))
                ch0.link(dve.tensor_copy(affs[:, :, :, 1], arest[:]))
                ch0.link(dve.tensor_tensor(affs[:, :, :, 2], arest[:], affs[:, :, :, 1], ALU.subtract))
                for c in range(2):
                    ch0.link(dve.tensor_copy(affs[:, :, :, 3 + c], tok[:, :, c:c + 1].broadcast_to([P, NT, B * E])))
                N0 = ch0.n

                def make_onehot(n, col):
                    dve.wait_ge(gathered, FLOOR + n)
                    for t in range(NT):
                        ins = dve.tensor_scalar(onehot[:, t, :], iotab[:], posT[:, t, bass.ds(col, 1)], None, ALU.is_equal)
                    ins.then_inc(hot_ready, 1)

                def next_turn(i, b, ahead):
                    if b + ahead < NB:
                        return ((i // E) * NB + (b + ahead)) * E + i % E
                    i1 = (i + 1) % WAY
                    return ((i1 // E) * NB + (b + ahead - NB)) * E + i1 % E

                def gates(n, j):
                    ch = Chain(dve, chain, n, 4)
                    ch.base = ch.base + N0
                    dve.wait_ge(gathered, FLOOR + (n + 1))
                    ch.link(dve.tensor_copy(gi[:], pi))
                    dve.sem_inc(gi_read, 1)
                    dve.wait_ge(high_ready, FLOOR + ((n - 1) * NS if not isinstance(n, int) else 0))
                    ch.link(dve.tensor_tensor(gate[j][:], gi[:, :, 0], gi[:, :, 1], ALU.add))
                    ch.link(dve.tensor_tensor(gate[j][:], gate[j][:], gi[:, :, 2], ALU.add))
                    ch.link(dve.tensor_tensor(idx[j][:], gi[:, :, 3], gi[:, :, 4], ALU.add))
                    ch.close()

                dve.memset(onehotT[:], 0.0).then_inc(hotT_ready, 1)
                def split_batch(b):
                    dve.wait_ge(part_made, FLOOR + (2 * b + 1))
                    dve.tensor_tensor(stage[b % 2][:], stage[b % 2][:], xs[b][:, :, 0, :], ALU.subtract
                                      ).then_inc(part_off, 1)
                    dve.wait_ge(part_made, FLOOR + (2 * b + 2))
                    dve.tensor_tensor(xs[b][:, :, 2, :], stage[b % 2][:], xs[b][:, :, 1, :], ALU.subtract
                                      ).then_inc(split, 1)

                make_onehot(0, 0)
                split_batch(0)
                split_batch(1)
                gates(0, 0)
                make_onehot(1, E)
                split_batch(2)
                split_batch(3)
                dve.wait_ge(acc_in[NB - 1], FLOOR + 16)
                with dve.Fori(0, WAY) as i:
                    for b in range(NB):
                        turn = i * NB + b
                        dve.wait_ge(silued, FLOOR + (turn + 1))
                        dve.wait_ge(down, FLOOR + turn)
                        dve.tensor_tensor(hT[:], sg[:], up[:], ALU.mult).then_inc(h_ready, 1)
                        gates(turn + 1, (b + 1) % 2)
                        last = (b - 1) % NB
                        if b:
                            dve.wait_ge(acc_in[last], FLOOR + ((i // E + 1) * 16))
                        else:
                            dve.wait_ge(acc_in[last], FLOOR + ((i + E - 1) // E * 16))
                        for q in range(4):
                            dve.wait_ge(scat, FLOOR + (turn * 4 + (q + 1)))
                            tiles = acc[last][:, 2 * q:2 * q + 2, :]
                            dve.tensor_tensor(tiles, tiles, back[q % 2][:], ALU.add).then_inc(added, 1)
                        make_onehot(turn + 2, next_turn(i, b, 2))
                        for s in range(NS):
                            ins = dve.tensor_scalar(onehotT[:, s, :], iota[:], idx[b % 2][:, s:s + 1], None, ALU.is_equal)
                        ins.then_inc(hotT_ready, 1)
                        dve.wait_ge(y_ready, FLOOR + (turn + 1))
                        dve.wait_ge(high_ready, FLOOR + (turn * NS + NS))
                        for s in range(NS):
                            ins = dve.scalar_tensor_tensor(rest[:, s, :], yp[:, s, :], gate[b % 2][:, s:s + 1],
                                                           y[:, 0, s, :], ALU.mult, ALU.subtract)
                        ins.then_inc(rest_ready, 1)
                for q in range(4):
                    dve.wait_ge(scat, FLOOR + (NB * WAY * 4 + (q + 1)))
                    tiles = acc[NB - 1][:, 2 * q:2 * q + 2, :]
                    dve.tensor_tensor(tiles, tiles, back[q % 2][:], ALU.add).then_inc(added, 1)

            @block.tensor
            def _(pe):
                def gather(n, b, col, need):
                    pe.wait_ge(hot_ready, FLOOR + (n + 1))
                    pe.wait_ge(split, FLOOR + need)
                    pe.wait_ge(xsel_ready, FLOOR + n)
                    for k in range(KD):
                        for t in range(NT):
                            for part in range(3):
                                pe.matmul(pg[:, k, :], xs[b][:, t, part, k * P:(k + 1) * P], onehot[:, t, :],
                                          start=t == 0 and part == 0, stop=t == NT - 1 and part == 2)
                    if not isinstance(n, int):
                        pe.wait_ge(rest_ready, FLOOR + (n - 1))
                    for s in range(NS):
                        for t in range(NT):
                            ins = pe.matmul(pi[:, s, :], onehot[:, t, s * P:(s + 1) * P],
                                            affs[:, t, bass.ds(col, 1), :].rearrange("p a c -> p (a c)"),
                                            start=t == 0, stop=t == NT - 1)
                    ins.then_inc(gathered, 1)

                def add_back(n):
                    pe.wait_ge(y_ready, FLOOR + (n + 1))
                    pe.wait_ge(hotT_ready, FLOOR + (n + 1))
                    for q in range(4):
                        pe.wait_ge(added, FLOOR + (n * 4 + max(q - 1, 0)))
                        for t in range(2):
                            tokens = slice((2 * q + t) * P, (2 * q + t + 1) * P)
                            for s in range(NS):
                                for part in range(3):
                                    ins = pe.matmul(back[q % 2][:, t, :], onehotT[:, s, tokens], y[:, part, s, :],
                                                    start=s == 0 and part == 0, stop=s == NS - 1 and part == 2)
                        ins.then_inc(scat, 1)

                gather(0, 0, 0, 1)
                with pe.Fori(0, WAY) as i:
                    for b in range(NB):
                        turn = i * NB + b
                        if b == 0:
                            pe.wait_ge(w_in, FLOOR + (i * 32 + 32))
                        pe.wait_ge(xsel_ready, FLOOR + (turn + 1))
                        pe.wait_ge(h_ready, FLOOR + turn)
                        for w_, o_ in ((wg, gp), (wu, up)):
                            for m in range(NI):
                                for k in range(KD):
                                    ins = pe.matmul(o_[:, m, :], w_[:, k, m * P:(m + 1) * P], xsel[:, k, :],
                                                    start=k == 0, stop=k == KD - 1)
                        ins.then_inc(gu_done, 1)
                        if b < NB - 1:
                            gather(turn + 1, b + 1, ((i // E) * NB + (b + 1)) * E + i % E, (i // E) * NB + (b + 2))
                        else:
                            i1 = (i + 1) % WAY
                            gather(turn + 1, 0, ((i1 // E) * NB) * E + i1 % E, (i1 // E) * NB + 1)
                        add_back(turn)
                        pe.wait_ge(h_ready, FLOOR + (turn + 1))
                        pe.wait_ge(gi_read, FLOOR + (turn + 2))
                        if b == 0:
                            pe.wait_ge(wd_in, FLOOR + (i * 16 + 16))
                        for s in range(NS):
                            for m in range(NI):
                                ins = pe.matmul(yp[:, s, :], hT[:, m, s * P:(s + 1) * P], wd[:, m, :],
                                                start=m == 0, stop=m == NI - 1)
                        ins.then_inc(down, 1)
                add_back(NB * WAY)
PI = 3.14159265358979
TWO_PI_PARTS = (6.28125, 0.0019353071795864769)
PI_IN = 3.1415925
ROUND = 12582912.0


def phases(nc, xn_d, xnT_d, x_d, ppT_d, wpv, bpv, wk, bk, wkv, bkv, wg1, bg1, wg2, bg2, wb1, bb1, wb2, bb2,
           ln_g, ln_b, wo, bo, out_d):
    C = 2
    NAMES = ["k0", "kv0", "pv0", "k1", "kv1", "pv1", "gh0", "gh1", "bh", "gate", "z", "mean", "outA", "var", "outB"]
    FRONT = NAMES[6:11]
    NPROD, NPRE = len(NAMES), len(FRONT)
    SLOT = {n: q % 4 for q, n in enumerate(NAMES)}

    def made_at(name, turn):
        if turn is None:
            return FRONT.index(name) + 1
        return turn * NPROD + (NPRE + NAMES.index(name) + 1)

    def before(name, turn):
        s = SLOT[name]
        if turn is None:
            return [n for n in FRONT if SLOT[n] == s].index(name)
        mates = [n for n in NAMES if SLOT[n] == s]
        return turn * len(mates) + (len([n for n in FRONT if SLOT[n] == s]) + mates.index(name))

    with Stage(nc, "ph") as st:
        cosP = st.sb("cosP", [P, KD, T])
        sinP = st.sb("sinP", [P, KD, T])
        wpv_s, wk_s, wkv_s, wo_s = [st.sb(n, [P, KD, D]) for n in ("wpv", "wk", "wkv", "wo")]
        wg1_s = st.sb("wg1", [P, 2 * KD, D])
        wb1_s = st.sb("wb1", [P, KD, P])
        wg2_c = st.sb("wg2c", [P, KD])
        wb2_c = st.sb("wb2c", [P, 2])
        wb2_n = st.sb("wb2n", [P, 1])
        wg2_s = st.sb("wg2", [P, KD, P])
        wbd_s = st.sb("wbd", [P, P])
        col = st.sb("col", [P, 12])
        bb1_c = st.sb("bb1", [P, 1])
        bg2_c = st.sb("bg2", [P, 1])
        bb2_c = st.sb("bb2", [P, 2])
        bd = st.sb("bd", [P, 2])
        bo_r = st.sb("bo", [P, D])
        lnb_s = st.sb("lnb", [P, KD, P])
        ones = st.sb("ones", [P, T])
        avg = st.sb("avg", [P, P])
        avg16 = st.sb("avg16", [P, P])
        xT = [st.sb(f"xT{j}", [P, KD, 1 + T]) for j in range(2)]
        gh = st.sb("gh", [P, KD, T])
        bh = st.sb("bh", [P, T])
        gt = [st.sb(f"gt{j}", [P, T]) for j in range(2)]
        w0 = st.sb("w0", [P, 2, T])
        w1 = [st.sb(f"w1{j}", [P, T]) for j in range(2)]
        th = st.sb("th", [P, T])
        hs = st.sb("hs", [P, T])
        kc = st.sb("kc", [P, 1 + T])
        ks = st.sb("ks", [P, 1 + T])
        kvg = st.sb("kvg", [P, T])
        a = st.sb("a", [P, T])
        b_ = st.sb("b", [P, T])
        sa = st.sb("sa", [P, T])
        sb_ = st.sb("sb", [P, T])
        mc = st.sb("mc", [P, T])
        ms = st.sb("ms", [P, T])
        bl = st.sb("bl", [P, KD, T])
        sq = st.sb("sq", [P, KD, T])
        cs = st.sb("cs", [P, T])
        psa = st.sb("psa", [P, T])
        psb = st.sb("psb", [P, T])
        rstd = st.sb("rstd", [P, NT])
        eps = st.sb("eps", [P, 1])
        base = st.sb("base", [P, NT, D])
        xnat = st.sb("xnat", [P, NT, D])
        ps = [st.ps(f"ps{s}", [P, C, 512]) for s in range(4)]
        psf = [q[:].rearrange("p c n -> p (c n)") for q in ps]
        c_in = st.sem("c_in")
        x_in = [st.sem(f"x_in{j}") for j in range(2)]
        nat_in = st.sem("nat_in")
        made = st.sem("made")
        freed = [st.sem(f"freed{s}") for s in range(4)]
        ready0 = st.sem("ready0")
        bd_ready = st.sem("bd_ready")
        columns = st.sem("columns")
        wo_made = st.sem("wo_made")
        wo_ready = st.sem("wo_ready")
        scanned = st.sem("scanned")
        pos_ready = st.sem("pos_ready")
        dev = st.sem("dev")
        zeroed = st.sem("zeroed")
        chain = st.sem("chain")
        achain = st.sem("achain")
        pchain = st.sem("pchain")
        cs_ready = st.sem("cs_ready")
        ln_made = st.sem("ln_made")
        dev_ready = st.sem("dev_ready")
        reduced = st.sem("reduced")
        k_ready = st.sem("k_ready")
        kc_ready = st.sem("kc_ready")
        m_ready = st.sem("m_ready")
        m_used = st.sem("m_used")
        blended = st.sem("blended")
        cent = st.sem("cent")
        squared = st.sem("squared")
        base_ready = st.sem("base_ready")
        stored = st.sem("stored")

        def taken(eng, name, turn):
            eng.wait_ge(freed[SLOT[name]], FLOOR + (before(name, turn) + 1))

        with st.block() as block:

            @block.sync
            def _(sp):
                for dst, src in ((wpv_s, wpv), (wk_s, wk), (wkv_s, wkv), (wo_s, wo), (wg1_s, wg1), (wb1_s, wb1)):
                    sp.dma_start(dst[:], src.rearrange("(k p) n -> p k n", p=P)).then_inc(c_in, 16)
                sp.dma_start(wg2_c[:], wg2.rearrange("(k p) a -> p (k a)", p=P), allow_slow_non_contiguous=True).then_inc(c_in, 16)
                sp.dma_start(wb2_c[:], wb2).then_inc(c_in, 16)
                for q, v in enumerate((bpv, bk, bkv, bg1, ln_g, ln_b)):
                    sp.dma_start(col[:, 2 * q:2 * q + 2], v.rearrange("(k p) -> p k", p=P),
                                 allow_slow_non_contiguous=True).then_inc(c_in, 16)
                sp.dma_start(bb1_c[:], bb1.rearrange("(p a) -> p a", a=1)).then_inc(c_in, 16)
                sp.dma_start(bg2_c[:], col_bcast(bg2)).then_inc(c_in, 16)
                sp.dma_start(bb2_c[:], col_bcast(bb2)).then_inc(c_in, 16)
                sp.dma_start(bo_r[:], col_bcast(bo)).then_inc(c_in, 16)
                sp.dma_start(cosP[:], ppT_d.rearrange("(k p) t -> p k t", p=P)).then_inc(c_in, 16)
                sp.wait_ge(zeroed, FLOOR + 1)
                for k in range(KD):
                    sp.dma_start(xT[0][:, k, 1:], xnT_d[k, :, 0:T]).then_inc(x_in[0], 16)
                with sp.Fori(0, B // 2) as i:
                    for j in range(2):
                        turn, n = i * 2 + j, i * 2 + (j + 1)
                        sp.wait_ge(made, FLOOR + turn * NPROD)
                        for k in range(KD):
                            sp.dma_start(xT[1 - j][:, k, 1:], xnT_d[k, :, bass.ds((n % B) * T, T)]).then_inc(x_in[1 - j], 16)
                        sp.wait_ge(stored, FLOOR + turn * 16)
                        sp.dma_start(base[:], x_d[bass.ds(turn * T, T), :].rearrange("(t p) d -> p t d", p=P)).then_inc(nat_in, 16)
                        sp.wait_ge(base_ready, FLOOR + turn)
                        sp.dma_start(xnat[:], xn_d[bass.ds(turn * T, T), :].rearrange("(t p) d -> p t d", p=P)).then_inc(nat_in, 16)
                        taken(sp, "outA", turn)
                        st.settle(sp)
                        taken(sp, "outB", turn)
                        st.settle(sp)
                        sp.dma_start(out_d[bass.ds(turn * T, T), :].rearrange("(t p) d -> p t d", p=P), base[:]).then_inc(stored, 16)
                sp.wait_ge(stored, FLOOR + 16 * B)
                sp.wait_ge(x_in[0], FLOOR + (32 * (B // 2 + 1)))

            NC = 19

            @block.gpsimd
            def _(pool):
                for j in range(2):
                    pool.memset(xT[j][:, :, 0:1], 0.0)
                pool.memset(kc[:, 0:1], 0.0)
                pool.memset(ks[:, 0:1], 0.0).then_inc(zeroed, 1)
                pool.memset(avg[:], 1.0 / D)
                pool.memset(avg16[:], 1.0 / D / 16).then_inc(zeroed, 1)
                pool.wait_ge(wo_ready, FLOOR + 1)
                pool.wait_ge(ready0, FLOOR + 1)
                with pool.Fori(0, B) as i:
                    ch = Chain(pool, pchain, i, 1)
                    for mo in range(KD):
                        u = i * 2 + mo
                        pool.wait_ge(k_ready, FLOOR + (u + 1))
                        pool.wait_ge(m_used, FLOOR + u)
                        st.settle(pool)
                        pool.tensor_scalar(kc[:, 1:], hs[:], -2.0, 1.0, ALU.mult, ALU.add).then_inc(kc_ready, 1)
                        pool.wait_ge(kc_ready, FLOOR + (u + 1))
                        taken(pool, f"kv{mo}", i)
                        pool.tensor_tensor(mc[:], kvg[:], kc[:, 0:T], ALU.mult)
                        pool.tensor_tensor(ms[:], kvg[:], ks[:, 0:T], ALU.mult).then_inc(m_ready, 1)
                        pool.wait_ge(scanned, FLOOR + (u + 1))
                        pool.tensor_tensor(psa[:], cosP[:, mo, :], psa[:], ALU.mult)
                        pool.tensor_tensor(psb[:], sinP[:, mo, :], psb[:], ALU.mult).then_inc(pos_ready, 1)
                    pool.wait_ge(nat_in, FLOOR + (i * 32 + 32))
                    ch.link(pool.tensor_tensor(base[:], base[:], xnat[:], ALU.add))
                    pool.tensor_tensor(base[:], base[:], bo_r[:].rearrange("p (a n) -> p a n", a=1).broadcast_to([P, NT, D]),
                                       ALU.add).then_inc(base_ready, 1)
                    ch.close()

            @block.tensor
            def _(pe):
                def product(name, turn, lhs, rhs, nk):
                    pe.wait_ge(freed[SLOT[name]], FLOOR + before(name, turn))
                    for c in range(C):
                        for k in range(nk):
                            ins = pe.matmul(ps[SLOT[name]][:, c, :], lhs(k), rhs(k, c), start=k == 0, stop=k == nk - 1)
                    ins.then_inc(made, 1)

                def front(n, par, loads):
                    pe.wait_ge(x_in[par], FLOOR + loads)
                    for mo in range(KD):
                        product(f"gh{mo}", n, lambda k: wg1_s[:, k, mo * P:(mo + 1) * P],
                                lambda k, c: xT[par][:, k % KD, 1 - k // KD + c * 512:1 - k // KD + (c + 1) * 512], 2 * KD)
                    product("bh", n, lambda k: wb1_s[:, k, :], lambda k, c: xT[par][:, k, 1 + c * 512:1 + (c + 1) * 512], KD)
                    taken(pe, "gh0", n)
                    taken(pe, "gh1", n)
                    product("gate", n, lambda k: wg2_s[:, k, :], lambda k, c: gh[:, k, c * 512:(c + 1) * 512], KD)
                    taken(pe, "bh", n)
                    product("z", n, lambda k: wbd_s[:], lambda k, c: bh[:, c * 512:(c + 1) * 512], 1)

                pe.wait_ge(c_in, FLOOR + 16 * NC)
                pe.wait_ge(zeroed, FLOOR + 2)
                pe.wait_ge(columns, FLOOR + 1)
                for k in range(KD):
                    ins = pe.matmul(ps[3][:, 0, 0:D], lnb_s[:, k, :], wo_s[:, k, :], start=k == 0, stop=k == KD - 1)
                ins.then_inc(wo_made, 1)
                pe.wait_ge(wo_ready, FLOOR + 1)
                for k in range(KD):
                    ins = pe.matmul(ps[3][:, 1, 0:D], avg[:], wo_s[:, k, :], start=k == 0, stop=k == KD - 1)
                ins.then_inc(wo_made, 1)
                pe.wait_ge(wo_ready, FLOOR + 2)
                front(None, 0, 32)
                with pe.Fori(0, B // 2) as i:
                    for j in range(2):
                        turn = i * 2 + j
                        for mo in range(KD):
                            for nm, w_ in (("k", wk_s), ("kv", wkv_s), ("pv", wpv_s)):
                                product(f"{nm}{mo}", turn, lambda k: w_[:, k, mo * P:(mo + 1) * P],
                                        lambda k, c: xT[j][:, k, 1 + c * 512:1 + (c + 1) * 512], KD)
                        front(turn, 1 - j, (i + (1 + j)) * 32)
                        pe.wait_ge(blended, FLOOR + (turn * 2 + 2))
                        product("mean", turn, lambda k: avg16[:], lambda k, c: bl[:, k, c * 512:(c + 1) * 512], KD)
                        for hf, name in enumerate(("outA", "outB")):
                            pe.wait_ge(freed[SLOT[name]], FLOOR + before(name, turn))
                            pv = psf[SLOT[name]].rearrange("p (t n) -> p t n", n=D)
                            for t in range(4):
                                for k in range(KD):
                                    tt = hf * 4 + t
                                    ins = pe.matmul(pv[:, t, :], bl[:, k, tt * P:(tt + 1) * P], wo_s[:, k, :],
                                                    start=k == 0, stop=k == KD - 1)
                            ins.then_inc(made, 1)
                            if hf == 0:
                                pe.wait_ge(squared, FLOOR + (turn * 2 + 2))
                                pe.wait_ge(freed[SLOT["var"]], FLOOR + before("var", turn))
                                for t in range(NT):
                                    for k in range(KD):
                                        ins = pe.matmul(psf[SLOT["var"]][:, t:t + 1], sq[:, k, t * P:(t + 1) * P],
                                                        avg[:, 0:1], start=k == 0, stop=k == KD - 1)
                                ins.then_inc(made, 1)

            @block.scalar
            def _(act):
                def front(n, t, par):
                    for name, dst, bias in (("gh0", gh[:, 0, :], col[:, 6:7]), ("gh1", gh[:, 1, :], col[:, 7:8]),
                                            ("bh", bh[:], bb1_c[:, 0:1])):
                        act.wait_ge(made, FLOOR + made_at(name, t))
                        act.activation(dst, psf[SLOT[name]], ACT.Gelu, bias=bias).then_inc(freed[SLOT[name]], 1)
                    if t is not None:
                        act.wait_ge(blended, FLOOR + t * 2)
                    act.wait_ge(made, FLOOR + made_at("gate", t))
                    act.activation(gt[par][:], psf[SLOT["gate"]], ACT.Sigmoid, bias=bg2_c[:, 0:1]
                                   ).then_inc(freed[SLOT["gate"]], 1)
                    act.wait_ge(made, FLOOR + made_at("z", t))
                    act.activation(w0[:, par, :], psf[SLOT["z"]], ACT.Sigmoid, bias=bd[:, 0:1])
                    act.activation(w1[par][:], psf[SLOT["z"]], ACT.Sigmoid, bias=bd[:, 1:2], scale=-1.0
                                   ).then_inc(freed[SLOT["z"]], 1)
                    act.wait_ge(cs_ready, FLOOR + (n + 1))
                    act.activation(cs[:], cs[:], ACT.Ln).then_inc(ln_made, 1)
                    act.wait_ge(ln_made, FLOOR + (n + 1))
                    act.activation(cs[:], cs[:], ACT.Exp, scale=-0.5).then_inc(dev_ready, 1)

                ch = Chain(act, achain)
                for k in range(KD):
                    act.wait_ge(reduced, FLOOR + (k + 1))
                    ch.link(act.activation(sinP[:, k, :], cosP[:, k, :], ACT.Sin))
                    ch.link(act.activation(cosP[:, k, :], cosP[:, k, :], ACT.Sin, scale=0.5))
                    ch.link(act.activation(cosP[:, k, :], cosP[:, k, :], ACT.Square))
                pre = ch.n
                act.wait_ge(bd_ready, FLOOR + 1)
                front(0, None, 0)
                with act.Fori(0, B // 2) as i:
                    for j in range(2):
                        turn = i * 2 + j
                        ch = Chain(act, achain, turn, 4)
                        ch.base = ch.base + pre
                        for mo in range(KD):
                            u = turn * 2 + mo
                            act.wait_ge(made, FLOOR + made_at(f"k{mo}", turn))
                            act.activation(th[:], psf[SLOT[f"k{mo}"]], ACT.Tanh, bias=col[:, 2 + mo:3 + mo]
                                           ).then_inc(freed[SLOT[f"k{mo}"]], 1)
                            taken(act, f"k{mo}", turn)
                            act.wait_ge(m_used, FLOOR + u)
                            act.wait_ge(kc_ready, FLOOR + u)
                            act.activation(ks[:, 1:], th[:], ACT.Sin, scale=PI_IN)
                            ch.link(act.activation(hs[:], th[:], ACT.Sin, scale=PI_IN / 2))
                            ch.link(act.activation(hs[:], hs[:], ACT.Square))
                            act.sem_inc(k_ready, 1)
                        ch.close()
                        front(turn + 1, turn, 1 - j)
                        for mo in range(KD):
                            act.wait_ge(cent, FLOOR + (turn * 2 + mo + 1))
                            act.activation(sq[:, mo, :], sq[:, mo, :], ACT.Square).then_inc(squared, 1)
                        act.wait_ge(made, FLOOR + made_at("var", turn))
                        act.wait_ge(freed[SLOT["outB"]], FLOOR + before("outB", turn))
                        act.activation(rstd[:], psf[SLOT["var"]][:, 0:NT], ACT.Sqrt, bias=eps[:, 0:1]
                                       ).then_inc(freed[SLOT["var"]], 1)

            @block.vector
            def _(dve):
                STT = dve.scalar_tensor_tensor

                def gate_sums(n, t, par, ch):
                    taken(dve, "gate", t)
                    ch.link(dve.tensor_tensor_scan(cs[:], ones[:], gt[par][:], 0.0, ALU.mult, ALU.add))
                    dve.tensor_scalar(cs[:], cs[:], 1.0, None, ALU.max).then_inc(cs_ready, 1)

                def value_weight(n, t, par, ch):
                    dve.wait_ge(dev_ready, FLOOR + (n + 1))
                    taken(dve, "z", t)
                    ch.link(dve.tensor_tensor(w1[par][:], w1[par][:], cs[:], ALU.mult))

                dve.wait_ge(c_in, FLOOR + 16 * NC)
                ch = Chain(dve, chain)
                dve.memset(ones[:], 1.0)
                dve.memset(eps[:], LN_EPS)
                ch.link(dve.tensor_tensor(bd[:, 0:1], bb2_c[:, 0:1], bb2_c[:, 1:2], ALU.subtract))
                ch.link(dve.tensor_scalar(bd[:, 1:2], bd[:, 0:1], -1.0, None, ALU.mult))
                ch.link(dve.tensor_tensor(wb2_n[:], wb2_c[:, 0:1], wb2_c[:, 1:2], ALU.subtract))
                for k in range(KD):
                    ch.link(dve.tensor_copy(wg2_s[:, k, :], wg2_c[:, k:k + 1].broadcast_to([P, P])))
                    ch.link(dve.tensor_copy(lnb_s[:, k, :], col[:, 10 + k:11 + k].broadcast_to([P, P])))
                ch.link(dve.tensor_copy(wbd_s[:], wb2_n[:, 0:1].broadcast_to([P, P])))
                dve.sem_inc(bd_ready, 1)
                dve.sem_inc(columns, 1)
                dve.wait_ge(wo_made, FLOOR + 1)
                ch.link(dve.tensor_tensor(bo_r[:], bo_r[:], ps[3][:, 0, 0:D], ALU.add))
                for k in range(KD):
                    ch.link(dve.tensor_scalar(wo_s[:, k, :], wo_s[:, k, :], col[:, 8 + k:9 + k], 1.0 / 16, ALU.mult, ALU.mult))
                dve.sem_inc(wo_ready, 1)
                dve.wait_ge(wo_made, FLOOR + 2)
                for k in range(KD):
                    ch.link(dve.tensor_tensor(wo_s[:, k, :], wo_s[:, k, :], ps[3][:, 1, 0:D], ALU.subtract))
                dve.sem_inc(wo_ready, 1)
                for k in range(KD):
                    p = cosP[:, k, :]
                    ch.link(dve.tensor_scalar(a[:], p, 1.0 / (2 * PI), ROUND, ALU.mult, ALU.add))
                    ch.link(dve.tensor_scalar(a[:], a[:], -ROUND, None, ALU.add))
                    ch.link(STT(p, a[:], -TWO_PI_PARTS[0], p, ALU.mult, ALU.add))
                    ch.link(STT(p, a[:], -TWO_PI_PARTS[1], p, ALU.mult, ALU.add))
                    dve.tensor_scalar(p, p, PI_IN, -PI_IN, ALU.min, ALU.max).then_inc(reduced, 1)
                dve.wait_ge(achain, FLOOR + 3 * KD)
                dve.tensor_scalar(cosP[:], cosP[:], -2.0, 1.0, ALU.mult, ALU.add).then_inc(ready0, 1)
                dve.wait_ge(ready0, FLOOR + 1)
                gate_sums(0, None, 0, ch)
                value_weight(0, None, 0, ch)
                pre = ch.n
                with dve.Fori(0, B // 2) as i:
                    for j in range(2):
                        turn = i * 2 + j
                        ch = Chain(dve, chain, turn, 2 * 7 + 1 + 1 + 1)
                        ch.base = ch.base + pre
                        for mo in range(KD):
                            u = turn * 2 + mo
                            kv, pv = f"kv{mo}", f"pv{mo}"
                            dve.wait_ge(made, FLOOR + made_at(kv, turn))
                            dve.wait_ge(m_ready, FLOOR + u)
                            STT(kvg[:], psf[SLOT[kv]], col[:, 4 + mo:5 + mo], gt[j][:], ALU.add, ALU.mult
                                ).then_inc(freed[SLOT[kv]], 1)
                            dve.wait_ge(made, FLOOR + made_at(pv, turn))
                            dve.wait_ge(blended, FLOOR + u)
                            ch.link(STT(a[:], psf[SLOT[pv]], col[:, mo:mo + 1], cosP[:, mo, :], ALU.add, ALU.mult))
                            STT(b_[:], psf[SLOT[pv]], col[:, mo:mo + 1], sinP[:, mo, :], ALU.add, ALU.mult
                                ).then_inc(freed[SLOT[pv]], 1)
                            dve.wait_ge(blended, FLOOR + u)
                            dve.tensor_tensor_scan(psa[:], ones[:], a[:], 0.0, ALU.mult, ALU.add)
                            taken(dve, pv, turn)
                            dve.tensor_tensor_scan(psb[:], ones[:], b_[:], 0.0, ALU.mult, ALU.add).then_inc(scanned, 1)
                            dve.wait_ge(m_ready, FLOOR + (u + 1))
                            ch.link(dve.tensor_tensor_scan(sa[:], ones[:], mc[:], 0.0, ALU.mult, ALU.add))
                            ch.link(dve.tensor_tensor_scan(sb_[:], ones[:], ms[:], 0.0, ALU.mult, ALU.add))
                            dve.wait_ge(scanned, FLOOR + (u + 1))
                            dve.tensor_tensor(a[:], kc[:, 1:], sa[:], ALU.mult)
                            dve.tensor_tensor(b_[:], ks[:, 1:], sb_[:], ALU.mult).then_inc(m_used, 1)
                            dve.wait_ge(m_used, FLOOR + (u + 1))
                            ch.link(dve.tensor_tensor(a[:], a[:], b_[:], ALU.add))
                            ch.link(dve.tensor_tensor(a[:], a[:], w1[j][:], ALU.mult))
                            dve.wait_ge(pos_ready, FLOOR + (u + 1))
                            ch.link(dve.tensor_tensor(psa[:], psa[:], psb[:], ALU.add))
                            dve.wait_ge(made, FLOOR + turn * NPROD)
                            ch.link(dve.tensor_tensor(bl[:, mo, :], psa[:], w0[:, j, :], ALU.mult))
                            dve.tensor_tensor(bl[:, mo, :], bl[:, mo, :], a[:], ALU.add).then_inc(blended, 1)
                        gate_sums(turn + 1, turn, 1 - j, ch)
                        dve.wait_ge(blended, FLOOR + (turn * 2 + 2))
                        dve.wait_ge(made, FLOOR + made_at("mean", turn))
                        for mo in range(KD):
                            ins = STT(sq[:, mo, :], bl[:, mo, :], 1.0 / 16, psf[SLOT["mean"]], ALU.mult, ALU.subtract)
                            ins.then_inc(cent, 1)
                        dve.wait_ge(cent, FLOOR + (turn * 2 + 2))
                        dve.sem_inc(freed[SLOT["mean"]], 1)
                        value_weight(turn + 1, turn, 1 - j, ch)
                        taken(dve, "var", turn)
                        ch.link(dve.reciprocal(rstd[:], rstd[:]))
                        ch.close()
                        dve.wait_ge(base_ready, FLOOR + (turn + 1))
                        for hf, name in enumerate(("outA", "outB")):
                            dve.wait_ge(made, FLOOR + made_at(name, turn))
                            pv = psf[SLOT[name]].rearrange("p (t n) -> p t n", n=D)
                            for t in range(4):
                                tt = hf * 4 + t
                                ins = STT(base[:, tt, :], pv[:, t, :], rstd[:, tt:tt + 1], base[:, tt, :], ALU.mult, ALU.add)
                            ins.then_inc(freed[SLOT[name]], 1)
def soft_slots(nc, xn_d, xnT_d, phi, W_d, b_d, ident_d, y_d, nm_d):
    CH = NP // P
    NE = P // SLOTS
    HB = B // 2
    PAIRS = NT // 2
    AHEAD = 2
    with Stage(nc, "sl") as st:
        xn = st.sb("xn", [P, TILES, D])
        xT = st.sb("xT", [P, KD, B * T])
        ph = st.sb("phi", [P, KD, NP])
        w = st.sb("w", [P, NE, KD, D])
        bias = st.sb("bias", [P, D])
        ident = st.sb("ident", [P, P])
        lg = [st.sb(f"lg{j}", [P, B, P]) for j in range(4)]
        mx = st.sb("mx", [P, P])
        sm = [st.sb(f"sm{j}", [P, P]) for j in range(2)]
        slT = st.sb("slT", [P, KD, B, P])
        y = st.sb("y", [P, B, D])
        tmax = st.sb("tmax", [P, CH, B, NT])
        rest = st.sb("rest", [P, B * NT])
        part_b = st.sb("part_b", [P, 3, B * NT], BF16)
        part = st.sb("part", [P, 3, B * NT])
        part_r = [st.sb(f"part_r{h}", [P, P], BF16) for h in range(2)]
        lp = [st.ps(f"lp{j}", [P, B, P]) for j in range(2)]
        yp = [q[:].rearrange("p b n -> p (b n)").rearrange("p (b n) -> p b n", n=D) for q in lp[::-1]]
        acc = st.ps("acc", [P, KD, B, P])
        c_in = st.sem("c_in")
        t_in = [st.sem(f"t_in{q}") for q in range(PAIRS)]
        n_in = [st.sem(f"n_in{q}") for q in range(PAIRS)]
        i_in = st.sem("i_in")
        w_in = st.sem("w_in")
        bias_in = st.sem("bias_in")
        logits = st.sem("logits")
        shifted = st.sem("shifted")
        lp_read = st.sem("lp_read")
        chain = st.sem("chain")
        exped = st.sem("exped")
        inverted = st.sem("inverted")
        shared = st.sem("shared")
        slotted = st.sem("slotted")
        slT_ready = st.sem("slT_ready")
        y_made = st.sem("y_made")
        y_ready = st.sem("y_ready")
        stored = st.sem("stored")
        parts_ready = st.sem("parts_ready")
        parts_turned = st.sem("parts_turned")
        rows_ready = st.sem("rows_ready")
        parts_stored = st.sem("parts_stored")
        with st.block() as block:

            @block.sync
            def _(sp):
                sp.dma_start(ph[:], phi.rearrange("(k p) n -> p k n", p=P)).then_inc(c_in, 16)
                def channels(q):
                    cols = slice(2 * q * P, (2 * q + 2) * P)
                    for k in range(KD):
                        sp.dma_start(xT[:, k, :].rearrange("p (b t) -> p b t", b=B)[:, :, cols],
                                     xnT_d[k].rearrange("p (b t) -> p b t", b=B)[:, :, cols]).then_inc(t_in[q], 16)

                def tokens(q):
                    for b in range(B):
                        sp.dma_start(xn[:, b * NT + 2 * q:b * NT + 2 * q + 2, :],
                                     xn_d[b * T + 2 * q * P:b * T + (2 * q + 2) * P, :].rearrange("(t p) d -> p t d", p=P)
                                     ).then_inc(n_in[q], 16)

                channels(0)
                for q in range(1, PAIRS):
                    channels(q)
                    tokens(q - 1)
                tokens(PAIRS - 1)
                sp.dma_start(ident[:], ident_d).then_inc(i_in, 16)

                def weights(c):
                    for e in range(NE):
                        sp.dma_start(w[:, e], W_d[c * NE + e, :, :].rearrange("(k p) n -> p k n", p=P)).then_inc(w_in, 16)

                def biases(c):
                    for e in range(NE):
                        row = b_d[c * NE + e:c * NE + e + 1, :] if isinstance(c, int) else b_d[bass.ds(c * NE + e, 1), :]
                        sp.dma_start(bias[e * SLOTS:(e + 1) * SLOTS, :], row.to_broadcast([SLOTS, D])
                                     ).then_inc(bias_in, 16)

                weights(0)
                biases(0)
                with sp.Fori(0, CH) as c:
                    sp.wait_ge(y_made, FLOOR + (c * 2 + 2))
                    weights((c + 1) % CH)
                    sp.wait_ge(y_ready, FLOOR + (c * 2 + 2))
                    sp.dma_start(y_d[:, bass.ds(c * P, P), :].rearrange("b p d -> p b d"), y[:]).then_inc(stored, 16)
                    biases((c + 1) % CH)
                sp.wait_ge(stored, FLOOR + 16 * CH)
                sp.wait_ge(w_in, FLOOR + 64 * (CH + 1))
                sp.wait_ge(bias_in, FLOOR + 64 * (CH + 1))
                for h in range(2):
                    sp.wait_ge(rows_ready, FLOOR + h + 1)
                    n = 2 - h
                    sp.dma_start(nm_d[2 * h:2 * h + n, :].rearrange("q (t p) -> (q t) p", p=P),
                                 part_r[h][0:n * TILES, :]).then_inc(parts_stored, 16)
                sp.wait_ge(parts_stored, FLOOR + 32)

            @block.gpsimd
            def _(pool):
                with pool.Fori(0, CH) as c:
                    for m in range(NT):
                        j = m % 2
                        pool.wait_ge(inverted, FLOOR + (c * NT + (m + 1)))
                        for half in range(2):
                            part_ = lg[m % 4][:, half * HB:(half + 1) * HB, :]
                            pool.tensor_tensor(part_, part_,
                                               sm[j][:].rearrange("p (a n) -> p a n", a=1).broadcast_to([P, HB, P]),
                                               ALU.mult).then_inc(shared, 1)

            @block.tensor
            def _(pe):
                def token_logits(c, m):
                    j = m % 2
                    for b in range(B):
                        for k in range(KD):
                            ins = pe.matmul(lp[j][:, b, :], xT[:, k, b * T + m * P:b * T + (m + 1) * P],
                                            ph[:, k, bass.ds(c * P, P)], start=k == 0, stop=k == KD - 1)
                    ins.then_inc(logits, 1)

                def through_experts(c, read):
                    pe.wait_ge(w_in, FLOOR + (c * 64 + 64))
                    for h in range(2):
                        if read is not None:
                            pe.wait_ge(lp_read, FLOOR + (read + h))
                        for b in range(HB):
                            for k in range(KD):
                                for e in range(NE):
                                    ins = pe.matmul(yp[h][e * SLOTS:(e + 1) * SLOTS, b, :],
                                                    slT[:, k, h * HB + b, e * SLOTS:(e + 1) * SLOTS],
                                                    w[:, e, k, :], start=k == 0, stop=k == KD - 1)
                        ins.then_inc(y_made, 1)

                def turn(c, first):
                    for m in range(NT):
                        u = c * NT + m
                        pe.wait_ge(lp_read, FLOOR + (u + 1))
                        if m in (1, 2) and not first:
                            pe.wait_ge(y_ready, FLOOR + (c * 2 + (m - 2)))
                        if first and m % 2 == 0:
                            if m + AHEAD < NT:
                                pe.wait_ge(t_in[(m + AHEAD) // 2], FLOOR + 16 * KD)
                            pe.wait_ge(n_in[m // 2], FLOOR + 16 * B)
                        token_logits(c if m < NT - AHEAD else (c + 1) % CH, (m + AHEAD) % NT)
                        for half in range(2):
                            pe.wait_ge(shared, FLOOR + (u * 2 + half + 1))
                            if m == 0 and half == 0 and not first:
                                pe.wait_ge(slT_ready, FLOOR + c * 4)
                            for k in range(KD):
                                for b in range(half * HB, (half + 1) * HB):
                                    ins = pe.matmul(acc[:, k, b, :], xn[:, b * NT + m, k * P:(k + 1) * P],
                                                    lg[m % 4][:, b, :], start=m == 0 and b % 4 == 0,
                                                    stop=m == NT - 1, skip_group_check=True)
                        ins.then_inc(slotted, 1)
                        if m == 0 and not first:
                            through_experts(c - 1, c * NT + 2)

                pe.wait_ge(c_in, FLOOR + 16)
                pe.wait_ge(t_in[0], FLOOR + 16 * KD)
                for m in range(AHEAD):
                    token_logits(0, m)
                turn(0, True)
                with pe.Fori(1, CH) as c:
                    turn(c, False)
                pe.wait_ge(slT_ready, FLOOR + CH * 4)
                through_experts(CH - 1, None)
                pe.wait_ge(i_in, FLOOR + 16)
                pe.wait_ge(parts_ready, FLOOR + 1)
                parts = part[:].rearrange("p q t -> p (q t)")
                for h in range(2):
                    n = (2 - h) * TILES
                    pe.transpose(acc[0:n, 0, 4 * h, :], parts[:, h * P:h * P + n], ident[:]).then_inc(parts_turned, 1)

            @block.scalar
            def _(act):
                def exponential(c, m):
                    act.wait_ge(shifted, FLOOR + (c * NT + (m + 1)))
                    act.activation(lg[m % 4][:], lg[m % 4][:], ACT.Exp).then_inc(exped, 1)

                def slots_out(c):
                    act.wait_ge(slotted, FLOOR + (c * NT + NT))
                    act.wait_ge(y_made, FLOOR + c * 2)
                    for k in range(KD):
                        for h in range(2):
                            act.activation(slT[:, k, 4 * h:4 * h + 4, :], acc[:, k, 4 * h:4 * h + 4, :], ACT.Copy
                                           ).then_inc(slT_ready, 1)

                for m in range(AHEAD):
                    exponential(0, m)
                with act.Fori(0, CH - 1) as c:
                    for m in range(AHEAD, NT + AHEAD):
                        exponential(c, m)
                    slots_out(c)
                for m in range(AHEAD, NT):
                    exponential(CH - 1, m)
                slots_out(CH - 1)

            @block.vector
            def _(dve):
                def add_bias(c, h):
                    dve.wait_ge(y_made, FLOOR + (c * 2 + h + 1))
                    dve.wait_ge(stored, FLOOR + c * 16)
                    dve.wait_ge(bias_in, FLOOR + (c * 64 + 64))
                    dve.tensor_tensor(y[:, h * HB:(h + 1) * HB, :], yp[h],
                                      bias[:].rearrange("p (a n) -> p a n", a=1).broadcast_to([P, HB, D]),
                                      ALU.add).then_inc(y_ready, 1)

                def turn(c, first):
                    for m in range(NT):
                        j, l = m % 2, m % 4
                        u = c * NT + m
                        ch = Chain(dve, chain, u, 2)
                        dve.wait_ge(logits, FLOOR + (u + 1))
                        ch.link(dve.tensor_reduce(mx[:], lp[j][:].rearrange("p b n -> p n b"), AX.X, ALU.max))
                        if m >= 4 or not first:
                            dve.wait_ge(slotted, FLOOR + (u - 3))
                        dve.tensor_tensor(lg[l][:], lp[j][:], mx[:].rearrange("p (a n) -> p a n", a=1).broadcast_to([P, B, P]),
                                          ALU.subtract).then_inc(shifted, 1)
                        dve.tensor_reduce(tmax[:, bass.ds(c, 1), :, m].rearrange("p c b -> p (c b)"), lp[j][:],
                                          AX.X, ALU.max).then_inc(lp_read, 1)
                        if m == 2 and not first:
                            for h in range(2):
                                add_bias(c - 1, h)
                        dve.wait_ge(exped, FLOOR + (u + 1))
                        if m >= 2 or not first:
                            dve.wait_ge(shared, FLOOR + (u - 1) * 2)
                        ch.link(dve.tensor_reduce(sm[j][:], lg[l][:].rearrange("p b n -> p n b"), AX.X, ALU.add))
                        ch.close()
                        dve.reciprocal(sm[j][:], sm[j][:]).then_inc(inverted, 1)

                turn(0, True)
                with dve.Fori(1, CH) as c:
                    turn(c, False)
                ch = Chain(dve, chain)
                ch.base = 2 * CH * NT
                ch.link(dve.tensor_reduce(rest[:], tmax[:].rearrange("p c b m -> p (b m) c"), AX.X, ALU.max))
                ch.link(dve.tensor_scalar(rest[:], rest[:], -1.0, None, ALU.mult))
                for q in range(3):
                    ch.link(dve.tensor_copy(part_b[:, q, :], rest[:]))
                    ch.link(dve.tensor_tensor(rest[:], rest[:], part_b[:, q, :], ALU.subtract))
                dve.tensor_copy(part[:], part_b[:]).then_inc(parts_ready, 1)
                for h in range(2):
                    add_bias(CH - 1, h)
                for h in range(2):
                    n = (2 - h) * TILES
                    dve.wait_ge(parts_turned, FLOOR + h + 1)
                    dve.tensor_copy(part_r[h][0:n, :], acc[0:n, 0, 4 * h, :]).then_inc(rows_ready, 1)


def soft_combine(nc, xnT_d, phi, y_d, nm_d, x_d, out_d):
    SK = NP // P
    GT = 4
    GN = GT * P
    PL = 4
    LAG = 3
    with Stage(nc, "cb") as st:
        ph = st.sb("phi", [P, KD, NP])
        y = st.sb("y", [P, 2, SK, D + 1])
        nm = st.sb("nm", [3, B * T], BF16)
        ones = st.sb("ones", [3, P], BF16)
        xT = [st.sb(f"xT{h}", [P, KD, GN]) for h in range(2)]
        x = [st.sb(f"x{h}", [P, GT, D]) for h in range(2)]
        ex = [st.sb(f"ex{j}", [P, GN]) for j in range(PL)]
        rs = [st.sb(f"rs{h}", [P, GT]) for h in range(2)]
        lp = [st.ps(f"lp{j}", [P, GN]) for j in range(4)]
        op = st.ps("op", [P, GT, 512])
        c_in = st.sem("c_in")
        y_in = st.sem("y_in")
        ones_ready = st.sem("ones_ready")
        x_in = [st.sem(f"x_in{h}") for h in range(2)]
        r_in = [st.sem(f"r_in{h}") for h in range(2)]
        logits = st.sem("logits")
        exped = st.sem("exped")
        used = st.sem("used")
        inverted = st.sem("inverted")
        read = st.sem("read")
        stored = [st.sem(f"stored{h}") for h in range(2)]
        with st.block() as block:

            @block.sync
            def _(sp):
                tokens = lambda n0: xnT_d[:, :, bass.ds(n0, GN)].rearrange("k p t -> p k t")
                slots = lambda b: y_d[b, :, :].rearrange("(k p) d -> p k d", p=P)
                sp.dma_start(ph[:], phi.rearrange("(k p) n -> p k n", p=P)).then_inc(c_in, 16)
                sp.dma_start(nm[:], nm_d).then_inc(c_in, 16)
                sp.dma_start(xT[0][:], tokens(0)).then_inc(x_in[0], 16)
                sp.dma_start(y[:, 0, :, 0:D], slots(0)).then_inc(y_in, 16)
                with sp.Fori(0, B) as b:
                    for h in range(2):
                        g = b * 2 + h
                        sp.wait_ge(used, FLOOR + (g * SK + PL))
                        if h == 0:
                            sp.dma_start(xT[1][:], tokens(b * T + GN)).then_inc(x_in[1], 16)
                            sp.wait_ge(y_in, FLOOR + (b * 16 + 16))
                            sp.dma_start(y[:, bass.ds((b + 1) % 2, 1), :, 0:D].rearrange("p a k d -> p (a k) d"),
                                         slots((b + 1) % B)).then_inc(y_in, 16)
                        else:
                            sp.dma_start(xT[0][:], tokens((b + 1) % B * T)).then_inc(x_in[0], 16)
                        sp.wait_ge(stored[h], FLOOR + b * 16)
                        sp.dma_start(x[h][:], x_d[bass.ds(g * GN, GN), :].rearrange("(t p) d -> p t d", p=P)
                                     ).then_inc(r_in[h], 16)
                        sp.wait_ge(read, FLOOR + (g * GT + 2 * GT))
                        sp.dma_start(out_d[bass.ds(g * GN, GN), :].rearrange("(t p) d -> p t d", p=P), x[h][:]
                                     ).then_inc(stored[h], 16)
                for h in range(2):
                    sp.wait_ge(stored[h], FLOOR + 16 * B)
                sp.wait_ge(y_in, FLOOR + 16 * (B + 1))
                sp.wait_ge(x_in[0], FLOOR + 16 * (B + 1))

            @block.tensor
            def _(pe):
                def slot_logits(g, n0, h, s, loads):
                    j = s % 4
                    if s == 0:
                        pe.wait_ge(x_in[h], FLOOR + loads * 16)
                    for k in range(KD):
                        pe.matmul(lp[j][:], ph[:, k, s * P:(s + 1) * P], xT[h][:, k, :], start=k == 0, stop=False)
                    pe.matmul(lp[j][:], ones[:], nm[:, bass.ds(n0, GN)], start=False, stop=True).then_inc(logits, 1)

                pe.wait_ge(c_in, FLOOR + 32)
                pe.wait_ge(ones_ready, FLOOR + 2)
                for s in range(LAG):
                    slot_logits(0, 0, 0, s, 1)
                with pe.Fori(0, B) as b:
                    for h in range(2):
                        g = b * 2 + h
                        for s in range(SK):
                            pe.wait_ge(exped, FLOOR + (g * SK + (s + 1)))
                            ahead = s + LAG
                            if ahead < SK:
                                slot_logits(g, b * T + h * GN, h, ahead, 0)
                            else:
                                slot_logits(g + 1, (b * T + (h + 1) * GN) if h == 0 else (b + 1) % B * T,
                                            1 - h, ahead - SK, b + 1 + h)
                            if s == 0:
                                pe.wait_ge(y_in, FLOOR + (b * 16 + 16))
                            for q in range(GT):
                                if s == 0:
                                    pe.wait_ge(read, FLOOR + (g * GT + q + 1))
                                ins = pe.matmul(op[:, q, 0:D + 1], ex[s % 4][:, q * P:(q + 1) * P],
                                                y[:, bass.ds(b % 2, 1), s, :].rearrange("p a d -> p (a d)"),
                                                start=s == 0, stop=s == SK - 1)
                            ins.then_inc(used, 1)

            @block.scalar
            def _(act):
                with act.Fori(0, B) as b:
                    for h in range(2):
                        g = b * 2 + h
                        for s in range(SK):
                            act.wait_ge(used, FLOOR + (g * SK + s + 1))
                            act.wait_ge(logits, FLOOR + (g * SK + s + 1))
                            act.activation(ex[s % 4][:], lp[s % 4][:], ACT.Exp).then_inc(exped, 1)

            @block.vector
            def _(dve):
                dve.sem_inc(used, PL)
                dve.memset(ones[:], 1.0).then_inc(ones_ready, 1)
                dve.memset(y[:, :, :, D:D + 1], 1.0).then_inc(ones_ready, 1)
                dve.sem_inc(read, GT)
                with dve.Fori(0, B) as b:
                    for h in range(2):
                        g = b * 2 + h
                        dve.wait_ge(used, FLOOR + (g * SK + SK + PL))
                        dve.reciprocal(rs[h][:], op[:, :, D]).then_inc(inverted, 1)
                        dve.wait_ge(inverted, FLOOR + (g + 1))
                        dve.wait_ge(r_in[h], FLOOR + (b * 16 + 16))
                        for q in range(GT):
                            dve.scalar_tensor_tensor(x[h][:, q, :], op[:, q, 0:D], rs[h][:, q:q + 1], x[h][:, q, :],
                                                     ALU.mult, ALU.add).then_inc(read, 1)
def build_program(nc, a, out):
    def scratch(name, shape):
        return nc.dram_tensor(name, shape, F32, kind="Internal").ap()

    x0, ident = a["x"], a["ident"]
    xn, xnT = scratch("xn", (B * T, D)), scratch("xnT", (KD, P, B * T))
    qkv, ctx = scratch("qkv", (B * T, 3 * D)), scratch("ctx", (B * T, D))
    x1, x2, x3 = (scratch(n, (B * T, D)) for n in ("x1", "x2", "x3"))
    pos, aff = scratch("pos", (P, NT, B * E)), scratch("aff", (P, NT, B, E))
    y = scratch("y", (B, NP, D))
    nm = nc.dram_tensor("nm", (3, B * T), BF16, kind="Internal").ap()

    normalise(nc, "n0", x0, None, xnT, ident)
    qkv_rope(nc, xnT, *(a["L0_attn_" + n] for n in ("Wq", "Wk", "Wv", "bq", "bk", "bv")), a["cos"], a["sin"], qkv)
    attend(nc, qkv, ident, a["kaug"], ctx)
    project(nc, "pj", ctx, a["L0_attn_Wo"], a["L0_attn_bo"], x0, ident, x1)
    normalise(nc, "n1", x1, xn, xnT, ident)
    route(nc, xnT, a["L0_ffn_gate_w"], ident, pos, aff)
    experts(nc, xn, pos, aff, a["L0_ffn_Wg"], a["L0_ffn_Wu"], a["L0_ffn_Wd"], a["iota"], a["tok"], x1, x2)
    normalise(nc, "n2", x2, xn, xnT, ident)
    phases(nc, xn, xnT, x2, a["ppT"], *(a["L1_attn_" + n] for n in (
        "Wpv", "bpv", "Wk", "bk", "Wkv", "bkv", "Wg1", "bg1", "Wg2", "bg2", "Wb1", "bb1", "Wb2", "bb2",
        "ln_g", "ln_b", "Wo", "bo")), x3)
    normalise(nc, "n3", x3, xn, xnT, ident)
    soft_slots(nc, xn, xnT, a["phi"], a["L1_ffn_W"], a["L1_ffn_b"], ident, y, nm)
    soft_combine(nc, xnT, a["phi"], y, nm, x3, out)


def kernel(**inputs):
    import concourse.bacc as _bacc
    from concourse.bass_utils import run_bass_kernel_spmd as _run

    given = {k: np.asarray(v) for k, v in inputs.items()}
    arrays = {k: v for k, v in given.items() if k not in ("L0_attn_x", "L1_attn_pos_phases", "L1_ffn_phi")}
    arrays["x"] = given["L0_attn_x"].reshape(B * T, D)
    arrays["ppT"] = given["L1_attn_pos_phases"][:T].T
    arrays["phi"] = given["L1_ffn_phi"].reshape(D, NP)
    arrays.update(consts())
    nc = _bacc.Bacc("TRN2", target_bir_lowering=False, num_devices=1)
    sent, aps = {}, {}
    for name, v in arrays.items():
        sent[f"in_{name}"] = np.ascontiguousarray(v)
        aps[name] = nc.dram_tensor(f"in_{name}", v.shape, mybir.dt.from_np(v.dtype), kind="ExternalInput").ap()
    out = nc.dram_tensor("out", (B * T, D), F32, kind="ExternalOutput").ap()
    build_program(nc, aps, out)
    r = _run(nc, [sent], core_ids=[0])
    return r.results[0]["out"].reshape(B, T, D)
```
